# Optimizing a Trainium2 kernel written in Bass

```python
import numpy as np
import jax
import jax.numpy as jnp

def _softmax(x, axis=-1):
    return jax.nn.softmax(x, axis=axis)

def _gelu(x):
    return jax.nn.gelu(x, approximate=True)

def _silu(x):
    return jax.nn.silu(x)

def _sigmoid(x):
    return jax.nn.sigmoid(x)

def _layernorm(x, axis=-1, eps=1e-05):
    m = jnp.mean(x, axis=axis, keepdims=True)
    v = jnp.var(x, axis=axis, keepdims=True)
    return (x - m) / jnp.sqrt(v + eps)

def _scatter_add(tgt, idx, src, axis=0):
    return tgt.at[idx].add(src)

def _segment_sum(src, seg, n):
    return jax.ops.segment_sum(src, seg, n)
kernel_name = 'mk_xattn_ffn_d2_seqx_r8_913b9a'

def setup_inputs(seed: int=0):
    np.random.seed(seed)
    _w = jnp.asarray

    def _rec_inputs():
        import jax
        import jax.numpy as jnp
        _rk = jax.random.key(seed)
        x = -0.0002928 + 1 * jax.random.normal(jax.random.fold_in(_rk, 1), (2, 256, 128), jnp.float32)
        _lenS = 256 - jax.random.randint(jax.random.fold_in(_rk, 7), (2,), 0, max(1, 256 // 4) + 1, jnp.int32)
        _lenS2 = 512 - jax.random.randint(jax.random.fold_in(_rk, 8), (2,), 0, max(1, 512 // 4) + 1, jnp.int32)
        _ctx_1024P = jax.random.normal(jax.random.fold_in(_rk, 11), (2, 16, 128), jnp.float32)
        _ctx_1024c = jax.random.dirichlet(jax.random.fold_in(_rk, 511), 0.3 * jnp.ones((16,), jnp.float32), (2, 512))
        _ctx_1024t = jnp.einsum('bsk,bkd->bsd', _ctx_1024c, _ctx_1024P)
        _ctx_1024t = _ctx_1024t * jax.lax.rsqrt(jnp.mean(jnp.square(_ctx_1024t)) + 1e-12) * 0.953939
        ctx_1024 = -1.39393e-06 + 0.999914 * (_ctx_1024t + 0.3 * jax.random.normal(jax.random.fold_in(_rk, 611), (2, 512, 128), jnp.float32))
        _validS = jnp.arange(256)[None, :] < _lenS[:, None]
        _validS2 = jnp.arange(512)[None, :] < _lenS2[:, None]
        _causal = jnp.tril(jnp.ones((256, 256), dtype=bool))
        mask_SxS2_ik0 = jnp.where(jnp.broadcast_to(_validS2[0:1, :], (256, 512)), 0, 1).astype(jnp.int32)
        return (x, ctx_1024, mask_SxS2_ik0)
    x, ctx_1024, mask_SxS2_ik0 = _rec_inputs()

    def _L0_xattn_setup():
        import jax, jax.numpy as jnp
        import numpy as np
        H = 16
        D = 128
        DK = D // H
        B, S = (2, 256)
        key = jax.random.key(seed)
        ks = jax.random.split(key, 11)
        scale = 1.0 / np.sqrt(D)
        inp = {'query': jax.random.normal(ks[0], (B, S, D), jnp.float32), 'key': jax.random.normal(ks[1], (B, S, D), jnp.float32), 'value': jax.random.normal(ks[2], (B, S, D), jnp.float32), 'mask': jnp.tril(jnp.ones((S, S), jnp.int32)), 'w_q': jax.random.normal(ks[3], (D, D), jnp.float32) * scale, 'b_q': jax.random.normal(ks[4], (D,), jnp.float32) * scale, 'w_k': jax.random.normal(ks[5], (D, D), jnp.float32) * scale, 'b_k': jax.random.normal(ks[6], (D,), jnp.float32) * scale, 'w_v': jax.random.normal(ks[7], (D, D), jnp.float32) * scale, 'b_v': jax.random.normal(ks[8], (D,), jnp.float32) * scale, 'w_out': jax.random.normal(ks[9], (D, D), jnp.float32) * scale, 'b_out': jax.random.normal(ks[10], (D,), jnp.float32) * scale}
        return inp
    _L0_xattn_all = _L0_xattn_setup()
    _L0_xattn_in = {k: v for k, v in _L0_xattn_all.items() if k in ('w_q', 'b_q', 'w_k', 'b_k', 'w_v', 'b_v', 'w_out', 'b_out')}
    del _L0_xattn_all

    def _L0_ffn_setup():
        import jax, jax.numpy as jnp
        import numpy as np
        B, S, H = (1, 256, 128)
        E = 16
        I = 96
        TOPK = 4
        G = 4
        TOPK_G = 2
        SCALE = 2.5
        N_SHARED = 1

        def _route(x, gate_w, gate_bias):
            n = x.shape[0]
            logits = jnp.einsum('nh,eh->ne', x.astype(jnp.float32), gate_w)
            scores = jax.nn.sigmoid(logits)
            sb = scores + gate_bias
            gs = sb.reshape(n, G, E // G)
            group_scores = jnp.sum(jax.lax.top_k(gs, 2)[0], axis=-1)
            _, gidx = jax.lax.top_k(group_scores, TOPK_G)
            gmask = jnp.sum(jax.nn.one_hot(gidx, G, dtype=sb.dtype), axis=1)
            emask = jnp.repeat(gmask, E // G, axis=-1)
            masked = jnp.where(emask > 0, sb, -jnp.inf)
            _, tidx = jax.lax.top_k(masked, TOPK)
            w = jnp.take_along_axis(scores, tidx, axis=1)
            w = w / (jnp.sum(w, axis=-1, keepdims=True) + 1e-20)
            return (tidx, w * SCALE)
        key = jax.random.key(seed)
        ks = jax.random.split(key, 9)

        def rn(k, shape, scale=0.02):
            return jax.random.normal(k, shape, dtype=jnp.float32) * scale
        return dict(hidden_states=jax.random.normal(ks[0], (B, S, H), dtype=jnp.float32), gate_w=rn(ks[1], (E, H)), gate_bias=jax.random.normal(ks[2], (E,), dtype=jnp.float32) * 0.1, w1=rn(ks[3], (E, I, H)), w2=rn(ks[4], (E, H, I)), w3=rn(ks[5], (E, I, H)), ws1=rn(ks[6], (I * N_SHARED, H)), ws2=rn(ks[7], (H, I * N_SHARED)), ws3=rn(ks[8], (I * N_SHARED, H)))
    _L0_ffn_all = _L0_ffn_setup()
    _L0_ffn_in = {k: v for k, v in _L0_ffn_all.items() if k in ('gate_w', 'gate_bias', 'w1', 'w2', 'w3', 'ws1', 'ws2', 'ws3')}
    del _L0_ffn_all

    def _L1_xattn_setup():
        import jax, jax.numpy as jnp
        import numpy as np
        DIM = 128
        NUM_HEADS = 16
        HEAD_DIM = DIM // NUM_HEADS
        EPS = 1e-05

        def _layer_norm(x, g, b):
            mu = jnp.mean(x, axis=-1, keepdims=True)
            var = jnp.mean((x - mu) ** 2, axis=-1, keepdims=True)
            return (x - mu) * jax.lax.rsqrt(var + EPS) * g + b
        key = jax.random.key(seed)
        ks = jax.random.split(key, 12)
        B, TQ, TKV = (8, 64, 256)
        s = 1.0 / np.sqrt(DIM)
        return {'q': jax.random.normal(ks[0], (B, TQ, DIM), jnp.float32), 'k': jax.random.normal(ks[1], (B, TKV, DIM), jnp.float32), 'v': jax.random.normal(ks[2], (B, TKV, DIM), jnp.float32), 'Wq': jax.random.normal(ks[3], (DIM, DIM), jnp.float32) * s, 'bq': jnp.zeros((DIM,), jnp.float32), 'Wk': jax.random.normal(ks[4], (DIM, DIM), jnp.float32) * s, 'bk': jnp.zeros((DIM,), jnp.float32), 'Wv': jax.random.normal(ks[5], (DIM, DIM), jnp.float32) * s, 'bv': jnp.zeros((DIM,), jnp.float32), 'Wo': jax.random.normal(ks[6], (DIM, DIM), jnp.float32) * s, 'bo': jnp.zeros((DIM,), jnp.float32), 'ln_g': jnp.ones((DIM,), jnp.float32), 'ln_b': jnp.zeros((DIM,), jnp.float32)}
    _L1_xattn_all = _L1_xattn_setup()
    _L1_xattn_in = {k: v for k, v in _L1_xattn_all.items() if k in ('Wq', 'bq', 'Wk', 'bk', 'Wv', 'bv', 'Wo', 'bo', 'ln_g', 'ln_b')}
    del _L1_xattn_all

    def _L1_ffn_setup():
        import jax, jax.numpy as jnp
        import numpy as np
        DIM = 128
        E = 8
        K = 2
        EPS = 1e-05

        def _ln(x, g, b):
            mu = jnp.mean(x, axis=-1, keepdims=True)
            var = jnp.mean(jnp.square(x - mu), axis=-1, keepdims=True)
            return (x - mu) * jax.lax.rsqrt(var + EPS) * g + b
        key = jax.random.key(seed)
        ks = jax.random.split(key, 8)
        H = 2 * DIM
        s_in = 1.0 / np.sqrt(DIM)
        s_h = 1.0 / np.sqrt(H)
        return {'x': jax.random.normal(ks[0], (2, 256, DIM), dtype=jnp.float32), 'gate_w': jax.random.uniform(ks[1], (DIM, E), minval=-s_in, maxval=s_in, dtype=jnp.float32), 'w1': jax.random.uniform(ks[2], (E, DIM, H), minval=-s_in, maxval=s_in, dtype=jnp.float32), 'b1': jax.random.uniform(ks[3], (E, H), minval=-s_in, maxval=s_in, dtype=jnp.float32), 'ln1_g': jnp.ones((E, H), dtype=jnp.float32), 'ln1_b': jnp.zeros((E, H), dtype=jnp.float32), 'w2': jax.random.uniform(ks[4], (E, H, DIM), minval=-s_h, maxval=s_h, dtype=jnp.float32), 'b2': jax.random.uniform(ks[5], (E, DIM), minval=-s_h, maxval=s_h, dtype=jnp.float32), 'ln_g': jnp.ones((DIM,), dtype=jnp.float32), 'ln_b': jnp.zeros((DIM,), dtype=jnp.float32)}
    _L1_ffn_all = _L1_ffn_setup()
    _L1_ffn_in = {k: v for k, v in _L1_ffn_all.items() if k in ('gate_w', 'w1', 'b1', 'ln1_g', 'ln1_b', 'w2', 'b2', 'ln_g', 'ln_b')}
    del _L1_ffn_all
    return {'x': x, 'ctx_1024': ctx_1024, 'mask_SxS2_ik0': mask_SxS2_ik0, 'L0_xattn_w_q': _L0_xattn_in['w_q'], 'L0_xattn_b_q': _L0_xattn_in['b_q'], 'L0_xattn_w_k': _L0_xattn_in['w_k'], 'L0_xattn_b_k': _L0_xattn_in['b_k'], 'L0_xattn_w_v': _L0_xattn_in['w_v'], 'L0_xattn_b_v': _L0_xattn_in['b_v'], 'L0_xattn_w_out': _L0_xattn_in['w_out'], 'L0_xattn_b_out': _L0_xattn_in['b_out'], 'L0_ffn_gate_w': _L0_ffn_in['gate_w'], 'L0_ffn_gate_bias': _L0_ffn_in['gate_bias'], 'L0_ffn_w1': _L0_ffn_in['w1'], 'L0_ffn_w2': _L0_ffn_in['w2'], 'L0_ffn_w3': _L0_ffn_in['w3'], 'L0_ffn_ws1': _L0_ffn_in['ws1'], 'L0_ffn_ws2': _L0_ffn_in['ws2'], 'L0_ffn_ws3': _L0_ffn_in['ws3'], 'L1_xattn_Wq': _L1_xattn_in['Wq'], 'L1_xattn_bq': _L1_xattn_in['bq'], 'L1_xattn_Wk': _L1_xattn_in['Wk'], 'L1_xattn_bk': _L1_xattn_in['bk'], 'L1_xattn_Wv': _L1_xattn_in['Wv'], 'L1_xattn_bv': _L1_xattn_in['bv'], 'L1_xattn_Wo': _L1_xattn_in['Wo'], 'L1_xattn_bo': _L1_xattn_in['bo'], 'L1_xattn_ln_g': _L1_xattn_in['ln_g'], 'L1_xattn_ln_b': _L1_xattn_in['ln_b'], 'L1_ffn_gate_w': _L1_ffn_in['gate_w'], 'L1_ffn_w1': _L1_ffn_in['w1'], 'L1_ffn_b1': _L1_ffn_in['b1'], 'L1_ffn_ln1_g': _L1_ffn_in['ln1_g'], 'L1_ffn_ln1_b': _L1_ffn_in['ln1_b'], 'L1_ffn_w2': _L1_ffn_in['w2'], 'L1_ffn_b2': _L1_ffn_in['b2'], 'L1_ffn_ln_g': _L1_ffn_in['ln_g'], 'L1_ffn_ln_b': _L1_ffn_in['ln_b']}

def reference(x, ctx_1024, mask_SxS2_ik0, L0_xattn_w_q, L0_xattn_b_q, L0_xattn_w_k, L0_xattn_b_k, L0_xattn_w_v, L0_xattn_b_v, L0_xattn_w_out, L0_xattn_b_out, L0_ffn_gate_w, L0_ffn_gate_bias, L0_ffn_w1, L0_ffn_w2, L0_ffn_w3, L0_ffn_ws1, L0_ffn_ws2, L0_ffn_ws3, L1_xattn_Wq, L1_xattn_bq, L1_xattn_Wk, L1_xattn_bk, L1_xattn_Wv, L1_xattn_bv, L1_xattn_Wo, L1_xattn_bo, L1_xattn_ln_g, L1_xattn_ln_b, L1_ffn_gate_w, L1_ffn_w1, L1_ffn_b1, L1_ffn_ln1_g, L1_ffn_ln1_b, L1_ffn_w2, L1_ffn_b2, L1_ffn_ln_g, L1_ffn_ln_b):
    import jax
    import jax.numpy as jnp

    def _L0_xattn_ref(query, key, value, mask, w_q, b_q, w_k, b_k, w_v, b_v, w_out, b_out):
        import jax, jax.numpy as jnp
        import numpy as np
        H = 16
        D = 128
        DK = D // H
        B, S = (2, 256)
        b = query.shape[0]

        def proj(x, w, bias):
            y = x @ w.T + bias
            return y.reshape(b, -1, H, DK).transpose(0, 2, 1, 3)
        q = proj(query, w_q, b_q)
        k = proj(key, w_k, b_k)
        v = proj(value, w_v, b_v)
        scores = jnp.einsum('bhqd,bhkd->bhqk', q, k) / np.sqrt(DK).astype(jnp.float32)
        scores = jnp.where(mask == 0, jnp.float32(-1000000000.0), scores)
        attn = jax.nn.softmax(scores, axis=-1)
        x = jnp.einsum('bhqk,bhkd->bhqd', attn, v)
        x = x.transpose(0, 2, 1, 3).reshape(b, -1, H * DK)
        return x @ w_out.T + b_out

    def _L0_ffn_ref(hidden_states, gate_w, gate_bias, w1, w2, w3, ws1, ws2, ws3):
        import jax, jax.numpy as jnp
        import numpy as np
        B, S, H = (1, 256, 128)
        E = 16
        I = 96
        TOPK = 4
        G = 4
        TOPK_G = 2
        SCALE = 2.5
        N_SHARED = 1

        def _route(x, gate_w, gate_bias):
            n = x.shape[0]
            logits = jnp.einsum('nh,eh->ne', x.astype(jnp.float32), gate_w)
            scores = jax.nn.sigmoid(logits)
            sb = scores + gate_bias
            gs = sb.reshape(n, G, E // G)
            group_scores = jnp.sum(jax.lax.top_k(gs, 2)[0], axis=-1)
            _, gidx = jax.lax.top_k(group_scores, TOPK_G)
            gmask = jnp.sum(jax.nn.one_hot(gidx, G, dtype=sb.dtype), axis=1)
            emask = jnp.repeat(gmask, E // G, axis=-1)
            masked = jnp.where(emask > 0, sb, -jnp.inf)
            _, tidx = jax.lax.top_k(masked, TOPK)
            w = jnp.take_along_axis(scores, tidx, axis=1)
            w = w / (jnp.sum(w, axis=-1, keepdims=True) + 1e-20)
            return (tidx, w * SCALE)
        b, s, h = hidden_states.shape
        x = hidden_states.reshape(-1, h)
        tidx, tw = _route(x, gate_w, gate_bias)
        n = x.shape[0]
        combine = jnp.zeros((n, E), x.dtype).at[jnp.arange(n)[:, None], tidx].add(tw)
        g = jnp.einsum('nh,eih->nei', x, w1)
        u = jnp.einsum('nh,eih->nei', x, w3)
        hact = jax.nn.silu(g) * u * combine[:, :, None]
        y = jnp.einsum('nei,ehi->nh', hact, w2)
        shared = jnp.einsum('ni,hi->nh', jax.nn.silu(x @ ws1.T) * (x @ ws3.T), ws2)
        return (y + shared).reshape(b, s, h)

    def _L1_xattn_ref(q, k, v, Wq, bq, Wk, bk, Wv, bv, Wo, bo, ln_g, ln_b):
        import jax, jax.numpy as jnp
        import numpy as np
        DIM = 128
        NUM_HEADS = 16
        HEAD_DIM = DIM // NUM_HEADS
        EPS = 1e-05

        def _layer_norm(x, g, b):
            mu = jnp.mean(x, axis=-1, keepdims=True)
            var = jnp.mean((x - mu) ** 2, axis=-1, keepdims=True)
            return (x - mu) * jax.lax.rsqrt(var + EPS) * g + b
        B, TQ, _ = q.shape
        TKV = k.shape[1]
        qn = _layer_norm(q, ln_g, ln_b)
        qp = qn @ Wq.T + bq
        kp = k @ Wk.T + bk
        vp = v @ Wv.T + bv
        qh = qp.reshape(B, TQ, NUM_HEADS, HEAD_DIM).transpose(0, 2, 1, 3)
        kh = kp.reshape(B, TKV, NUM_HEADS, HEAD_DIM).transpose(0, 2, 1, 3)
        vh = vp.reshape(B, TKV, NUM_HEADS, HEAD_DIM).transpose(0, 2, 1, 3)
        scale = HEAD_DIM ** (-0.5)
        scores = jnp.einsum('bhqd,bhkd->bhqk', qh, kh) * scale
        attn = jax.nn.softmax(scores, axis=-1)
        out = jnp.einsum('bhqk,bhkd->bhqd', attn, vh)
        out = out.transpose(0, 2, 1, 3).reshape(B, TQ, DIM)
        return out @ Wo.T + bo

    def _L1_ffn_ref(x, gate_w, w1, b1, ln1_g, ln1_b, w2, b2, ln_g, ln_b):
        import jax, jax.numpy as jnp
        import numpy as np
        DIM = 128
        E = 8
        K = 2
        EPS = 1e-05

        def _ln(x, g, b):
            mu = jnp.mean(x, axis=-1, keepdims=True)
            var = jnp.mean(jnp.square(x - mu), axis=-1, keepdims=True)
            return (x - mu) * jax.lax.rsqrt(var + EPS) * g + b
        shape = x.shape
        xf = x.reshape(-1, shape[-1])
        gates = jax.nn.softmax(xf @ gate_w, axis=-1)
        topw, topi = jax.lax.top_k(gates, K)
        topw = topw / jnp.sum(topw, axis=-1, keepdims=True)
        combine = jnp.sum(topw[:, :, None] * jax.nn.one_hot(topi, E, dtype=xf.dtype), axis=1)
        h = jnp.einsum('td,edh->teh', xf, w1) + b1
        h = _ln(h, ln1_g, ln1_b)
        h = jax.nn.gelu(h, approximate=False)
        y = jnp.einsum('teh,ehd->ted', h, w2) + b2
        out = jnp.einsum('ted,te->td', y, combine)
        out = _ln(out + xf, ln_g, ln_b)
        return out.reshape(shape)
    x = x + _L0_xattn_ref(_layernorm(x, axis=-1), ctx_1024, ctx_1024, mask_SxS2_ik0, L0_xattn_w_q, L0_xattn_b_q, L0_xattn_w_k, L0_xattn_b_k, L0_xattn_w_v, L0_xattn_b_v, L0_xattn_w_out, L0_xattn_b_out)
    x = x + _L0_ffn_ref(_layernorm(x, axis=-1), L0_ffn_gate_w, L0_ffn_gate_bias, L0_ffn_w1, L0_ffn_w2, L0_ffn_w3, L0_ffn_ws1, L0_ffn_ws2, L0_ffn_ws3)
    x = x + _L1_xattn_ref(_layernorm(x, axis=-1), ctx_1024, ctx_1024, L1_xattn_Wq, L1_xattn_bq, L1_xattn_Wk, L1_xattn_bk, L1_xattn_Wv, L1_xattn_bv, L1_xattn_Wo, L1_xattn_bo, L1_xattn_ln_g, L1_xattn_ln_b)
    x = x + _L1_ffn_ref(_layernorm(x, axis=-1), L1_ffn_gate_w, L1_ffn_w1, L1_ffn_b1, L1_ffn_ln1_g, L1_ffn_ln1_b, L1_ffn_w2, L1_ffn_b2, L1_ffn_ln_g, L1_ffn_ln_b)
    return x

_drawn_inputs = setup_inputs


def setup_inputs(seed=0):
    import zlib

    import numpy as np

    out = dict(_drawn_inputs(seed))
    spreads = {'L1_xattn_bq': (0.0, 0.348),
     'L1_xattn_bk': (0.0, 2.0),
     'L1_xattn_bv': (0.0, 0.1),
     'L1_xattn_bo': (0.0, 0.1),
     'L1_xattn_ln_g': (1.0, 0.6),
     'L1_xattn_ln_b': (0.0, 0.293),
     'L1_ffn_ln1_g': (1.0, 0.547),
     'L1_ffn_ln1_b': (0.0, 0.659),
     'L1_ffn_ln_g': (1.0, 0.2),
     'L1_ffn_ln_b': (0.0, 0.1)}
    factors = {'L0_xattn_b_q': 2.678,
     'L0_xattn_b_k': 64.0,
     'L0_ffn_gate_w': 5.74,
     'L0_ffn_gate_bias': 7.702,
     'L0_ffn_w1': 5.163,
     'L0_ffn_w2': 6.14,
     'L0_ffn_w3': 6.047,
     'L0_ffn_ws1': 5.994,
     'L0_ffn_ws2': 5.24,
     'L0_ffn_ws3': 6.673,
     'L1_ffn_b1': 4.955,
     'L1_ffn_b2': 4.927}
    for name, (base, spread) in spreads.items():
        noise = np.random.default_rng([zlib.crc32(name.encode()), seed]).standard_normal(out[name].shape)
        drawn = base * np.exp(spread * noise) if base else spread * noise
        out[name] = jnp.asarray(drawn.astype(out[name].dtype))
    for name, factor in factors.items():
        out[name] = (out[name] * factor).astype(out[name].dtype)
    return out
```

```python
from contextlib import ExitStack

import numpy as np

import concourse.bass as bass
from concourse import mybir

F32, BF16, I32 = mybir.dt.float32, mybir.dt.bfloat16, mybir.dt.int32
ALU = mybir.AluOpType
ACT = mybir.ActivationFunctionType
AX = mybir.AxisListType

B, S, S2, D = 2, 256, 512, 128
H, DK = 16, 8
QT, KT = S // 128, S2 // 128
PARTS = 3
STACK = PARTS * PARTS * DK
ROWS_K = STACK + PARTS
E0, I0 = 16, 96
T0 = E0 * I0 // 128
E1, H1 = 8, 256
GROUPS0 = 4
HG = 4
NG = H // HG
VW = 32
SCALE = float(DK) ** -0.5
EPS = 1e-5
MASKED = -float(2.0 ** 100)
LOWEST = -3.0e38
LAG = 8
HEADS = B * H
BATCH_STEPS = HEADS + LAG + 2

ROW_NAMES = ["bv0", "bo0", "bv1", "bo1", "lnf_g", "lnf_b"]
COL_BK0, COL_BQ0, COL_BK1, COL_BQ1, COL_LNG, COL_LNB, COL_G1 = 0, 1, 2, 3, 4, 5, 6
COL_B1 = COL_G1 + 2 * E1
NCOLS = COL_B1 + 2 * E1


def attention_ffn_kernel(nc, x, ctxT, mask, maskT, attn_w, cols, rows, gate_bias, ties, ident,
                         gate0, gate1, wg0, wu0, wd0, wsd0, select0, wu1, bu1, wd1, bd1, out):
    ctx = ExitStack()
    with ctx:
        def sb(name, shape, dt=F32):
            return ctx.enter_context(nc.sbuf_tensor(name, shape, dt))

        def sem(name):
            return ctx.enter_context(nc.semaphore(name))

        k_bounce = [nc.dram_tensor(f"k_bounce{i}", [PARTS, PARTS, 128, S2], BF16, kind="Internal").ap()
                    for i in range(4)]
        q_bounce = [nc.dram_tensor(f"q_bounce{i}", [PARTS, PARTS, 128, S], BF16, kind="Internal").ap()
                    for i in range(4)]

        x_sb = sb("x_sb", [128, B, QT, D])
        ctxT_sb = sb("ctxT_sb", [128, B, S2])
        probs = sb("probs", [128, 2 * HG, KT * S])
        mask_q = probs[:, 0, :].bitcast(I32).rearrange("p (t k) -> p t k", t=QT)
        mask_k = probs[:, 1, :].bitcast(I32).rearrange("p (t q) -> p t q", t=KT)
        experts_w = sb("experts_w", [128, 2 * (T0 * 128 + I0) + T0 * D])
        early = sb("early", [128, 4 * (2 * S2 + PARTS * S2 // 2)])
        shared_area = sb("shared_area", [128, T0 * 128])
        aw = sb("aw", [128, 2, 4, 128])
        W_K, W_Q, W_V, W_O = 0, 1, 2, 3
        col = sb("col", [128, NCOLS])
        row = sb("row", [128, len(ROW_NAMES), D])
        gbias = sb("gbias", [128, E0])
        tie = sb("tie", [128, E0, E0])
        idf = sb("idf", [128, 128])
        g0_sb = sb("g0_sb", [128, E0])
        g1_sb = sb("g1_sb", [128, E1])
        up_cols = E0 * I0 + I0
        wg0_sb = experts_w[:, 0:up_cols]
        wu0_sb = experts_w[:, up_cols:2 * up_cols]
        wd0_sb = experts_w[:, 2 * up_cols:2 * up_cols + T0 * D].rearrange("p (t d) -> p t d", t=T0)
        wsd0_sb = sb("wsd0_sb", [I0, D])
        sel_f = shared_area[0:PARTS * E0, :].rearrange("p (t r) -> p t r", t=T0)
        wu1_sb = experts_w[:, 0:E1 * H1].rearrange("p (e n) -> p e n", e=E1)
        bu1_sb = sb("bu1_sb", [128, E1 * H1 // 128])
        wd1_sb = experts_w[:, E1 * H1:2 * E1 * H1].rearrange("p (t d) -> p t d", t=2 * E1)
        bd1_sb = sb("bd1_sb", [E1, D])

        idb = sb("idb", [128, 128], BF16)
        sel = sb("sel", [PARTS * E0, T0, 128], BF16)
        bias_q = sb("bias_q", [128, QT, S2])
        bias_k = sb("bias_k", [128, KT, S], BF16)
        minus_half = sb("minus_half", [128, 4])
        ones_parts = sb("ones_parts", [PARTS, S2], BF16)
        bu1_part = sb("bu1_part", [128, PARTS, E1 * H1 // 128], BF16)
        bu1_rest = sb("bu1_rest", [128, E1 * H1 // 128])
        bu1_rows = ctxT_sb[0:PARTS].rearrange("p b k -> p (b k)").bitcast(BF16)

        k_full = [early[:, i * S2:(i + 1) * S2] for i in range(4)]
        k_rest = [early[:, (4 + i) * S2:(5 + i) * S2] for i in range(4)]
        part_cols = PARTS * S2 // 2
        k_part = [early[:, 8 * S2 + i * part_cols:8 * S2 + (i + 1) * part_cols].bitcast(BF16)
                  .rearrange("p (a s) -> p a s", a=PARTS) for i in range(4)]
        q_full = sb("q_full", [128, S])
        q_rest = sb("q_rest", [128, S])
        q_part = [sb(f"q_part{b}", [128, PARTS, S], BF16) for b in range(B)]
        k_stack = sb("k_stack", [ROWS_K, B, H, S2], BF16)
        q_stack = sb("q_stack", [ROWS_K, B, H, S], BF16)
        v_ext = [sb(f"v_ext{l}", [128, B * KT, H * (DK + 1) + VW - DK - 1]) for l in range(2)]
        v_heads = [v[:, :, 0:H * (DK + 1)].rearrange("p t (h c) -> p t h c", h=H) for v in v_ext]
        row_max = sb("row_max", [128, 2, HG, QT])
        max_rest = sb("max_rest", [128, HG, QT])
        max_part = sb("max_part", [128, QT, PARTS, HG], BF16)
        max_rows = sb("max_rows", [PARTS * HG, 2, S], BF16)
        discard = sb("discard", [128, QT, S2], BF16)
        o_sb = sb("o_sb", [128, 2, S])
        rden = sb("rden", [128, QT, HG])
        att = [[sb(f"att{b}", [128, QT, D]) for b in range(B)],
               [shared_area[:, b * S:(b + 1) * S].rearrange("p (t d) -> p t d", t=QT) for b in range(B)]]
        attT = [[sb(f"attT{b}", [128, S]) for b in range(B)],
                [shared_area[:, (2 + b) * S:(3 + b) * S] for b in range(B)]]

        res = [[x_sb[:, b] for b in range(B)]] + [
            [sb(f"res{s}{b}", [128, QT, D])[:] for b in range(B)] for s in range(1, 3)]
        res.append(res[1])
        res_bias = {s: [sb(f"res_bias{s}{b}", [128, QT, D]) for b in range(B)] for s in (0, 3)}
        res_bias[2] = res_bias[0]
        norm = {n: [sb(f"norm_{n}{b}", [128, QT, D]) for b in range(B)] for n in ("a0", "f0", "f1")}
        norm["a1n"], norm["a1"], norm["out"] = norm["a0"], norm["f0"], norm["f0"]
        mean_var = {(n, b): sb(f"mv_{n}{b}", [128, QT, 2]) for n in norm for b in range(B)}
        rstd = {(n, b): sb(f"rstd_{n}{b}", [128, QT]) for n in norm for b in range(B)}
        var_eps = sb("var_eps", [128, QT])
        stats = sb("stats", [128, QT, 6])
        xT = {n: [sb(f"xT_{n}{b}", [128, S]) for b in range(B)] for n in ("a0", "f0")}
        xT["a1n"], xT["f1"] = xT["a0"], xT["f0"]

        r_exp = sb("r_exp", [128, QT, E0])
        r_score = sb("r_score", [128, QT, E0])
        r_biased = sb("r_biased", [128, QT, E0])
        r_pair = sb("r_pair", [128, 4, QT, GROUPS0])
        r_top = sb("r_top", [128, 3, QT, GROUPS0])
        r_gsum = sb("r_gsum", [128, QT, GROUPS0])
        r_ge, r_gt = [bias_q[:, t, :].rearrange("p (t i j) -> p t i j", t=QT, i=E0) for t in range(QT)]
        r_rank = sb("r_rank", [128, QT, E0])
        r_keep = sb("r_keep", [128, QT, GROUPS0])
        r_drop = sb("r_drop", [128, QT, GROUPS0])
        r_small = sb("r_small", [128, 2, QT])
        combine = [[sb(f"combine{l}{b}", [128, QT, (E0, E1)[l]]) for b in range(B)] for l in range(2)]
        c_part = sb("c_part", [128, QT, PARTS, E0], BF16)
        c_rest = sb("c_rest", [128, QT, E0])
        c_rows = [sb(f"c_rows{b}", [PARTS * E0, S], BF16) for b in range(B)]
        cT1 = [sb(f"cT1{b}", [E1, S]) for b in range(B)]

        def late(at, size, pattern, **kw):
            return early[:, at:at + size].rearrange(pattern, **kw)

        silu_g, gated, hid0 = [late(i * 4 * S, 4 * S, "p (u j s) -> p u j s", u=2, j=2) for i in range(3)]
        hn1 = late(12 * S, 2 * QT * 2 * H1, "p (u t e n) -> p u t e n", u=2, t=QT, e=2)
        hid1 = late(12 * S + 2 * QT * 2 * H1, 8 * S, "p (u k s) -> p u k s", u=2, k=4)
        st1 = sb("st1", [128, 4, 6])
        mv1 = sb("mv1", [128, 2, 4, 2])
        ve1 = sb("ve1", [128, 4])
        rs1 = sb("rs1", [128, 2, 4])
        acc = [shared_area[:, (4 + b) * S:(5 + b) * S].rearrange("p (t d) -> p t d", t=QT) for b in range(B)]
        result = x_sb

        bank = ctx.enter_context(nc.psum_tensor("bank", [128, 8, 512], F32))
        MISC, OUT = 7, 6

        ld = {n: sem(f"ld_{n}") for n in ("ctx0", "ctx1", "x", "aw0", "aw1", "col", "row", "ident", "mask",
                                          "router", "wg0", "wu0", "wd0", "sel", "wu1", "bu1", "wd1")}
        consts_ready = sem("consts_ready")
        half_ready = sem("half_ready")
        v_zeroed = [sem(f"v_zeroed{l}") for l in range(2)]
        ones_ready = sem("ones_ready")
        k_ones = sem("k_ones")
        mask_ready = sem("mask_ready")
        sel_ready = sem("sel_ready")
        bu1_split = sem("bu1_split")
        bu1_ready = sem("bu1_ready")
        k_proj = sem("k_proj")
        k_evacuated = sem("k_evacuated")
        k_rest_ready = [sem(f"k_rest_ready{i}") for i in range(4)]
        k_second = sem("k_second")
        k_parts = [sem(f"k_parts{i}") for i in range(4)]
        k_written = [sem(f"k_written{i}") for i in range(4)]
        k_stacked = [sem(f"k_stacked{i}") for i in range(4)]
        q_parts = [sem(f"q_parts{i}") for i in range(4)]
        q_written = [sem(f"q_written{i}") for i in range(4)]
        q_stacked = [sem(f"q_stacked{i}") for i in range(4)]
        v_proj = sem("v_proj")
        v_ready = sem("v_ready")
        misc_ready = sem("misc_ready")
        misc_free = sem("misc_free")
        for_max = sem("for_max")
        max_done = sem("max_done")
        max_parts = sem("max_parts")
        max_copied = sem("max_copied")
        max_stacked = [sem("max_stacked0"), sem("max_stacked1")]
        scores_ready = sem("scores_ready")
        exp_done = sem("exp_done")
        pv_done = sem("pv_done")
        o_copied = sem("o_copied")
        att_done = sem("att_done")
        attT_done = sem("attT_done")
        var_ready = {n: sem(f"var_{n}") for n in norm}
        rstd_ready = {n: sem(f"rstd_{n}") for n in norm}
        normed = {n: sem(f"normed_{n}") for n in norm if n not in ("a1", "out")}
        xT_ready = {n: sem(f"xT_ready_{n}") for n in xT}
        res_ready = {s: sem(f"res_ready{s}") for s in (2, 3)}
        res_bias_ready = {s: sem(f"res_bias_ready{s}") for s in (0, 2, 3)}
        gate_in = sem("gate_in")
        gate_exp = [sem(f"gate_exp{l}") for l in range(2)]
        combined = [sem(f"combined{l}") for l in range(2)]
        c_ready = [sem(f"c_ready{l}") for l in range(2)]
        gu_ready = sem("gu_ready")
        silu_done = sem("silu_done")
        hid0_ready = sem("hid0_ready")
        down0_done = sem("down0_done")
        up1_ready = sem("up1_ready")
        var1_ready = sem("var1_ready")
        rstd1_ready = sem("rstd1_ready")
        norm1_done = sem("norm1_done")
        tr1_ready = sem("tr1_ready")
        gelu_done = sem("gelu_done")
        down1_done = sem("down1_done")
        acc_done = sem("acc_done")
        stored_ready = sem("stored_ready")
        stored = sem("stored")
        dve_step = sem("dve_step")
        pool_step = sem("pool_step")

        block = ctx.enter_context(nc.Block())
        use = {}

        @block.tensor
        def _(pe):
            mm = pe.matmul

            def misc(name):
                if use:
                    pe.wait_ge(misc_free, len(use))
                use[name] = len(use) + 1

            def k_projection(i):
                l, b = divmod(i, B)
                pe.wait_ge(ld[f"ctx{b}"], 16)
                pe.wait_ge(ld[f"aw{l}"], 16)
                mm(bank[:, i, :], aw[:, l, W_K, :], ctxT_sb[:, b, :], start=True, stop=True).then_inc(k_proj, 1)

            def v_projection(i, at):
                l, b = divmod(i, B)
                pe.wait_ge(ld[f"ctx{b}"], 16)
                pe.wait_ge(ld[f"aw{l}"], 16)
                for t in range(KT):
                    last = mm(bank[:, at, t * D:(t + 1) * D], ctxT_sb[:, b, t * 128:(t + 1) * 128],
                              aw[:, l, W_V, :], start=True, stop=True)
                last.then_inc(v_proj, 1)

            def transpose_tokens(n, b):
                pe.wait_ge(normed[n], QT * (b + 1))
                misc(f"xT_{n}{b}")
                for t in range(QT):
                    last = pe.transpose(bank[:, MISC, t * 128:(t + 1) * 128], norm[n][b][:, t, :], idf[:, :])
                last.then_inc(misc_ready, 1)

            def q_projection(l, b):
                n = ("a0", "a1n")[l]
                pe.wait_ge(xT_ready[n], b + 1)
                misc(f"q{l}{b}")
                mm(bank[:, MISC, 0:S], aw[:, l, W_Q, :], xT[n][b][:, :], start=True, stop=True).then_inc(misc_ready, 1)

            def score_rows(n, qt):
                l, b, h = n // HEADS, n % HEADS // H, n % H
                if h == 0 and qt == 0:
                    pe.wait_ge(k_stacked[l * B + b], 16)
                    pe.wait_ge(q_stacked[l * B + b], 16)
                if n == 0 and qt == 0:
                    pe.wait_ge(k_evacuated, 4)
                if n == HEADS and qt == 0:
                    pe.wait_ge(hid0_ready, 2 * 7)
                if n >= 1:
                    pe.wait_ge(max_done, 2 * (n - 1) + qt + 1)
                mm(bank[:, qt, :], q_stack[0:STACK, b, h, qt * 128:(qt + 1) * 128],
                   k_stack[0:STACK, b, h, :], start=True, stop=True).then_inc(for_max, 1)

            def max_transpose(g):
                pe.wait_ge(max_parts, g + 1)
                misc(f"max{g}")
                o = bank[0:PARTS * HG, MISC, 0:128].bitcast(BF16)
                for t in range(QT):
                    last = pe.transpose(o[:, t * 128:(t + 1) * 128], max_part[:, t].rearrange("p a h -> p (a h)"), idb[:, :])
                last.then_inc(misc_ready, 1)

            def score_cols(n, kts):
                l, b, h = n // HEADS, n % HEADS // H, n % H
                g = n // HG
                if kts[0] == 0:
                    if n % HG == 0:
                        pe.wait_ge(max_stacked[g % 2], 16 * PARTS * (g // 2 + 1))
                    if n == 0:
                        pe.wait_ge(k_ones, 16)
                        pe.wait_ge(v_ready, 3)
                    if n >= 2:
                        pe.wait_ge(exp_done, n - 1)
                at = 2 + 2 * (n % 2)
                for kt in kts:
                    o = bank[:, at + kt // 2, kt % 2 * S:(kt % 2 + 1) * S]
                    last = mm(o, k_stack[:, b, h, kt * 128:(kt + 1) * 128], q_stack[:, b, h, :],
                              start=True, stop=(l == 1))
                    if l == 0:
                        last = mm(o, idb[:, :], bias_k[:, kt, :], start=False, stop=True)
                if kts[-1] == KT - 1:
                    last.then_inc(scores_ready, 1)

            def values(g):
                l, b = g // (B * NG), g % (B * NG) // NG
                pe.wait_ge(exp_done, HG * (g + 1))
                pe.wait_ge(v_ready, l * B + b + 1)
                if g >= 1:
                    pe.wait_ge(o_copied, g)
                if g == B * NG:
                    pe.wait_ge(res_ready[2], QT * B)
                for kt in range(KT):
                    for j in range(HG):
                        h = g % NG * HG + j
                        last = mm(bank[VW * j:VW * (j + 1), OUT, 0:S], v_ext[l][:, b * KT + kt, h * (DK + 1):h * (DK + 1) + VW],
                                  probs[:, (g * HG + j) % (2 * HG), kt * S:(kt + 1) * S],
                                  start=(kt == 0), stop=(kt == KT - 1))
                last.then_inc(pv_done, 1)

            def o_transpose(g):
                pe.wait_ge(o_copied, g + 1)
                misc(f"o{g}")
                for t in range(QT):
                    last = pe.transpose(bank[:, MISC, t * 128:(t + 1) * 128], o_sb[:, g % 2, t * 128:(t + 1) * 128], idf[:, :])
                last.then_inc(misc_ready, 1)

            def att_transpose(l, b):
                pe.wait_ge(att_done, NG * (l * B + b + 1))
                misc(f"attT{l}{b}")
                for t in range(QT):
                    last = pe.transpose(bank[:, MISC, t * 128:(t + 1) * 128], att[l][b][:, t, :], idf[:, :])
                last.then_inc(misc_ready, 1)

            def out_projection(l, b):
                pe.wait_ge(attT_done, l * B + b + 1)
                misc(f"out{l}{b}")
                for t in range(QT):
                    last = mm(bank[:, MISC, t * D:(t + 1) * D], attT[l][b][:, t * 128:(t + 1) * 128], aw[:, l, W_O, :],
                              start=True, stop=True)
                last.then_inc(misc_ready, 1)

            def gate_logits(l, b):
                n, e, w = (("f0", E0, g0_sb), ("f1", E1, g1_sb))[l]
                pe.wait_ge(xT_ready[n], b + 1)
                pe.wait_ge(ld["router"], 16 * 4)
                misc(f"gate{l}{b}")
                for t in range(QT):
                    last = mm(bank[:, MISC, t * e:(t + 1) * e], xT[n][b][:, t * 128:(t + 1) * 128], w[:, :],
                              start=True, stop=True)
                last.then_inc(misc_ready, 1)

            def combine_transpose(l, b):
                pe.wait_ge(combined[l], b + 1)
                misc(f"c{l}{b}")
                for t in range(QT):
                    if l == 0:
                        o = bank[0:PARTS * E0, MISC, 0:128].bitcast(BF16)
                        last = pe.transpose(o[:, t * 128:(t + 1) * 128], c_part[:, t].rearrange("p a e -> p (a e)"), idb[:, :])
                    else:
                        last = pe.transpose(bank[0:E1, MISC, t * 128:(t + 1) * 128], combine[1][b][:, t, :], idf[:, :])
                last.then_inc(misc_ready, 1)

            def bias_down1(b):
                pe.wait_ge(c_ready[1], b + 1)
                misc(f"b2{b}")
                for t in range(QT):
                    last = mm(bank[:, MISC, t * D:(t + 1) * D], cT1[b][:, t * 128:(t + 1) * 128], bd1_sb[:, :],
                              start=True, stop=True)
                last.then_inc(misc_ready, 1)

            def up0(b, i):
                u = b * (T0 // 2 + 1) + i
                at, c_at = (0, 2) if u % 2 == 0 else (4, 3)
                if i == 0 and b == 0:
                    pe.wait_ge(max_done, 2 * HEADS)
                    pe.wait_ge(exp_done, HEADS)
                    pe.wait_ge(ld["wg0"], 16)
                    pe.wait_ge(ld["wu0"], 16)
                if i == 0:
                    pe.wait_ge(sel_ready, 1)
                    pe.wait_ge(c_ready[0], b + 1)
                if u >= 2:
                    pe.wait_ge(hid0_ready, u - 1)
                shared = i == T0 // 2
                m = I0 if shared else 128
                for j in range(1 if shared else 2):
                    t = 2 * i + j
                    mm(bank[0:m, at + j, 0:S], wg0_sb[:, t * 128:t * 128 + m], xT["f0"][b][:, :], start=True, stop=True)
                    last = mm(bank[0:m, at + j, S:2 * S], wu0_sb[:, t * 128:t * 128 + m], xT["f0"][b][:, :], start=True, stop=True)
                    if not shared:
                        last = mm(bank[:, c_at, j * S:(j + 1) * S], sel[:, t, :], c_rows[b][:, :], start=True, stop=True)
                last.then_inc(gu_ready, 1)

            def down0(b, i):
                u = b * (T0 // 2 + 1) + i
                shared = i == T0 // 2
                pe.wait_ge(hid0_ready, u + 1)
                if u == 0:
                    pe.wait_ge(o_copied, B * NG)
                    pe.wait_ge(ld["wd0"], 32)
                if b == 1 and i == 0:
                    pe.wait_ge(res_ready[2], QT)
                m = I0 if shared else 128
                for j in range(1 if shared else 2):
                    w = wsd0_sb[:, :] if shared else wd0_sb[:, 2 * i + j, :]
                    for t in range(QT):
                        last = mm(bank[:, OUT, t * D:(t + 1) * D], hid0[0:m, u % 2, j, t * 128:(t + 1) * 128], w,
                                  start=(i == 0 and j == 0 and t == 0), stop=shared, skip_group_check=True)
                last.then_inc(down0_done, 1)

            def up1(b, i):
                w = b * (E1 // 2) + i
                if w == 0:
                    pe.wait_ge(max_done, 4 * HEADS)
                    pe.wait_ge(exp_done, 2 * HEADS)
                    pe.wait_ge(ld["wu1"], 16)
                    pe.wait_ge(bu1_ready, 16 * PARTS)
                    pe.wait_ge(ones_ready, 1)
                if w >= 2:
                    pe.wait_ge(norm1_done, 4 * (w - 1))
                for t in range(QT):
                    o = bank[:, 2 * (w % 2) + t, :]
                    mm(o, xT["f1"][b][:, t * 128:(t + 1) * 128],
                       wu1_sb[:, 2 * i:2 * i + 2, :].rearrange("p e n -> p (e n)"), start=True, stop=False)
                    last = mm(o, ones_parts[:, 0:128], bu1_rows[:, 2 * i * H1:(2 * i + 2) * H1], start=False, stop=True)
                last.then_inc(up1_ready, 1)

            def transpose1(b, i):
                w = b * (E1 // 2) + i
                pe.wait_ge(norm1_done, 4 * (w + 1))
                if w >= 1:
                    pe.wait_ge(gelu_done, 4 * w)
                for e in range(2):
                    for half in range(2):
                        for t in range(QT):
                            at = half * S + t * 128
                            last = pe.transpose(bank[:, 4 + e, at:at + 128],
                                                hn1[:, w % 2, t, e, half * 128:(half + 1) * 128], idf[:, :])
                        last.then_inc(tr1_ready, 1)

            def down1(b, i):
                w = b * (E1 // 2) + i
                pe.wait_ge(gelu_done, 4 * (w + 1))
                if w == 0:
                    pe.wait_ge(o_copied, 2 * B * NG)
                    pe.wait_ge(ld["wd1"], 32)
                if w >= 1:
                    pe.wait_ge(acc_done, 4 * w)
                for e in range(2):
                    for t in range(QT):
                        for half in range(2):
                            last = mm(bank[:, OUT, (e * QT + t) * D:(e * QT + t + 1) * D],
                                      hid1[:, w % 2, 2 * e + half, t * 128:(t + 1) * 128],
                                      wd1_sb[:, 2 * (2 * i + e) + half, :], start=(half == 0), stop=(half == 1))
                last.then_inc(down1_done, 1)

            def attention(l, extra):
                for s in range(BATCH_STEPS):
                    n, m = l * HEADS + s, l * HEADS + s - LAG
                    if s < HEADS:
                        score_rows(n, 0)
                    if 0 <= s - LAG < HEADS:
                        score_cols(m, range(0, KT // 2))
                    if s < HEADS:
                        score_rows(n, 1)
                    if 0 <= s - LAG < HEADS:
                        score_cols(m, range(KT // 2, KT))
                    if s % HG == 1 and 0 <= (s - 5) // HG < B * NG:
                        max_transpose(l * B * NG + (s - 5) // HG)
                    if s % HG == 1 and s >= 13:
                        o_transpose(l * B * NG + (s - 13) // HG)
                    if s % HG == 0 and s >= 12:
                        values(l * B * NG + (s - 12) // HG)
                    for f in extra.get(s, []):
                        f()

            pe.wait_ge(consts_ready, 1)
            k_projection(0)
            transpose_tokens("a0", 0)
            v_projection(0, 4)
            q_projection(0, 0)
            k_projection(1)
            transpose_tokens("a0", 1)
            v_projection(1, 5)
            q_projection(0, 1)
            k_projection(2)
            k_projection(3)

            def v_rest():
                pe.wait_ge(v_ready, 1)
                v_projection(2, 4)
                v_projection(3, 6)

            attention(0, {
                2: [v_rest],
                27: [lambda: att_transpose(0, 0)],
                28: [lambda: out_projection(0, 0)],
                30: [lambda: transpose_tokens("f0", 0)],
                31: [lambda: gate_logits(0, 0)],
                36: [lambda: combine_transpose(0, 0)],
            })

            def experts0(b, extra):
                up0(b, 0)
                for i in range(1, T0 // 2 + 1):
                    up0(b, i)
                    down0(b, i - 1)
                    for f in extra.get(i, []):
                        f()
                down0(b, T0 // 2)

            experts0(0, {
                1: [lambda: att_transpose(0, 1)],
                2: [lambda: out_projection(0, 1)],
                3: [lambda: transpose_tokens("f0", 1)],
                4: [lambda: gate_logits(0, 1)],
                6: [lambda: combine_transpose(0, 1)],
            })
            experts0(1, {
                3: [lambda: transpose_tokens("a1n", 0)],
                4: [lambda: q_projection(1, 0)],
            })
            attention(1, {
                2: [lambda: transpose_tokens("a1n", 1)],
                3: [lambda: q_projection(1, 1)],
                27: [lambda: att_transpose(1, 0)],
                28: [lambda: out_projection(1, 0)],
                30: [lambda: transpose_tokens("f1", 0)],
                31: [lambda: gate_logits(1, 0)],
                34: [lambda: combine_transpose(1, 0)],
                36: [lambda: bias_down1(0)],
            })

            steps = [(b, i) for b in range(B) for i in range(E1 // 2)]
            tail = {0: [lambda: att_transpose(1, 1)], 1: [lambda: out_projection(1, 1)],
                    2: [lambda: transpose_tokens("f1", 1), lambda: gate_logits(1, 1)],
                    3: [lambda: combine_transpose(1, 1), lambda: bias_down1(1)]}
            for k in range(len(steps) + 2):
                if k < len(steps):
                    up1(*steps[k])
                if 1 <= k <= len(steps):
                    transpose1(*steps[k - 1])
                if k >= 2:
                    down1(*steps[k - 2])
                for f in tail.get(k, []):
                    f()

        @block.vector
        def _(dve):
            steps = [0]

            def then(ins):
                steps[0] += 1
                ins.then_inc(dve_step, 1)
                dve.wait_ge(dve_step, steps[0])

            def noted(ins):
                steps[0] += 1
                ins.then_inc(dve_step, 1)

            tt, ts, copy = dve.tensor_tensor, dve.tensor_scalar, dve.tensor_copy

            def norm_stats(n, b, src):
                for t in range(QT):
                    (then if t == QT - 1 else noted)(dve.bn_stats(stats[:, t, :], src[:, t, :]))
                for t in range(QT):
                    dve.bn_aggr(mean_var[n, b][:, t, :], stats[:, t, :]).then_inc(var_ready[n], 1)

            def normalise(n, b, src):
                dve.wait_ge(rstd_ready[n], b + 1)
                for t in range(QT):
                    ins = ts(norm[n][b][:, t, :], src[:, t, :], mean_var[n, b][:, t, 0:1], rstd[n, b][:, t:t + 1],
                             ALU.subtract, ALU.mult)
                    if n in normed:
                        ins.then_inc(normed[n], 1)
                    else:
                        (then if t == QT - 1 else noted)(ins)

            def xT_copy(n, b):
                dve.wait_ge(misc_ready, use[f"xT_{n}{b}"])
                if n == "a1n":
                    then(ts(xT[n][b][:, :], bank[:, MISC, 0:S], col[:, COL_LNG:COL_LNG + 1],
                            col[:, COL_LNB:COL_LNB + 1], ALU.mult, ALU.add))
                else:
                    then(copy(xT[n][b][:, :], bank[:, MISC, 0:S]))
                dve.sem_inc(xT_ready[n], 1)
                dve.sem_inc(misc_free, 1)

            def q_split(l, b):
                i = l * B + b
                c = (COL_BQ0, COL_BQ1)[l]
                dve.wait_ge(misc_ready, use[f"q{l}{b}"])
                then(ts(q_full[:, :], bank[:, MISC, 0:S], col[:, c:c + 1], SCALE, ALU.add, ALU.mult))
                dve.sem_inc(misc_free, 1)
                if l == 1:
                    dve.wait_ge(q_written[b], 16 * PARTS)
                then(copy(q_part[b][:, 0, :], q_full[:, :]))
                then(tt(q_rest[:, :], q_full[:, :], q_part[b][:, 0, :], ALU.subtract))
                then(copy(q_part[b][:, 1, :], q_rest[:, :]))
                tt(q_part[b][:, 2, :], q_rest[:, :], q_part[b][:, 1, :], ALU.subtract).then_inc(q_parts[i], 1)

            def v_copy(i, at):
                l, b = divmod(i, B)
                dve.wait_ge(v_proj, i + 1)
                dve.wait_ge(v_zeroed[l], 2)
                dve.wait_ge(ld["row"], 16)
                src = bank[:, at, :].rearrange("p (t h d) -> p t h d", t=KT, h=H)
                bias = row[:, ROW_NAMES.index(f"bv{l}"), :].rearrange("p (h d) -> p h d", h=H)
                for t in range(KT):
                    ins = tt(v_heads[l][:, b * KT + t, :, 0:DK], src[:, t], bias, ALU.add)
                    (then if t == KT - 1 else noted)(ins)
                dve.sem_inc(v_ready, 1)

            def head_max(n, qt):
                dve.wait_ge(for_max, 2 * n + qt + 1)
                g = n // HG
                o = row_max[:, g % 2, n % HG, qt:qt + 1]
                if 2 * n + qt >= 2:
                    dve.wait_ge(max_done, 2 * n + qt - 1)
                if n < HEADS:
                    ins = dve.tensor_tensor_reduce(discard[:, qt, :], bank[:, qt, :], bias_q[:, qt, :], 1.0, LOWEST,
                                                   ALU.add, ALU.max, o)
                else:
                    ins = dve.tensor_reduce(o, bank[:, qt, :], AX.X, ALU.max)
                ins.then_inc(max_done, 1)

            def max_split(g):
                dve.wait_ge(max_done, 2 * HG * (g + 1))
                if g >= 1:
                    dve.wait_ge(misc_ready, use[f"max{g - 1}"])
                m = row_max[:, g % 2]
                part = [max_part[:, :, a, :].rearrange("p t h -> p h t") for a in range(PARTS)]
                then(ts(part[0], m, -1.0, None, ALU.mult))
                then(dve.scalar_tensor_tensor(out=max_rest[:, :, :], in0=m, scalar=-1.0, in1=part[0],
                                              op0=ALU.mult, op1=ALU.subtract))
                then(copy(part[1], max_rest[:, :, :]))
                tt(part[2], max_rest[:, :, :], part[1], ALU.subtract).then_inc(max_parts, 1)

            def max_copy(g):
                dve.wait_ge(misc_ready, use[f"max{g}"])
                if g >= 2:
                    dve.wait_ge(max_stacked[g % 2], 16 * PARTS * (g // 2))
                then(copy(max_rows[:, g % 2, :], bank[0:PARTS * HG, MISC, 0:128].bitcast(BF16)))
                dve.sem_inc(max_copied, 1)
                dve.sem_inc(misc_free, 1)

            def divide(g):
                l, b = g // (B * NG), g % (B * NG) // NG
                dve.wait_ge(misc_ready, use[f"o{g}"])
                src = bank[:, MISC, 0:S].rearrange("p (t j v) -> p t j v", t=QT, j=HG)
                then(dve.reciprocal(rden[:, :, :], src[:, :, :, DK]))
                o = att[l][b][:, :, g % NG * HG * DK:(g % NG + 1) * HG * DK].rearrange("p t (j d) -> p t j d", j=HG)
                then(tt(o, src[:, :, :, 0:DK], rden[:, :, :].unsqueeze(3).to_broadcast([128, QT, HG, DK]), ALU.mult))
                dve.sem_inc(att_done, 1)
                dve.sem_inc(misc_free, 1)

            def attT_copy(l, b):
                dve.wait_ge(misc_ready, use[f"attT{l}{b}"])
                then(copy(attT[l][b][:, :], bank[:, MISC, 0:S]))
                dve.sem_inc(attT_done, 1)
                dve.sem_inc(misc_free, 1)

            def add_attention(l, b):
                s = 2 * l
                dve.wait_ge(misc_ready, use[f"out{l}{b}"])
                dve.wait_ge(res_bias_ready[s], b + 1)
                r = res[s + 1][b]
                then(tt(r, bank[:, MISC, 0:S].rearrange("p (t d) -> p t d", t=QT), res_bias[s][b][:, :, :], ALU.add))
                dve.sem_inc(misc_free, 1)
                if s + 1 == 3:
                    dve.sem_inc(res_ready[3], 1)
                norm_stats(("f0", "f1")[l], b, r)

            def ranks(values, e, beats_ge, beats_gt):
                mine = values.unsqueeze(3).to_broadcast([128, QT, e, e])
                other = values.unsqueeze(2).to_broadcast([128, QT, e, e])
                ge, gt = beats_ge[:, :, 0:e, 0:e], beats_gt[:, :, 0:e, 0:e]
                noted(tt(ge, other, mine, ALU.is_ge))
                then(tt(gt, other, mine, ALU.is_gt))
                for t in range(QT):
                    ins = tt(ge[:, t], ge[:, t], tie[:, 0:e, 0:e], ALU.mult)
                    (then if t == QT - 1 else noted)(ins)
                for t in range(QT):
                    ins = tt(gt[:, t], gt[:, t], ge[:, t], ALU.max)
                    (then if t == QT - 1 else noted)(ins)
                then(dve.tensor_reduce(r_rank[:, :, 0:e], gt, AX.X, ALU.add))

            def route0(b):
                dve.wait_ge(gate_exp[0], b + 1)
                then(ts(r_exp[:, :, :], r_exp[:, :, :], 1.0, None, ALU.add))
                then(dve.reciprocal(r_score[:, :, :], r_exp[:, :, :]))
                for t in range(QT):
                    ins = tt(r_biased[:, t, :], r_score[:, t, :], gbias[:, :], ALU.add)
                    (then if t == QT - 1 else noted)(ins)
                v = r_biased[:, :, :].rearrange("p t (g k) -> p t g k", g=GROUPS0)
                for i, (op, lo) in enumerate(((ALU.max, 0), (ALU.min, 0), (ALU.max, 2), (ALU.min, 2))):
                    ins = tt(r_pair[:, i], v[:, :, :, lo], v[:, :, :, lo + 1], op)
                    (then if i == 3 else noted)(ins)
                noted(tt(r_top[:, 0], r_pair[:, 0], r_pair[:, 2], ALU.max))
                noted(tt(r_top[:, 1], r_pair[:, 0], r_pair[:, 2], ALU.min))
                then(tt(r_top[:, 2], r_pair[:, 1], r_pair[:, 3], ALU.max))
                then(tt(r_top[:, 1], r_top[:, 1], r_top[:, 2], ALU.max))
                then(tt(r_gsum[:, :, :], r_top[:, 0], r_top[:, 1], ALU.add))
                ranks(r_gsum[:, :, :], GROUPS0, r_ge, r_gt)
                noted(ts(r_keep[:, :, :], r_rank[:, :, 0:GROUPS0], 2.0, None, ALU.is_lt))
                then(ts(r_drop[:, :, :], r_rank[:, :, 0:GROUPS0], 2.0, LOWEST, ALU.is_ge, ALU.mult))
                for t in range(QT):
                    keep = r_keep[:, t, :].unsqueeze(2).to_broadcast([128, GROUPS0, E0 // GROUPS0])
                    ins = tt(v[:, t], v[:, t], keep, ALU.mult)
                    (then if t == QT - 1 else noted)(ins)
                for t in range(QT):
                    drop = r_drop[:, t, :].unsqueeze(2).to_broadcast([128, GROUPS0, E0 // GROUPS0])
                    ins = tt(v[:, t], v[:, t], drop, ALU.add)
                    (then if t == QT - 1 else noted)(ins)
                ranks(r_biased[:, :, :], E0, r_ge, r_gt)
                c = combine[0][b]
                then(dve.scalar_tensor_tensor(out=c[:, :, :], in0=r_rank[:, :, :], scalar=4.0, in1=r_score[:, :, :],
                                              op0=ALU.is_lt, op1=ALU.mult))
                then(dve.tensor_reduce(r_small[:, 0, :], c[:, :, :], AX.X, ALU.add))
                then(ts(r_small[:, 0, :], r_small[:, 0, :], 1e-20, None, ALU.add))
                then(dve.reciprocal(r_small[:, 1, :], r_small[:, 0, :]))
                for t in range(QT):
                    ins = ts(c[:, t, :], c[:, t, :], r_small[:, 1, t:t + 1], 2.5, ALU.mult, ALU.mult)
                    (then if t == QT - 1 else noted)(ins)
                then(copy(c_part[:, :, 0, :], c[:, :, :]))
                then(tt(c_rest[:, :, :], c[:, :, :], c_part[:, :, 0, :], ALU.subtract))
                then(copy(c_part[:, :, 1, :], c_rest[:, :, :]))
                tt(c_part[:, :, 2, :], c_rest[:, :, :], c_part[:, :, 1, :], ALU.subtract).then_inc(combined[0], 1)

            def c_copy(l, b):
                dve.wait_ge(misc_ready, use[f"c{l}{b}"])
                if l == 0:
                    then(copy(c_rows[b][:, :], bank[0:PARTS * E0, MISC, 0:128].bitcast(BF16)))
                else:
                    then(copy(cT1[b][:, :], bank[0:E1, MISC, 0:S]))
                dve.sem_inc(c_ready[l], 1)
                dve.sem_inc(misc_free, 1)

            def gate_shift1(b):
                dve.wait_ge(misc_ready, use[f"gate1{b}"])
                src = bank[:, MISC, 0:QT * E1].rearrange("p (t e) -> p t e", t=QT)
                then(dve.tensor_reduce(r_small[:, 0, :], src, AX.X, ALU.max))
                then(tt(r_score[:, :, 0:E1], src, r_small[:, 0, :].unsqueeze(2).to_broadcast([128, QT, E1]), ALU.subtract))
                dve.sem_inc(misc_free, 1)
                dve.sem_inc(gate_in, 1)

            def route1(b):
                dve.wait_ge(gate_exp[1], b + 1)
                e = r_exp[:, :, 0:E1]
                then(dve.tensor_reduce(r_small[:, 0, :], e, AX.X, ALU.add))
                then(dve.reciprocal(r_small[:, 1, :], r_small[:, 0, :]))
                then(tt(r_score[:, :, 0:E1], e, r_small[:, 1, :].unsqueeze(2).to_broadcast([128, QT, E1]), ALU.mult))
                ranks(r_score[:, :, 0:E1], E1, r_ge, r_gt)
                c = combine[1][b]
                then(dve.scalar_tensor_tensor(out=c[:, :, :], in0=r_rank[:, :, 0:E1], scalar=2.0, in1=r_score[:, :, 0:E1],
                                              op0=ALU.is_lt, op1=ALU.mult))
                then(dve.tensor_reduce(r_small[:, 0, :], c[:, :, :], AX.X, ALU.add))
                then(dve.reciprocal(r_small[:, 1, :], r_small[:, 0, :]))
                tt(c[:, :, :], c[:, :, :], r_small[:, 1, :].unsqueeze(2).to_broadcast([128, QT, E1]), ALU.mult)\
                    .then_inc(combined[1], 1)

            def hidden0(b, i):
                u = b * (T0 // 2 + 1) + i
                at, c_at = (0, 2) if u % 2 == 0 else (4, 3)
                dve.wait_ge(silu_done, u + 1)
                if u >= 2:
                    dve.wait_ge(down0_done, u - 1)
                if i == T0 // 2:
                    tt(hid0[0:I0, u % 2, 0, :], silu_g[0:I0, u % 2, 0, :], bank[0:I0, at, S:2 * S], ALU.mult)\
                        .then_inc(hid0_ready, 1)
                    return
                then(tt(gated[:, u % 2], silu_g[:, u % 2], bank[:, at:at + 2, S:2 * S], ALU.mult))
                tt(hid0[:, u % 2], gated[:, u % 2], bank[:, c_at, :].rearrange("p (j s) -> p j s", j=2), ALU.mult)\
                    .then_inc(hid0_ready, 1)

            def add_experts0(b):
                dve.wait_ge(down0_done, (b + 1) * (T0 // 2 + 1))
                for t in range(QT):
                    ins = tt(res[2][b][:, t, :], bank[:, OUT, t * D:(t + 1) * D], res[1][b][:, t, :], ALU.add)
                    ins.then_inc(res_ready[2], 1)
                dve.wait_ge(res_ready[2], QT * (b + 1))
                norm_stats("a1", b, res[2][b])

            def norm_twice(b):
                normalise("a1", b, res[2][b])
                norm_stats("a1n", b, norm["a1"][b])
                normalise("a1n", b, norm["a1"][b])

            def stats1(b, i):
                w = b * (E1 // 2) + i
                dve.wait_ge(up1_ready, w + 1)
                if w >= 2:
                    dve.wait_ge(rstd1_ready, w - 1)
                for t in range(QT):
                    for e in range(2):
                        k = 2 * t + e
                        ins = dve.bn_stats(st1[:, k, :], bank[:, 2 * (w % 2) + t, e * H1:(e + 1) * H1])
                        (then if k == 3 else noted)(ins)
                for k in range(4):
                    dve.bn_aggr(mv1[:, w % 2, k, :], st1[:, k, :]).then_inc(var1_ready, 1)

            def normalise1(b, i):
                w = b * (E1 // 2) + i
                dve.wait_ge(rstd1_ready, w + 1)
                if w >= 2:
                    dve.wait_ge(tr1_ready, 4 * (w - 1))
                for t in range(QT):
                    for e in range(2):
                        k = 2 * t + e
                        ts(hn1[:, w % 2, t, e, :], bank[:, 2 * (w % 2) + t, e * H1:(e + 1) * H1],
                           mv1[:, w % 2, k, 0:1], rs1[:, w % 2, k:k + 1], ALU.subtract, ALU.mult).then_inc(norm1_done, 1)

            def start_acc(b):
                dve.wait_ge(misc_ready, use[f"b2{b}"])
                then(tt(acc[b][:, :, :], bank[:, MISC, 0:S].rearrange("p (t d) -> p t d", t=QT), norm["f1"][b][:, :, :], ALU.add))
                dve.sem_inc(misc_free, 1)

            def accumulate1(b, i):
                w = b * (E1 // 2) + i
                dve.wait_ge(down1_done, w + 1)
                for e in range(2):
                    if e == 1:
                        dve.wait_ge(acc_done, 4 * w + QT)
                    elif i >= 1:
                        dve.wait_ge(acc_done, 4 * w)
                    for t in range(QT):
                        at = (e * QT + t) * D
                        dve.scalar_tensor_tensor(out=acc[b][:, t, :], in0=bank[:, OUT, at:at + D],
                                                 scalar=combine[1][b][:, t, 2 * i + e:2 * i + e + 1], in1=acc[b][:, t, :],
                                                 op0=ALU.mult, op1=ALU.add).then_inc(acc_done, 1)

            def last_stats(b):
                dve.wait_ge(acc_done, 4 * (E1 // 2) * (b + 1))
                norm_stats("out", b, acc[b])

            def finish(b):
                normalise("out", b, acc[b])
                g = row[:, ROW_NAMES.index("lnf_g"), :].unsqueeze(1).to_broadcast([128, QT, D])
                then(tt(norm["out"][b][:, :, :], norm["out"][b][:, :, :], g, ALU.mult))
                dve.wait_ge(res_bias_ready[3], b + 1)
                tt(result[:, b], norm["out"][b][:, :, :], res_bias[3][b][:, :, :], ALU.add).then_inc(stored_ready, 1)

            def attention(l, extra):
                for s in range(BATCH_STEPS + 1):
                    n = l * HEADS + s
                    if s < HEADS:
                        head_max(n, 0)
                        head_max(n, 1)
                        if s % HG == HG - 1:
                            max_split(n // HG)
                    if s % HG == 1 and 0 <= (s - 5) // HG < B * NG:
                        max_copy(l * B * NG + (s - 5) // HG)
                    if s % HG == 2 and s >= 14:
                        divide(l * B * NG + (s - 14) // HG)
                    for f in extra.get(s, []):
                        f()

            dve.wait_ge(ld["x"], 16)
            norm_stats("a0", 0, x_sb[:, 0])
            normalise("a0", 0, x_sb[:, 0])
            norm_stats("a0", 1, x_sb[:, 1])
            dve.wait_ge(k_evacuated, 1)
            tt(k_rest[0][:, :], k_full[0][:, :], k_part[0][:, 0, :], ALU.subtract).then_inc(k_rest_ready[0], 1)
            xT_copy("a0", 0)
            dve.wait_ge(k_second, 1)
            tt(k_part[0][:, 2, :], k_rest[0][:, :], k_part[0][:, 1, :], ALU.subtract).then_inc(k_parts[0], 1)
            dve.wait_ge(ld["col"], 16)
            q_split(0, 0)
            normalise("a0", 1, x_sb[:, 1])
            dve.wait_ge(ld["mask"], 32)
            ts(bias_q[:, :, :], mask_q[:, :, :], 0.0, MASKED, ALU.is_equal, ALU.mult).then_inc(mask_ready, 1)
            xT_copy("a0", 1)
            q_split(0, 1)
            v_copy(0, 4)
            v_copy(1, 5)
            ts(bias_k[:, :, :], mask_k[:, :, :], 0.0, MASKED, ALU.is_equal, ALU.mult).then_inc(mask_ready, 1)
            dve.wait_ge(mask_ready, 2)
            dve.wait_ge(ld["router"], 16 * 4)

            attention(0, {
                2: [lambda: v_copy(2, 4)],
                3: [lambda: v_copy(3, 6)],
                27: [lambda: attT_copy(0, 0)],
                28: [lambda: add_attention(0, 0)],
                29: [lambda: normalise("f0", 0, res[1][0])],
                30: [lambda: xT_copy("f0", 0)],
                32: [lambda: route0(0)],
                36: [lambda: c_copy(0, 0)],
            })

            def experts0(b, extra):
                for i in range(T0 // 2 + 1):
                    hidden0(b, i)
                    for f in extra.get(i, []):
                        f()
                add_experts0(b)

            experts0(0, {
                0: [lambda: attT_copy(0, 1)],
                1: [lambda: add_attention(0, 1), lambda: normalise("f0", 1, res[1][1])],
                2: [lambda: xT_copy("f0", 1)],
                4: [lambda: route0(1)],
                5: [lambda: c_copy(0, 1)],
            })
            experts0(1, {
                1: [lambda: norm_twice(0)],
                2: [lambda: xT_copy("a1n", 0)],
                3: [lambda: q_split(1, 0)],
            })
            dve.wait_ge(sel_ready, 1)
            attention(1, {
                0: [lambda: norm_twice(1)],
                2: [lambda: xT_copy("a1n", 1)],
                3: [lambda: q_split(1, 1)],
                27: [lambda: attT_copy(1, 0)],
                28: [lambda: add_attention(1, 0)],
                29: [lambda: normalise("f1", 0, res[3][0])],
                30: [lambda: xT_copy("f1", 0)],
                31: [lambda: gate_shift1(0)],
                32: [lambda: route1(0)],
                34: [lambda: c_copy(1, 0)],
                36: [lambda: start_acc(0)],
            })
            steps1 = [(b, i) for b in range(B) for i in range(E1 // 2)]
            tail = {0: [lambda: attT_copy(1, 1)],
                    1: [lambda: add_attention(1, 1), lambda: normalise("f1", 1, res[3][1])],
                    2: [lambda: xT_copy("f1", 1), lambda: gate_shift1(1), lambda: route1(1)],
                    3: [lambda: c_copy(1, 1), lambda: start_acc(1)]}
            for k in range(len(steps1) + 2):
                if k < len(steps1):
                    stats1(*steps1[k])
                    normalise1(*steps1[k])
                if k >= 2:
                    accumulate1(*steps1[k - 2])
                    if steps1[k - 2][1] == E1 // 2 - 1:
                        last_stats(steps1[k - 2][0])
                        finish(steps1[k - 2][0])
                for f in tail.get(k, []):
                    f()

        @block.scalar
        def _(act):
            def k_evacuate(i):
                c = (COL_BK0, COL_BK1)[i // B]
                act.wait_ge(k_proj, i + 1)
                act.activation(k_full[i][:, :], bank[:, i, :], ACT.Identity, bias=col[:, c:c + 1])
                act.activation(k_part[i][:, 0, :], bank[:, i, :], ACT.Identity, bias=col[:, c:c + 1]).then_inc(k_evacuated, 1)

            def k_second_part(i):
                act.wait_ge(k_rest_ready[i], 1)
                act.copy(k_part[i][:, 1, :], k_rest[i][:, :]).then_inc(k_second, 1)

            act.dma_start(aw[:, 0], attn_w[:, 0]).then_inc(ld["aw0"], 16)
            act.dma_start(col[:, :], cols).then_inc(ld["col"], 16)
            act.dma_start(row[:, :, :], rows.to_broadcast([128, len(ROW_NAMES), D])).then_inc(ld["row"], 16)
            act.dma_start(aw[:, 1], attn_w[:, 1]).then_inc(ld["aw1"], 16)
            act.wait_ge(ld["col"], 16)
            k_evacuate(0)
            k_second_part(0)
            for i in range(1, 4):
                k_evacuate(i)
            for i in range(1, 4):
                k_second_part(i)

            def exponentials(n):
                g = n // HG
                act.wait_ge(scores_ready, n + 1)
                if n >= 2 * HG:
                    act.wait_ge(pv_done, g - 1)
                at = 2 + 2 * (n % 2)
                act.activation(probs[:, n % (2 * HG), :], bank[:, at:at + 2, :].rearrange("p a n -> p (a n)"), ACT.Exp)\
                    .then_inc(exp_done, 1)

            def o_copy(g):
                act.wait_ge(pv_done, g + 1)
                if g >= 2:
                    act.wait_ge(misc_ready, use[f"o{g - 2}"])
                act.copy(o_sb[:, g % 2, :], bank[:, OUT, 0:S]).then_inc(o_copied, 1)

            def gate_exponential(l, b):
                e, src = (E0, bank[:, MISC, 0:QT * E0].rearrange("p (t e) -> p t e", t=QT)) if l == 0 else \
                    (E1, r_score[:, :, 0:E1])
                if l == 0:
                    act.wait_ge(misc_ready, use[f"gate0{b}"])
                else:
                    act.wait_ge(gate_in, b + 1)
                if b == 1:
                    act.wait_ge(combined[l], 1)
                elif l == 1:
                    act.wait_ge(combined[0], B)
                ins = act.activation(r_exp[:, :, 0:e], src, ACT.Exp, scale=(-1.0, 1.0)[l])
                ins.then_inc(gate_exp[l], 1)
                if l == 0:
                    act.wait_ge(gate_exp[l], b + 1)
                    act.sem_inc(misc_free, 1)

            def attention(l, extra):
                for s in range(LAG, BATCH_STEPS):
                    if s % HG == 1 and s >= 13:
                        o_copy(l * B * NG + (s - 13) // HG)
                    if s - LAG < HEADS:
                        exponentials(l * HEADS + s - LAG)
                    for f in extra.get(s, []):
                        f()

            def silu(b, i):
                u = b * (T0 // 2 + 1) + i
                at = 0 if u % 2 == 0 else 4
                act.wait_ge(gu_ready, u + 1)
                if u >= 2:
                    act.wait_ge(hid0_ready, u - 1)
                if i == T0 // 2:
                    ins = act.activation(silu_g[0:I0, u % 2, 0, :], bank[0:I0, at, 0:S], ACT.Silu)
                else:
                    ins = act.activation(silu_g[:, u % 2], bank[:, at:at + 2, 0:S], ACT.Silu)
                ins.then_inc(silu_done, 1)

            def gelu1(b, i):
                w = b * (E1 // 2) + i
                if w >= 2:
                    act.wait_ge(down1_done, w - 1)
                for e in range(2):
                    for half in range(2):
                        k = 2 * e + half
                        c = 2 * (2 * i + e) + half
                        act.wait_ge(tr1_ready, 4 * w + 2 * e + 2)
                        act.activation(hid1[:, w % 2, k, :], bank[:, 4 + e, half * S:(half + 1) * S], ACT.Gelu,
                                       bias=col[:, COL_B1 + c:COL_B1 + c + 1],
                                       scale=col[:, COL_G1 + c:COL_G1 + c + 1]).then_inc(gelu_done, 1)

            act.wait_ge(mask_ready, 2)
            attention(0, {31: [lambda: gate_exponential(0, 0)]})
            for i in range(4):
                act.wait_ge(k_written[i], 16 * PARTS)
            for b in range(B):
                for i in range(T0 // 2 + 1):
                    silu(b, i)
                    if (b, i) == (0, 4):
                        gate_exponential(0, 1)
            attention(1, {31: [lambda: gate_exponential(1, 0)]})
            for b in range(B):
                for i in range(E1 // 2):
                    gelu1(b, i)
                    if (b, i) == (0, 1):
                        gate_exponential(1, 1)

        @block.gpsimd
        def _(pool):
            steps = [0]

            def then(ins):
                steps[0] += 1
                ins.then_inc(pool_step, 1)
                pool.wait_ge(pool_step, steps[0])

            def root(n, b):
                pool.wait_ge(var_ready[n], QT * (b + 1))
                then(pool.tensor_scalar(var_eps[:, :], mean_var[n, b][:, :, 1], EPS, None, ALU.add))
                pool.tensor_tensor(rstd[n, b][:, :], var_eps[:, :], minus_half[:, 0:QT], ALU.pow).then_inc(rstd_ready[n], 1)

            def add_row(s, b, name):
                r = row[:, ROW_NAMES.index(name), :].unsqueeze(1).to_broadcast([128, QT, D])
                pool.tensor_tensor(res_bias[s][b][:, :, :], res[s][b], r, ALU.add).then_inc(res_bias_ready[s], 1)

            then(pool.memset(minus_half[:, :], -0.5))
            pool.wait_ge(ld["ident"], 16)
            pool.tensor_copy(idb[:, :], idf[:, :]).then_inc(consts_ready, 1)
            root("a0", 0)
            pool.memset(ones_parts[:, :], 1.0).then_inc(ones_ready, 1)
            pool.memset(v_ext[0][:, :, H * (DK + 1):], 0.0).then_inc(v_zeroed[0], 1)
            pool.memset(v_heads[0][:, :, :, DK], 1.0).then_inc(v_zeroed[0], 1)
            root("a0", 1)

            for i in range(1, 4):
                l, b = divmod(i, B)
                pool.wait_ge(k_evacuated, i + 1)
                pool.tensor_tensor(k_rest[i][:, :], k_full[i][:, :], k_part[i][:, 0, :], ALU.subtract).then_inc(k_rest_ready[i], 1)
                pool.wait_ge(k_second, i + 1)
                pool.tensor_tensor(k_part[i][:, 2, :], k_rest[i][:, :], k_part[i][:, 1, :], ALU.subtract).then_inc(k_parts[i], 1)
                pool.wait_ge(k_parts[i], 1)
                for a in range(PARTS):
                    pool.dma_start(k_bounce[i][a].rearrange("a p s -> p a s"), k_part[i][:, :, :]).then_inc(k_written[i], 16)
                if l == 0:
                    pool.wait_ge(k_written[i], 16 * PARTS)
                if l == 0:
                    pool.dma_start(k_stack[0:STACK, b].rearrange("r h s -> r (h s)"),
                                   k_bounce[i].rearrange("i j (d h) s -> (i j d) (h s)", h=H)).then_inc(k_stacked[i], 16)

            pool.memset(v_ext[1][:, :, H * (DK + 1):], 0.0).then_inc(v_zeroed[1], 1)
            pool.memset(v_heads[1][:, :, :, DK], 1.0).then_inc(v_zeroed[1], 1)
            pool.wait_ge(ld["sel"], 16)
            pool.tensor_copy(sel[:, :, :], sel_f[:, :, :]).then_inc(sel_ready, 1)
            pool.wait_ge(ld["row"], 16)
            pool.wait_ge(ld["x"], 16)
            for b in range(B):
                add_row(0, b, "bo0")
            pool.wait_ge(ld["bu1"], 16)
            then(pool.tensor_copy(bu1_part[:, 0, :], bu1_sb[:, :]))
            then(pool.tensor_tensor(bu1_rest[:, :], bu1_sb[:, :], bu1_part[:, 0, :], ALU.subtract))
            then(pool.tensor_copy(bu1_part[:, 1, :], bu1_rest[:, :]))
            pool.tensor_tensor(bu1_part[:, 2, :], bu1_rest[:, :], bu1_part[:, 1, :], ALU.subtract).then_inc(bu1_split, 1)
            pool.wait_ge(bu1_split, 1)
            pool.wait_ge(k_proj, 4)
            pool.wait_ge(v_proj, 4)
            for a in range(PARTS):
                pool.dma_start(bu1_rows[a:a + 1, :].rearrange("o (p c) -> o p c", p=128),
                               bu1_part[:, a, :]).then_inc(bu1_ready, 16)

            for b in range(B):
                root("f0", b)
            for b in range(B):
                root("a1", b)
                root("a1n", b)
                pool.wait_ge(res_ready[2], QT * (b + 1))
                add_row(2, b, "bo1")

            def root1(w):
                pool.wait_ge(var1_ready, 4 * (w + 1))
                then(pool.tensor_scalar(ve1[:, :], mv1[:, w % 2, :, 1], EPS, None, ALU.add))
                pool.tensor_tensor(rs1[:, w % 2, :], ve1[:, :], minus_half[:, :], ALU.pow).then_inc(rstd1_ready, 1)

            root("f1", 0)
            pool.wait_ge(res_ready[3], 1)
            add_row(3, 0, "lnf_b")
            root1(0)
            root1(1)
            root("f1", 1)
            pool.wait_ge(res_ready[3], 2)
            add_row(3, 1, "lnf_b")
            for w in range(2, 6):
                root1(w)
            root("out", 0)
            for w in range(6, 8):
                root1(w)
            root("out", 1)

        @block.sync
        def _(sp):
            sp.dma_start(ctxT_sb[:, 0], ctxT[:, 0]).then_inc(ld["ctx0"], 16)
            sp.dma_start(x_sb[:, :, :, :], x.rearrange("b (t p) d -> p b t d", p=128)).then_inc(ld["x"], 16)
            sp.dma_start(idf[:, :], ident).then_inc(ld["ident"], 16)
            sp.dma_start(ctxT_sb[:, 1], ctxT[:, 1]).then_inc(ld["ctx1"], 16)
            sp.dma_start(mask_q[:, :, :], mask.rearrange("(t p) k -> p t k", p=128)).then_inc(ld["mask"], 16)
            sp.dma_start(mask_k[:, :, :], maskT.rearrange("(t p) q -> p t q", p=128)).then_inc(ld["mask"], 16)

            sp.wait_ge(ones_ready, 1)
            sp.dma_start(k_stack[STACK:ROWS_K].rearrange("r b h s -> r (b h) s"),
                         ones_parts[:, :].unsqueeze(1).to_broadcast([PARTS, B * H, S2])).then_inc(k_ones, 16)

            def bounce_out(dst, src, signal, by_part):
                for a in range(PARTS):
                    d = dst[:, a] if by_part else dst[a]
                    sp.dma_start(d.rearrange("a p s -> p a s"), src[:, :, :]).then_inc(signal, 16)

            def bounce_in(dst, src, signal):
                sp.dma_start(dst.rearrange("r h s -> r (h s)"),
                             src.rearrange("i j (d h) s -> (i j d) (h s)", h=H)).then_inc(signal, 16)

            def q_out(i):
                sp.wait_ge(q_parts[i], 1)
                bounce_out(q_bounce[i], q_part[i % B], q_written[i], True)

            def q_in(i):
                sp.wait_ge(q_written[i], 16 * PARTS)
                bounce_in(q_stack[0:STACK, i % B], q_bounce[i], q_stacked[i])

            sp.wait_ge(k_parts[0], 1)
            bounce_out(k_bounce[0], k_part[0], k_written[0], False)
            q_out(0)
            sp.wait_ge(k_written[0], 16 * PARTS)
            bounce_in(k_stack[0:STACK, 0], k_bounce[0], k_stacked[0])
            q_in(0)
            q_out(1)
            q_in(1)
            sp.dma_start(g0_sb[:, :], gate0).then_inc(ld["router"], 16)
            sp.dma_start(g1_sb[:, :], gate1).then_inc(ld["router"], 16)
            sp.dma_start(gbias[:, :], gate_bias.to_broadcast([128, E0])).then_inc(ld["router"], 16)
            sp.dma_start(tie[:, :, :], ties.to_broadcast([128, E0, E0])).then_inc(ld["router"], 16)

            def max_in(g):
                l, b, h = g // (B * NG), g % (B * NG) // NG, g % NG * HG
                sp.wait_ge(max_copied, g + 1)
                for a in range(PARTS):
                    sp.dma_start(q_stack[STACK + a:STACK + a + 1, b, h:h + HG, :],
                                 max_rows[a * HG:(a + 1) * HG, g % 2, :]).then_inc(max_stacked[g % 2], 16)

            max_in(0)
            sp.dma_start(sel_f[:, :, :], select0).then_inc(ld["sel"], 16)
            sp.dma_start(bu1_sb[:, :], bu1).then_inc(ld["bu1"], 16)
            max_in(1)
            sp.dma_start(wg0_sb[:, :], wg0).then_inc(ld["wg0"], 16)
            sp.dma_start(wu0_sb[:, :], wu0).then_inc(ld["wu0"], 16)
            max_in(2)
            sp.dma_start(wd0_sb[:, :, :], wd0.rearrange("(t p) d -> p t d", p=128)).then_inc(ld["wd0"], 16)
            sp.dma_start(wsd0_sb[:, :], wsd0).then_inc(ld["wd0"], 16)
            max_in(3)
            sp.dma_start(bd1_sb[:, :], bd1).then_inc(ld["wd1"], 16)
            for g in range(4, B * NG):
                max_in(g)
            sp.wait_ge(scores_ready, HEADS)
            for i in range(B, 2 * B):
                sp.wait_ge(k_written[i], 16 * PARTS)
                bounce_in(k_stack[0:STACK, i % B], k_bounce[i], k_stacked[i])
            q_out(2)
            q_in(2)
            sp.wait_ge(down0_done, 2 * (T0 // 2 + 1))
            sp.dma_start(wu1_sb[:, :, :], wu1).then_inc(ld["wu1"], 16)
            sp.dma_start(wd1_sb[:, :, :], wd1.rearrange("(t p) d -> p t d", p=128)).then_inc(ld["wd1"], 16)
            max_in(B * NG)
            q_out(3)
            max_in(B * NG + 1)
            q_in(3)
            for g in range(B * NG + 2, 2 * B * NG):
                max_in(g)
            for b in range(B):
                sp.wait_ge(stored_ready, b + 1)
                sp.dma_start(out[b].rearrange("(t p) d -> p t d", p=128), result[:, b]).then_inc(stored, 16)
            sp.wait_ge(stored, 16 * B)


def kernel(**inputs):
    import concourse.bacc as _bacc
    from concourse.bass_utils import run_bass_kernel_spmd as _run

    a = {k: np.asarray(v) for k, v in inputs.items()}

    def head_minor(w):
        return w.reshape(H, DK, *w.shape[1:]).swapaxes(0, 1).reshape(w.shape)

    def proj(l):
        q, k, v, o = (("L0_xattn_w_q", "L0_xattn_w_k", "L0_xattn_w_v", "L0_xattn_w_out"),
                      ("L1_xattn_Wq", "L1_xattn_Wk", "L1_xattn_Wv", "L1_xattn_Wo"))[l]
        return np.stack([head_minor(a[k]).T, head_minor(a[q]).T, a[v].T, a[o].T], axis=1)

    by_unit = [a[n].reshape(E1, 2, 128).transpose(2, 0, 1).reshape(128, 2 * E1) for n in ("L1_ffn_ln1_g", "L1_ffn_ln1_b")]
    cols = np.concatenate([np.stack([head_minor(a["L0_xattn_b_k"]), head_minor(a["L0_xattn_b_q"]),
                                     head_minor(a["L1_xattn_bk"]), head_minor(a["L1_xattn_bq"]),
                                     a["L1_xattn_ln_g"], a["L1_xattn_ln_b"]], axis=1)] + by_unit, axis=1)
    rows = np.stack([a[n] for n in ("L0_xattn_b_v", "L0_xattn_b_out", "L1_xattn_bv", "L1_xattn_bo",
                                    "L1_ffn_ln_g", "L1_ffn_ln_b")])[None]
    index = np.arange(E0)
    ties = (index[None, :] < index[:, None]).astype(np.float32)[None]
    expert_of_row = (np.arange(E0 * I0) // I0).reshape(T0, 128)
    select = np.tile((expert_of_row[None] == index[:, None, None]).astype(np.float32), (PARTS, 1, 1))
    arrays = {
        "x": a["x"],
        "ctxT": a["ctx_1024"].transpose(2, 0, 1),
        "mask": a["mask_SxS2_ik0"],
        "maskT": a["mask_SxS2_ik0"].T,
        "attn_w": np.stack([proj(0), proj(1)], axis=1),
        "cols": cols,
        "rows": rows,
        "gate_bias": a["L0_ffn_gate_bias"][None],
        "ties": ties,
        "ident": np.eye(128, dtype=np.float32),
        "gate0": a["L0_ffn_gate_w"].T,
        "gate1": a["L1_ffn_gate_w"],
        "wg0": np.concatenate([a["L0_ffn_w1"].reshape(E0 * I0, D), a["L0_ffn_ws1"]]).T,
        "wu0": np.concatenate([a["L0_ffn_w3"].reshape(E0 * I0, D), a["L0_ffn_ws3"]]).T,
        "wd0": a["L0_ffn_w2"].transpose(0, 2, 1).reshape(E0 * I0, D),
        "wsd0": a["L0_ffn_ws2"].T,
        "select0": select,
        "wu1": a["L1_ffn_w1"].transpose(1, 0, 2),
        "bu1": a["L1_ffn_b1"].reshape(128, E1 * H1 // 128),
        "wd1": a["L1_ffn_w2"].reshape(E1 * H1, D),
        "bd1": a["L1_ffn_b2"],
    }
    arrays = {f"in_{k}": np.ascontiguousarray(v) for k, v in arrays.items()}
    nc = _bacc.Bacc("TRN2", target_bir_lowering=False, num_devices=1)
    args = [nc.dram_tensor(k, v.shape, mybir.dt.from_np(v.dtype), kind="ExternalInput").ap() for k, v in arrays.items()]
    args.append(nc.dram_tensor("out_0", (B, S, D), F32, kind="ExternalOutput").ap())
    attention_ffn_kernel(nc, *args)
    r = _run(nc, [arrays], core_ids=[0])
    return r.results[0]["out_0"]
```

```python
from contextlib import ExitStack

import numpy as np

import concourse.bass as bass
from concourse import mybir

F32, BF16, I32 = mybir.dt.float32, mybir.dt.bfloat16, mybir.dt.int32
ALU = mybir.AluOpType
ACT = mybir.ActivationFunctionType
AX = mybir.AxisListType

B, S, S2, D = 2, 256, 512, 128
H, DK = 16, 8
QT, KT = S // 128, S2 // 128
PARTS = 3
STACK = PARTS * PARTS * DK
MAX_ROW = 96
ROWS_K = MAX_ROW + PARTS
MG = 2
E0, I0 = 16, 96
T0 = E0 * I0 // 128
E1, H1 = 8, 256
GROUPS0 = 4
HG = 4
NG = H // HG
VW = 32
SCALE = float(DK) ** -0.5
EPS = 1e-5
MASKED = -float(2.0 ** 100)
LOWEST = -3.0e38
LAG = 5
PV_LAG = LAG + HG
HEADS = B * H

ROW_NAMES = ["bv0", "bo0", "bv1", "bo1", "lnf_g", "lnf_b"]
COL_BK0, COL_BQ0, COL_BK1, COL_BQ1, COL_LNG, COL_LNB, COL_G1 = 0, 1, 2, 3, 4, 5, 6
COL_B1 = COL_G1 + 2 * E1
NCOLS = COL_B1 + 2 * E1


def attention_ffn_kernel(nc, x, ctxT, mask, maskT, attn_w, cols, rows, gate_bias, ties, ident,
                         gate0, gate1, wg0, wu0, wd0, wsd0, select0, wu1, bu1, wd1, bd1, out):
    ctx = ExitStack()
    with ctx:
        def sb(name, shape, dt=F32):
            return ctx.enter_context(nc.sbuf_tensor(name, shape, dt))

        def sem(name):
            return ctx.enter_context(nc.semaphore(name))

        k_bounce = [nc.dram_tensor(f"k_bounce{i}", [PARTS, 128, S2], BF16, kind="Internal").ap()
                    for i in range(4)]
        q_bounce = [nc.dram_tensor(f"q_bounce{i}", [PARTS, PARTS, 128, S], BF16, kind="Internal").ap()
                    for i in range(4)]

        x_sb = sb("x_sb", [128, B, QT, D])
        ctxT_sb = sb("ctxT_sb", [128, B, S2])
        probs = sb("probs", [128, 2 * HG, KT * S])
        mask_q = probs[:, 0, :].bitcast(I32).rearrange("p (t k) -> p t k", t=QT)
        mask_k = probs[:, 1, :].bitcast(I32).rearrange("p (t q) -> p t q", t=KT)
        experts_w = sb("experts_w", [128, 2 * (T0 * 128 + I0) + T0 * D])
        early = sb("early", [128, 4 * (2 * S2 + PARTS * S2 // 2)])
        shared_area = sb("shared_area", [128, T0 * 128])
        aw = sb("aw", [128, 2, 4, 128])
        W_K, W_Q, W_V, W_O = 0, 1, 2, 3
        col = sb("col", [128, NCOLS])
        row = sb("row", [128, len(ROW_NAMES), D])
        gbias = sb("gbias", [128, E0])
        tie = sb("tie", [128, E0, E0])
        idf = sb("idf", [128, 128])
        g0_sb = sb("g0_sb", [128, E0])
        g1_sb = sb("g1_sb", [128, E1])
        up_cols = E0 * I0 + I0
        wg0_sb = experts_w[:, 0:up_cols]
        wu0_sb = experts_w[:, up_cols:2 * up_cols]
        wd0_sb = experts_w[:, 2 * up_cols:2 * up_cols + T0 * D].rearrange("p (t d) -> p t d", t=T0)
        wsd0_sb = sb("wsd0_sb", [I0, D])
        sel_f = shared_area[0:PARTS * E0, :].rearrange("p (t r) -> p t r", t=T0)
        wu1_sb = experts_w[:, 0:E1 * H1].rearrange("p (e n) -> p e n", e=E1)
        bu1_sb = sb("bu1_sb", [128, E1 * H1 // 128])
        wd1_sb = experts_w[:, E1 * H1:2 * E1 * H1].rearrange("p (t d) -> p t d", t=2 * E1)
        bd1_sb = sb("bd1_sb", [E1, D])

        idb = sb("idb", [128, 128], BF16)
        sel = sb("sel", [PARTS * E0, T0, 128], BF16)
        bias_q = sb("bias_q", [128, QT, S2])
        bias_k = sb("bias_k", [128, KT, S], BF16)
        minus_half = sb("minus_half", [128, 4])
        ones_parts = sb("ones_parts", [PARTS, 128], BF16)
        minus_ones = sb("minus_ones", [PARTS, S2], BF16)
        zero_rows = sb("zero_rows", [MAX_ROW - STACK, S2], BF16)
        bu1_part = sb("bu1_part", [128, PARTS, E1 * H1 // 128], BF16)
        bu1_rest = sb("bu1_rest", [128, E1 * H1 // 128])
        bu1_rows = ctxT_sb[0:PARTS].rearrange("p b k -> p (b k)").bitcast(BF16)

        k_full = [early[:, i * S2:(i + 1) * S2] for i in range(4)]
        k_rest = [early[:, (4 + i) * S2:(5 + i) * S2] for i in range(4)]
        part_cols = PARTS * S2 // 2
        k_part = [early[:, 8 * S2 + i * part_cols:8 * S2 + (i + 1) * part_cols].bitcast(BF16)
                  .rearrange("p (a s) -> p a s", a=PARTS) for i in range(4)]

        q_rest = sb("q_rest", [128, S])
        q_part = [sb(f"q_part{b}", [128, PARTS, S], BF16) for b in range(B)]
        k_stack = sb("k_stack", [ROWS_K, B, H, S2], BF16)
        q_stack = sb("q_stack", [ROWS_K, B, H, S], BF16)
        v_ext = [sb(f"v_ext{l}", [128, B * KT, H * (DK + 1) + VW - DK - 1]) for l in range(2)]
        v_heads = [v[:, :, 0:H * (DK + 1)].rearrange("p t (h c) -> p t h c", h=H) for v in v_ext]
        row_max = sb("row_max", [128, 2, MG, QT])
        max_rest = sb("max_rest", [128, MG, QT])
        max_part = sb("max_part", [128, 2, MG, QT, PARTS], BF16)
        table = sb("table", [128, 4])
        discard = sb("discard", [128, QT, S2], BF16)
        o_sb = sb("o_sb", [128, 2, S])
        rden = sb("rden", [128, QT, HG])
        att = [[sb(f"att{b}", [128, QT, D]) for b in range(B)],
               [shared_area[:, b * S:(b + 1) * S].rearrange("p (t d) -> p t d", t=QT) for b in range(B)]]
        attT = [[sb(f"attT{b}", [128, S]) for b in range(B)],
                [shared_area[:, (2 + b) * S:(3 + b) * S] for b in range(B)]]

        res = [[x_sb[:, b] for b in range(B)]] + [
            [sb(f"res{s}{b}", [128, QT, D])[:] for b in range(B)] for s in range(1, 3)]
        res.append(res[1])
        res_bias = {s: [sb(f"res_bias{s}{b}", [128, QT, D]) for b in range(B)] for s in (0, 3)}
        res_bias[2] = res_bias[0]
        norm = {n: [sb(f"norm_{n}{b}", [128, QT, D]) for b in range(B)] for n in ("a0", "f0", "f1")}
        norm["a1n"], norm["a1"], norm["out"] = norm["a0"], norm["f0"], norm["f0"]
        mean_var = {(n, b): sb(f"mv_{n}{b}", [128, QT, 2]) for n in norm for b in range(B)}
        rstd = {(n, b): sb(f"rstd_{n}{b}", [128, QT]) for n in norm for b in range(B)}
        var_eps = sb("var_eps", [128, QT])
        stats = sb("stats", [128, QT, 6])
        xT = {n: [sb(f"xT_{n}{b}", [128, S]) for b in range(B)] for n in ("a0", "f0")}
        xT["a1n"], xT["f1"] = xT["a0"], xT["f0"]

        r_exp = sb("r_exp", [128, QT, E0])
        r_score = sb("r_score", [128, QT, E0])
        r_biased = sb("r_biased", [128, QT, E0])
        r_pair = sb("r_pair", [128, 4, QT, GROUPS0])
        r_top = sb("r_top", [128, 3, QT, GROUPS0])
        r_gsum = sb("r_gsum", [128, QT, GROUPS0])
        r_ge, r_gt = [bias_q[:, t, :].rearrange("p (t i j) -> p t i j", t=QT, i=E0) for t in range(QT)]
        r_rank = sb("r_rank", [128, QT, E0])
        r_keep = sb("r_keep", [128, QT, GROUPS0])
        r_drop = sb("r_drop", [128, QT, GROUPS0])
        r_small = sb("r_small", [128, 2, QT])
        combine = [[sb(f"combine{l}{b}", [128, QT, (E0, E1)[l]]) for b in range(B)] for l in range(2)]
        c_part = sb("c_part", [128, QT, PARTS, E0], BF16)
        c_rest = sb("c_rest", [128, QT, E0])
        c_rows = [sb(f"c_rows{b}", [PARTS * E0, S], BF16) for b in range(B)]
        cT1 = [sb(f"cT1{b}", [E1, S]) for b in range(B)]

        def late(at, size, pattern, **kw):
            return early[:, at:at + size].rearrange(pattern, **kw)

        silu_g, gated, hid0 = [late(i * 4 * S, 4 * S, "p (u j s) -> p u j s", u=2, j=2) for i in range(3)]
        c_sb = late(12 * S, 4 * S, "p (u j s) -> p u j s", u=2, j=2)
        hn1 = late(12 * S, 2 * QT * 2 * H1, "p (u t e n) -> p u t e n", u=2, t=QT, e=2)
        hid1 = late(12 * S + 2 * QT * 2 * H1, 8 * S, "p (u k s) -> p u k s", u=2, k=4)
        st1 = sb("st1", [128, 4, 6])
        mv1 = sb("mv1", [128, 2, 4, 2])
        ve1 = sb("ve1", [128, 4])
        rs1 = sb("rs1", [128, 2, 4])
        shift1 = sb("shift1", [128, 2, 4])
        acc = [shared_area[:, (4 + b) * S:(5 + b) * S].rearrange("p (t d) -> p t d", t=QT) for b in range(B)]
        result = x_sb

        bank = ctx.enter_context(nc.psum_tensor("bank", [128, 8, 512], F32))
        MISC, OUT = 7, 6

        ld = {n: sem(f"ld_{n}") for n in ("ctx0", "ctx1", "x", "aw0", "aw1", "col", "row", "ident", "mask",
                                          "router", "wg0", "wu0", "wd0", "sel", "wu1", "bu1", "wd1", "pad")}
        consts_ready = sem("consts_ready")
        half_ready = sem("half_ready")
        v_zeroed = [sem(f"v_zeroed{l}") for l in range(2)]
        ones_ready = sem("ones_ready")
        pad_ready = sem("pad_ready")

        mask_ready = sem("mask_ready")
        sel_ready = sem("sel_ready")
        bu1_split = sem("bu1_split")
        bu1_ready = sem("bu1_ready")
        k_proj = sem("k_proj")
        k_evacuated = sem("k_evacuated")
        k_rest_ready = [sem(f"k_rest_ready{i}") for i in range(4)]
        k_second = sem("k_second")
        k_parts = [sem(f"k_parts{i}") for i in range(4)]
        k_written = [sem(f"k_written{i}") for i in range(4)]
        k_stacked = [sem(f"k_stacked{i}") for i in range(4)]
        first_stacked = sem("first_stacked")
        q_parts = [sem(f"q_parts{i}") for i in range(4)]
        q_written = [sem(f"q_written{i}") for i in range(4)]
        q_stacked = [sem(f"q_stacked{i}") for i in range(4)]
        v_proj = sem("v_proj")
        v_ready = sem("v_ready")
        misc_ready = sem("misc_ready")
        misc_free = sem("misc_free")
        for_max = sem("for_max")
        max_done = sem("max_done")
        max_parts = sem("max_parts")
        max_copied = sem("max_copied")
        scores_ready = sem("scores_ready")
        exp_done = sem("exp_done")
        pv_done = sem("pv_done")
        o_copied = sem("o_copied")
        att_done = sem("att_done")
        attT_done = sem("attT_done")
        var_ready = {n: sem(f"var_{n}") for n in norm}
        rstd_ready = {n: sem(f"rstd_{n}") for n in norm}
        normed = {n: sem(f"normed_{n}") for n in norm if n not in ("a1", "out")}
        xT_ready = {n: sem(f"xT_ready_{n}") for n in xT}
        res_ready = {s: sem(f"res_ready{s}") for s in (2, 3)}
        res_bias_ready = {s: sem(f"res_bias_ready{s}") for s in (0, 2, 3)}
        gate_in = sem("gate_in")
        gate_exp = [sem(f"gate_exp{l}") for l in range(2)]
        combined = [sem(f"combined{l}") for l in range(2)]
        c_ready = [sem(f"c_ready{l}") for l in range(2)]
        gu_ready = sem("gu_ready")
        silu_done = sem("silu_done")
        c_spread = sem("c_spread")
        hid0_ready = sem("hid0_ready")
        down0_done = sem("down0_done")
        up1_ready = sem("up1_ready")
        var1_ready = sem("var1_ready")
        rstd1_ready = sem("rstd1_ready")
        norm1_done = [sem(f"norm1_done{t}") for t in range(QT)]
        tr1_ready = sem("tr1_ready")
        gelu_done = sem("gelu_done")
        down1_done = sem("down1_done")
        acc_done = sem("acc_done")
        stored_ready = sem("stored_ready")
        stored = sem("stored")
        dve_step = sem("dve_step")
        pool_step = sem("pool_step")

        block = ctx.enter_context(nc.Block())
        use = {}

        @block.tensor
        def _(pe):
            mm = pe.matmul

            def misc(name):
                if use:
                    pe.wait_ge(misc_free, len(use))
                use[name] = len(use) + 1

            def k_projection(i):
                l, b = divmod(i, B)
                pe.wait_ge(ld[f"ctx{b}"], 16)
                pe.wait_ge(ld[f"aw{l}"], 16)
                mm(bank[:, i, :], aw[:, l, W_K, :], ctxT_sb[:, b, :], start=True, stop=True).then_inc(k_proj, 1)

            def v_projection(i, at):
                l, b = divmod(i, B)
                pe.wait_ge(ld[f"ctx{b}"], 16)
                pe.wait_ge(ld[f"aw{l}"], 16)
                for t in range(KT):
                    last = mm(bank[:, at, t * D:(t + 1) * D], ctxT_sb[:, b, t * 128:(t + 1) * 128],
                              aw[:, l, W_V, :], start=True, stop=True)
                last.then_inc(v_proj, 1)

            def transpose_tokens(n, b):
                pe.wait_ge(normed[n], QT * (b + 1))
                misc(f"xT_{n}{b}")
                for t in range(QT):
                    last = pe.transpose(bank[:, MISC, t * 128:(t + 1) * 128], norm[n][b][:, t, :], idf[:, :])
                last.then_inc(misc_ready, 1)

            def q_projection(l, b):
                n = ("a0", "a1n")[l]
                pe.wait_ge(xT_ready[n], b + 1)
                misc(f"q{l}{b}")
                mm(bank[:, MISC, 0:S], aw[:, l, W_Q, :], xT[n][b][:, :], start=True, stop=True).then_inc(misc_ready, 1)

            def score_rows(n, qt):
                l, b, h = n // HEADS, n % HEADS // H, n % H
                if n == 0 and qt == 0:
                    pe.wait_ge(first_stacked, 16 * (PARTS + 1))
                    pe.wait_ge(k_evacuated, 2)
                if h == (HG if n < H else 0) and qt == 0:
                    pe.wait_ge(k_stacked[l * B + b], 16 * PARTS)
                    pe.wait_ge(q_stacked[l * B + b], 16)
                if n >= 1:
                    pe.wait_ge(max_done, 2 * (n - 1) + qt + 1)
                mm(bank[:, qt, :], q_stack[0:STACK, b, h, qt * 128:(qt + 1) * 128],
                   k_stack[0:STACK, b, h, :], start=True, stop=True).then_inc(for_max, 1)

            def max_transpose(g):
                pe.wait_ge(max_parts, g + 1)
                if g == 0:
                    pe.wait_ge(consts_ready, 1)
                misc(f"max{g}")
                o = bank[MAX_ROW:ROWS_K, MISC, 0:MG * S // 2].bitcast(BF16)
                for j in range(MG):
                    for t in range(QT):
                        at = j * S + t * 128
                        last = pe.transpose(o[:, at:at + 128], max_part[:, g % 2, j, t, :], idb[:, :])
                last.then_inc(misc_ready, 1)

            def score_cols(n, kts):
                l, b, h = n // HEADS, n % HEADS // H, n % H
                if kts[0] == 0:
                    if n % MG == 0:
                        pe.wait_ge(max_copied, n // MG + 1)
                    if n == 0:
                        pe.wait_ge(ld["pad"], 16 * 3)
                        pe.wait_ge(k_evacuated, 4)
                        pe.wait_ge(mask_ready, 2)
                        pe.wait_ge(v_ready, 2)
                    if n == 1:
                        pe.wait_ge(v_ready, 3)
                    if n == HEADS:
                        pe.wait_ge(hid0_ready, B * (T0 // 2 + 1))
                    if n >= 2:
                        pe.wait_ge(exp_done, n - 1)
                at = 2 + 2 * (n % 2)
                for kt in kts:
                    o = bank[:, at + kt // 2, kt % 2 * S:(kt % 2 + 1) * S]
                    last = mm(o, k_stack[:, b, h, kt * 128:(kt + 1) * 128], q_stack[:, b, h, :],
                              start=True, stop=(l == 1))
                    if l == 0:
                        last = mm(o, idb[:, :], bias_k[:, kt, :], start=False, stop=True)
                if kts[-1] == KT - 1:
                    last.then_inc(scores_ready, 1)

            def values(g, kt):
                l, b = g // (B * NG), g % (B * NG) // NG
                if kt == 0:
                    pe.wait_ge(exp_done, HG * (g + 1))
                    pe.wait_ge(v_ready, 2 * B)
                    if g >= 1:
                        pe.wait_ge(o_copied, g)
                    if g == B * NG:
                        pe.wait_ge(res_ready[2], QT * B)
                for j in range(HG):
                    h = g % NG * HG + j
                    last = mm(bank[VW * j:VW * (j + 1), OUT, 0:S], v_ext[l][:, b * KT + kt, h * (DK + 1):h * (DK + 1) + VW],
                              probs[:, (g * HG + j) % (2 * HG), kt * S:(kt + 1) * S],
                              start=(kt == 0), stop=(kt == KT - 1))
                if kt == KT - 1:
                    last.then_inc(pv_done, 1)

            def o_transpose(g):
                pe.wait_ge(o_copied, g + 1)
                misc(f"o{g}")
                for t in range(QT):
                    last = pe.transpose(bank[:, MISC, t * 128:(t + 1) * 128], o_sb[:, g % 2, t * 128:(t + 1) * 128], idf[:, :])
                last.then_inc(misc_ready, 1)

            def att_transpose(l, b):
                pe.wait_ge(att_done, NG * (l * B + b + 1))
                misc(f"attT{l}{b}")
                for t in range(QT):
                    last = pe.transpose(bank[:, MISC, t * 128:(t + 1) * 128], att[l][b][:, t, :], idf[:, :])
                last.then_inc(misc_ready, 1)

            def out_projection(l, b):
                pe.wait_ge(attT_done, l * B + b + 1)
                misc(f"out{l}{b}")
                for t in range(QT):
                    last = mm(bank[:, MISC, t * D:(t + 1) * D], attT[l][b][:, t * 128:(t + 1) * 128], aw[:, l, W_O, :],
                              start=True, stop=True)
                last.then_inc(misc_ready, 1)

            def gate_logits(l, b):
                n, e, w = (("f0", E0, g0_sb), ("f1", E1, g1_sb))[l]
                pe.wait_ge(xT_ready[n], b + 1)
                pe.wait_ge(ld["router"], 16 * 4)
                misc(f"gate{l}{b}")
                for t in range(QT):
                    last = mm(bank[:, MISC, t * e:(t + 1) * e], xT[n][b][:, t * 128:(t + 1) * 128], w[:, :],
                              start=True, stop=True)
                last.then_inc(misc_ready, 1)

            def combine_transpose(l, b):
                pe.wait_ge(combined[l], b + 1)
                misc(f"c{l}{b}")
                for t in range(QT):
                    if l == 0:
                        o = bank[0:PARTS * E0, MISC, 0:128].bitcast(BF16)
                        last = pe.transpose(o[:, t * 128:(t + 1) * 128], c_part[:, t].rearrange("p a e -> p (a e)"), idb[:, :])
                    else:
                        last = pe.transpose(bank[0:E1, MISC, t * 128:(t + 1) * 128], combine[1][b][:, t, :], idf[:, :])
                last.then_inc(misc_ready, 1)

            def bias_down1(b):
                pe.wait_ge(c_ready[1], b + 1)
                misc(f"b2{b}")
                for t in range(QT):
                    last = mm(bank[:, MISC, t * D:(t + 1) * D], cT1[b][:, t * 128:(t + 1) * 128], bd1_sb[:, :],
                              start=True, stop=True)
                last.then_inc(misc_ready, 1)

            def up0(b, i):
                u = b * (T0 // 2 + 1) + i
                at = 2 + 2 * (u % 2)
                if i == 0 and b == 0:
                    pe.wait_ge(exp_done, HEADS)
                    pe.wait_ge(ld["wg0"], 16)
                    pe.wait_ge(ld["wu0"], 16)
                if i == 0:
                    pe.wait_ge(sel_ready, 1)
                    pe.wait_ge(c_ready[0], b + 1)
                shared = i == T0 // 2
                m = I0 if shared else 128
                if not shared:
                    misc(f"spread{u}")
                    for j in range(2):
                        last = mm(bank[:, MISC, j * S:(j + 1) * S], sel[:, 2 * i + j, :], c_rows[b][:, :], start=True, stop=True)
                    last.then_inc(misc_ready, 1)
                if u >= 2:
                    pe.wait_ge(hid0_ready, u - 1)
                for j in range(1 if shared else 2):
                    t = 2 * i + j
                    mm(bank[0:m, at + j, 0:S], wg0_sb[:, t * 128:t * 128 + m], xT["f0"][b][:, :], start=True, stop=True)
                    last = mm(bank[0:m, at + j, S:2 * S], wu0_sb[:, t * 128:t * 128 + m], xT["f0"][b][:, :], start=True, stop=True)
                last.then_inc(gu_ready, 1)

            def down0(b, i):
                u = b * (T0 // 2 + 1) + i
                shared = i == T0 // 2
                pe.wait_ge(hid0_ready, u + 1)
                if u == 0:
                    pe.wait_ge(o_copied, B * NG)
                    pe.wait_ge(ld["wd0"], 32)
                if b == 1 and i == 0:
                    pe.wait_ge(res_ready[2], QT)
                m = I0 if shared else 128
                for j in range(1 if shared else 2):
                    w = wsd0_sb[:, :] if shared else wd0_sb[:, 2 * i + j, :]
                    for t in range(QT):
                        last = mm(bank[:, OUT, t * D:(t + 1) * D], hid0[0:m, u % 2, j, t * 128:(t + 1) * 128], w,
                                  start=(i == 0 and j == 0 and t == 0), stop=shared, skip_group_check=True)
                last.then_inc(down0_done, 1)

            def up1(b, i):
                w = b * (E1 // 2) + i
                if w == 0:
                    pe.wait_ge(max_done, 4 * HEADS)
                    pe.wait_ge(exp_done, 2 * HEADS)
                    pe.wait_ge(ld["wu1"], 16)
                    pe.wait_ge(bu1_ready, 16 * PARTS)
                    pe.wait_ge(ones_ready, 1)
                if w >= 2:
                    for t in range(QT):
                        pe.wait_ge(norm1_done[t], 2 * (w - 1))
                for t in range(QT):
                    o = bank[:, 2 * (w % 2) + t, :]
                    mm(o, xT["f1"][b][:, t * 128:(t + 1) * 128],
                       wu1_sb[:, 2 * i:2 * i + 2, :].rearrange("p e n -> p (e n)"), start=True, stop=False)
                    last = mm(o, ones_parts[:, 0:128], bu1_rows[:, 2 * i * H1:(2 * i + 2) * H1], start=False, stop=True)
                last.then_inc(up1_ready, 1)

            def transpose1(b, i):
                w = b * (E1 // 2) + i
                for t in range(QT):
                    pe.wait_ge(norm1_done[t], 2 * (w + 1))
                if w >= 1:
                    pe.wait_ge(gelu_done, 4 * w)
                for e in range(2):
                    for half in range(2):
                        for t in range(QT):
                            at = half * S + t * 128
                            last = pe.transpose(bank[:, 4 + e, at:at + 128],
                                                hn1[:, w % 2, t, e, half * 128:(half + 1) * 128], idf[:, :])
                        last.then_inc(tr1_ready, 1)

            def down1(b, i):
                w = b * (E1 // 2) + i
                pe.wait_ge(gelu_done, 4 * (w + 1))
                if w == 0:
                    pe.wait_ge(o_copied, 2 * B * NG)
                    pe.wait_ge(ld["wd1"], 32)
                if w >= 1:
                    pe.wait_ge(acc_done, 4 * w)
                for e in range(2):
                    for t in range(QT):
                        for half in range(2):
                            last = mm(bank[:, OUT, (e * QT + t) * D:(e * QT + t + 1) * D],
                                      hid1[:, w % 2, 2 * e + half, t * 128:(t + 1) * 128],
                                      wd1_sb[:, 2 * (2 * i + e) + half, :], start=(half == 0), stop=(half == 1))
                last.then_inc(down1_done, 1)

            def attention(l, extra):
                for s in range(HEADS + PV_LAG):
                    n, m = l * HEADS + s, l * HEADS + s - LAG
                    if s < HEADS:
                        score_rows(n, 0)
                    if 0 <= s - LAG < HEADS:
                        score_cols(m, range(0, KT // 2))
                    if s < HEADS:
                        score_rows(n, 1)
                    if s % MG == 1 and 0 <= (s - 3) // MG < HEADS // MG:
                        max_transpose(l * HEADS // MG + (s - 3) // MG)
                    if 0 <= s - LAG < HEADS:
                        score_cols(m, range(KT // 2, KT))
                    if s % HG == (PV_LAG + 1) % HG and s >= PV_LAG + HG:
                        o_transpose(l * B * NG + (s - PV_LAG) // HG - 1)
                    if s >= PV_LAG:
                        values(l * B * NG + (s - PV_LAG) // HG, (s - PV_LAG) % HG)
                    for f in extra.get(s, []):
                        f()

            k_projection(0)
            pe.wait_ge(ld["ident"], 16)
            transpose_tokens("a0", 0)
            q_projection(0, 0)
            k_projection(1)
            transpose_tokens("a0", 1)
            v_projection(0, 4)
            q_projection(0, 1)
            v_projection(1, 5)
            v_projection(2, OUT)
            k_projection(2)
            k_projection(3)
            pe.wait_ge(k_evacuated, 4)
            v_projection(3, 3)

            attention(0, {
                27: [lambda: att_transpose(0, 0)],
                28: [lambda: out_projection(0, 0)],
                31: [lambda: transpose_tokens("f0", 0)],
                32: [lambda: gate_logits(0, 0)],
                40: [lambda: combine_transpose(0, 0)],
            })

            def experts0(b, extra):
                for i in range(T0 // 2 + 1):
                    up0(b, i)
                    for f in extra.get(i, []):
                        f()
                    if i >= 1:
                        down0(b, i - 1)
                    for f in extra.get(i + 0.5, []):
                        f()
                down0(b, T0 // 2)

            experts0(0, {
                0: [lambda: o_transpose(B * NG - 1)],
                1: [lambda: att_transpose(0, 1)],
                1.5: [lambda: out_projection(0, 1)],
                2.5: [lambda: transpose_tokens("f0", 1)],
                3: [lambda: gate_logits(0, 1)],
                6.5: [lambda: combine_transpose(0, 1)],
            })
            experts0(1, {
                2: [lambda: transpose_tokens("a1n", 0)],
                3: [lambda: q_projection(1, 0)],
            })
            attention(1, {
                2: [lambda: transpose_tokens("a1n", 1)],
                4: [lambda: q_projection(1, 1)],
                27: [lambda: att_transpose(1, 0)],
                28: [lambda: out_projection(1, 0)],
                31: [lambda: transpose_tokens("f1", 0)],
                32: [lambda: gate_logits(1, 0)],
                36: [lambda: combine_transpose(1, 0)],
                38: [lambda: bias_down1(0)],
            })

            steps = [(b, i) for b in range(B) for i in range(E1 // 2)]
            tail = {0: [lambda: o_transpose(2 * B * NG - 1)],
                    1: [lambda: att_transpose(1, 1)],
                    1.3: [lambda: out_projection(1, 1)],
                    2.3: [lambda: transpose_tokens("f1", 1)],
                    2.6: [lambda: gate_logits(1, 1)],
                    5.3: [lambda: combine_transpose(1, 1)],
                    5.6: [lambda: bias_down1(1)]}
            for k in range(len(steps) + 2):
                if k < len(steps):
                    up1(*steps[k])
                for f in tail.get(k, []):
                    f()
                if 1 <= k <= len(steps):
                    transpose1(*steps[k - 1])
                for f in tail.get(k + 0.3, []):
                    f()
                if k >= 2:
                    down1(*steps[k - 2])
                for f in tail.get(k + 0.6, []):
                    f()

        @block.vector
        def _(dve):
            steps = [0]

            def then(ins):
                steps[0] += 1
                ins.then_inc(dve_step, 1)
                dve.wait_ge(dve_step, steps[0])

            def noted(ins):
                steps[0] += 1
                ins.then_inc(dve_step, 1)

            tt, ts, copy = dve.tensor_tensor, dve.tensor_scalar, dve.tensor_copy

            def norm_stats(n, b, src):
                for t in range(QT):
                    (then if t == QT - 1 else noted)(dve.bn_stats(stats[:, t, :], src[:, t, :]))
                for t in range(QT):
                    dve.bn_aggr(mean_var[n, b][:, t, :], stats[:, t, :]).then_inc(var_ready[n], 1)

            def normalise(n, b, src):
                dve.wait_ge(rstd_ready[n], b + 1)
                for t in range(QT):
                    ins = ts(norm[n][b][:, t, :], src[:, t, :], mean_var[n, b][:, t, 0:1], rstd[n, b][:, t:t + 1],
                             ALU.subtract, ALU.mult)
                    if n in normed:
                        ins.then_inc(normed[n], 1)
                    else:
                        (then if t == QT - 1 else noted)(ins)

            def xT_copy(n, b):
                dve.wait_ge(misc_ready, use[f"xT_{n}{b}"])
                if n == "a1n":
                    then(ts(xT[n][b][:, :], bank[:, MISC, 0:S], col[:, COL_LNG:COL_LNG + 1],
                            col[:, COL_LNB:COL_LNB + 1], ALU.mult, ALU.add))
                else:
                    then(copy(xT[n][b][:, :], bank[:, MISC, 0:S]))
                dve.sem_inc(xT_ready[n], 1)
                dve.sem_inc(misc_free, 1)

            def q_split(l, b):
                i = l * B + b
                c = (COL_BQ0, COL_BQ1)[l]
                if l == 1:
                    dve.wait_ge(q_written[b], 16 * PARTS)
                dve.wait_ge(misc_ready, use[f"q{l}{b}"])
                then(ts(q_part[b][:, 0, :], bank[:, MISC, 0:S], col[:, c:c + 1], None, ALU.add))
                then(dve.scalar_tensor_tensor(out=q_rest[:, :], in0=bank[:, MISC, 0:S], scalar=col[:, c:c + 1],
                                              in1=q_part[b][:, 0, :], op0=ALU.add, op1=ALU.subtract))
                dve.sem_inc(misc_free, 1)
                then(copy(q_part[b][:, 1, :], q_rest[:, :]))
                tt(q_part[b][:, 2, :], q_rest[:, :], q_part[b][:, 1, :], ALU.subtract).then_inc(q_parts[i], 1)

            def v_copy(i, at):
                l, b = divmod(i, B)
                dve.wait_ge(v_proj, i + 1)
                dve.wait_ge(v_zeroed[l], 2)
                dve.wait_ge(ld["row"], 16)
                if i == 3:
                    dve.wait_ge(k_evacuated, 4)
                src = bank[:, at, :].rearrange("p (t h d) -> p t h d", t=KT, h=H)
                bias = row[:, ROW_NAMES.index(f"bv{l}"), :].rearrange("p (h d) -> p h d", h=H)
                for t in range(KT):
                    ins = tt(v_heads[l][:, b * KT + t, :, 0:DK], src[:, t], bias, ALU.add)
                    (then if t == KT - 1 else noted)(ins)
                dve.sem_inc(v_ready, 1)

            def head_max(n, qt):
                dve.wait_ge(for_max, 2 * n + qt + 1)
                g = n // MG
                if g >= 2 and n % MG == 0 and qt == 0:
                    dve.wait_ge(max_parts, g - 1)
                o = row_max[:, g % 2, n % MG, qt:qt + 1]
                if 2 * n + qt >= 2:
                    dve.wait_ge(max_done, 2 * n + qt - 1)
                if n < HEADS:
                    ins = dve.tensor_tensor_reduce(discard[:, qt, :], bank[:, qt, :], bias_q[:, qt, :], 1.0, LOWEST,
                                                   ALU.add, ALU.max, o)
                else:
                    ins = dve.tensor_reduce(o, bank[:, qt, :], AX.X, ALU.max)
                ins.then_inc(max_done, 1)



            def divide(g):
                l, b = g // (B * NG), g % (B * NG) // NG
                dve.wait_ge(misc_ready, use[f"o{g}"])
                src = bank[:, MISC, 0:S].rearrange("p (t j v) -> p t j v", t=QT, j=HG)
                then(dve.reciprocal(rden[:, :, :], src[:, :, :, DK]))
                o = att[l][b][:, :, g % NG * HG * DK:(g % NG + 1) * HG * DK].rearrange("p t (j d) -> p t j d", j=HG)
                then(tt(o, src[:, :, :, 0:DK], rden[:, :, :].unsqueeze(3).to_broadcast([128, QT, HG, DK]), ALU.mult))
                dve.sem_inc(att_done, 1)
                dve.sem_inc(misc_free, 1)

            def attT_copy(l, b):
                dve.wait_ge(misc_ready, use[f"attT{l}{b}"])
                then(copy(attT[l][b][:, :], bank[:, MISC, 0:S]))
                dve.sem_inc(attT_done, 1)
                dve.sem_inc(misc_free, 1)

            def add_attention(l, b):
                s = 2 * l
                dve.wait_ge(misc_ready, use[f"out{l}{b}"])
                dve.wait_ge(res_bias_ready[s], b + 1)
                r = res[s + 1][b]
                then(tt(r, bank[:, MISC, 0:S].rearrange("p (t d) -> p t d", t=QT), res_bias[s][b][:, :, :], ALU.add))
                dve.sem_inc(misc_free, 1)
                if s + 1 == 3:
                    dve.sem_inc(res_ready[3], 1)
                norm_stats(("f0", "f1")[l], b, r)

            def ranks(values, e, beats_ge, beats_gt):
                mine = values.unsqueeze(3).to_broadcast([128, QT, e, e])
                other = values.unsqueeze(2).to_broadcast([128, QT, e, e])
                ge, gt = beats_ge[:, :, 0:e, 0:e], beats_gt[:, :, 0:e, 0:e]
                noted(tt(ge, other, mine, ALU.is_ge))
                then(tt(gt, other, mine, ALU.is_gt))
                for t in range(QT):
                    ins = tt(ge[:, t], ge[:, t], tie[:, 0:e, 0:e], ALU.mult)
                    (then if t == QT - 1 else noted)(ins)
                for t in range(QT):
                    ins = tt(gt[:, t], gt[:, t], ge[:, t], ALU.max)
                    (then if t == QT - 1 else noted)(ins)
                then(dve.tensor_reduce(r_rank[:, :, 0:e], gt, AX.X, ALU.add))

            def route0(b, part):
                v = r_biased[:, :, :].rearrange("p t (g k) -> p t g k", g=GROUPS0)
                c = combine[0][b]
                if part == 0:
                    dve.wait_ge(gate_exp[0], b + 1)
                    dve.wait_ge(ld["router"], 16 * 4)
                    then(ts(r_exp[:, :, :], r_exp[:, :, :], 1.0, None, ALU.add))
                    then(dve.reciprocal(r_score[:, :, :], r_exp[:, :, :]))
                    for t in range(QT):
                        ins = tt(r_biased[:, t, :], r_score[:, t, :], gbias[:, :], ALU.add)
                        (then if t == QT - 1 else noted)(ins)
                    for i, (op, lo) in enumerate(((ALU.max, 0), (ALU.min, 0), (ALU.max, 2), (ALU.min, 2))):
                        ins = tt(r_pair[:, i], v[:, :, :, lo], v[:, :, :, lo + 1], op)
                        (then if i == 3 else noted)(ins)
                    noted(tt(r_top[:, 0], r_pair[:, 0], r_pair[:, 2], ALU.max))
                    noted(tt(r_top[:, 1], r_pair[:, 0], r_pair[:, 2], ALU.min))
                    then(tt(r_top[:, 2], r_pair[:, 1], r_pair[:, 3], ALU.max))
                    then(tt(r_top[:, 1], r_top[:, 1], r_top[:, 2], ALU.max))
                    then(tt(r_gsum[:, :, :], r_top[:, 0], r_top[:, 1], ALU.add))
                elif part == 1:
                    ranks(r_gsum[:, :, :], GROUPS0, r_ge, r_gt)
                    noted(ts(r_keep[:, :, :], r_rank[:, :, 0:GROUPS0], 2.0, None, ALU.is_lt))
                    then(ts(r_drop[:, :, :], r_rank[:, :, 0:GROUPS0], 2.0, LOWEST, ALU.is_ge, ALU.mult))
                    for t in range(QT):
                        keep = r_keep[:, t, :].unsqueeze(2).to_broadcast([128, GROUPS0, E0 // GROUPS0])
                        ins = tt(v[:, t], v[:, t], keep, ALU.mult)
                        (then if t == QT - 1 else noted)(ins)
                    for t in range(QT):
                        drop = r_drop[:, t, :].unsqueeze(2).to_broadcast([128, GROUPS0, E0 // GROUPS0])
                        ins = tt(v[:, t], v[:, t], drop, ALU.add)
                        (then if t == QT - 1 else noted)(ins)
                elif part == 2:
                    ranks(r_biased[:, :, :], E0, r_ge, r_gt)
                else:
                    then(dve.scalar_tensor_tensor(out=c[:, :, :], in0=r_rank[:, :, :], scalar=4.0, in1=r_score[:, :, :],
                                                  op0=ALU.is_lt, op1=ALU.mult))
                    then(dve.tensor_reduce(r_small[:, 0, :], c[:, :, :], AX.X, ALU.add))
                    then(ts(r_small[:, 0, :], r_small[:, 0, :], 1e-20, None, ALU.add))
                    then(dve.reciprocal(r_small[:, 1, :], r_small[:, 0, :]))
                    for t in range(QT):
                        ins = ts(c[:, t, :], c[:, t, :], r_small[:, 1, t:t + 1], 2.5, ALU.mult, ALU.mult)
                        (then if t == QT - 1 else noted)(ins)
                    then(copy(c_part[:, :, 0, :], c[:, :, :]))
                    then(tt(c_rest[:, :, :], c[:, :, :], c_part[:, :, 0, :], ALU.subtract))
                    then(copy(c_part[:, :, 1, :], c_rest[:, :, :]))
                    tt(c_part[:, :, 2, :], c_rest[:, :, :], c_part[:, :, 1, :], ALU.subtract).then_inc(combined[0], 1)

            def c_copy(l, b):
                dve.wait_ge(misc_ready, use[f"c{l}{b}"])
                if l == 0:
                    then(copy(c_rows[b][:, :], bank[0:PARTS * E0, MISC, 0:128].bitcast(BF16)))
                else:
                    then(copy(cT1[b][:, :], bank[0:E1, MISC, 0:S]))
                dve.sem_inc(c_ready[l], 1)
                dve.sem_inc(misc_free, 1)

            def gate_shift1(b):
                dve.wait_ge(misc_ready, use[f"gate1{b}"])
                src = bank[:, MISC, 0:QT * E1].rearrange("p (t e) -> p t e", t=QT)
                then(dve.tensor_reduce(r_small[:, 0, :], src, AX.X, ALU.max))
                then(tt(r_score[:, :, 0:E1], src, r_small[:, 0, :].unsqueeze(2).to_broadcast([128, QT, E1]), ALU.subtract))
                dve.sem_inc(misc_free, 1)
                dve.sem_inc(gate_in, 1)

            def route1(b):
                dve.wait_ge(gate_exp[1], b + 1)
                e = r_exp[:, :, 0:E1]
                then(dve.tensor_reduce(r_small[:, 0, :], e, AX.X, ALU.add))
                then(dve.reciprocal(r_small[:, 1, :], r_small[:, 0, :]))
                then(tt(r_score[:, :, 0:E1], e, r_small[:, 1, :].unsqueeze(2).to_broadcast([128, QT, E1]), ALU.mult))
                ranks(r_score[:, :, 0:E1], E1, r_ge, r_gt)
                c = combine[1][b]
                then(dve.scalar_tensor_tensor(out=c[:, :, :], in0=r_rank[:, :, 0:E1], scalar=2.0, in1=r_score[:, :, 0:E1],
                                              op0=ALU.is_lt, op1=ALU.mult))
                then(dve.tensor_reduce(r_small[:, 0, :], c[:, :, :], AX.X, ALU.add))
                then(dve.reciprocal(r_small[:, 1, :], r_small[:, 0, :]))
                tt(c[:, :, :], c[:, :, :], r_small[:, 1, :].unsqueeze(2).to_broadcast([128, QT, E1]), ALU.mult)\
                    .then_inc(combined[1], 1)

            def hidden0(b, i):
                u = b * (T0 // 2 + 1) + i
                at = 2 + 2 * (u % 2)
                dve.wait_ge(silu_done, u + 1)
                if u >= 2:
                    dve.wait_ge(down0_done, u - 1)
                if i == T0 // 2:
                    tt(hid0[0:I0, u % 2, 0, :], silu_g[0:I0, u % 2, 0, :], bank[0:I0, at, S:2 * S], ALU.mult)\
                        .then_inc(hid0_ready, 1)
                    return
                then(tt(gated[:, u % 2], silu_g[:, u % 2], bank[:, at:at + 2, S:2 * S], ALU.mult))
                dve.wait_ge(c_spread, b * (T0 // 2) + i + 1)
                tt(hid0[:, u % 2], gated[:, u % 2], c_sb[:, u % 2], ALU.mult).then_inc(hid0_ready, 1)

            def add_experts0(b):
                dve.wait_ge(down0_done, (b + 1) * (T0 // 2 + 1))
                for t in range(QT):
                    ins = tt(res[2][b][:, t, :], bank[:, OUT, t * D:(t + 1) * D], res[1][b][:, t, :], ALU.add)
                    ins.then_inc(res_ready[2], 1)
                dve.wait_ge(res_ready[2], QT * (b + 1))
                norm_stats("a1", b, res[2][b])

            def norm_twice(b):
                normalise("a1", b, res[2][b])
                norm_stats("a1n", b, norm["a1"][b])
                normalise("a1n", b, norm["a1"][b])

            def stats1(b, i):
                w = b * (E1 // 2) + i
                dve.wait_ge(up1_ready, w + 1)
                if w >= 2:
                    dve.wait_ge(rstd1_ready, w - 1)
                    dve.wait_ge(norm1_done[1], 2 * (w - 1))
                for t in range(QT):
                    for e in range(2):
                        k = 2 * t + e
                        ins = dve.bn_stats(st1[:, k, :], bank[:, 2 * (w % 2) + t, e * H1:(e + 1) * H1])
                        (then if k == 3 else noted)(ins)
                for k in range(4):
                    dve.bn_aggr(mv1[:, w % 2, k, :], st1[:, k, :]).then_inc(var1_ready, 1)

            def normalise1(b, i):
                w = b * (E1 // 2) + i
                dve.wait_ge(rstd1_ready, w + 1)
                if w >= 2:
                    dve.wait_ge(tr1_ready, 4 * (w - 1))
                for e in range(2):
                    ts(hn1[:, w % 2, 0, e, :], bank[:, 2 * (w % 2), e * H1:(e + 1) * H1],
                       mv1[:, w % 2, e, 0:1], rs1[:, w % 2, e:e + 1], ALU.subtract, ALU.mult).then_inc(norm1_done[0], 1)

            def start_acc(b):
                dve.wait_ge(misc_ready, use[f"b2{b}"])
                then(tt(acc[b][:, :, :], bank[:, MISC, 0:S].rearrange("p (t d) -> p t d", t=QT), norm["f1"][b][:, :, :], ALU.add))
                dve.sem_inc(misc_free, 1)

            def accumulate1(b, i):
                w = b * (E1 // 2) + i
                dve.wait_ge(down1_done, w + 1)
                for e in range(2):
                    if e == 1:
                        dve.wait_ge(acc_done, 4 * w + QT)
                    elif i >= 1:
                        dve.wait_ge(acc_done, 4 * w)
                    for t in range(QT):
                        at = (e * QT + t) * D
                        dve.scalar_tensor_tensor(out=acc[b][:, t, :], in0=bank[:, OUT, at:at + D],
                                                 scalar=combine[1][b][:, t, 2 * i + e:2 * i + e + 1], in1=acc[b][:, t, :],
                                                 op0=ALU.mult, op1=ALU.add).then_inc(acc_done, 1)

            def last_stats(b):
                dve.wait_ge(acc_done, 4 * (E1 // 2) * (b + 1))
                norm_stats("out", b, acc[b])

            def finish(b):
                normalise("out", b, acc[b])
                g = row[:, ROW_NAMES.index("lnf_g"), :].unsqueeze(1).to_broadcast([128, QT, D])
                then(tt(norm["out"][b][:, :, :], norm["out"][b][:, :, :], g, ALU.mult))
                dve.wait_ge(res_bias_ready[3], b + 1)
                tt(result[:, b], norm["out"][b][:, :, :], res_bias[3][b][:, :, :], ALU.add).then_inc(stored_ready, 1)

            def attention(l, extra):
                for s in range(HEADS + PV_LAG):
                    n = l * HEADS + s
                    if s % HG == (PV_LAG + 2) % HG and s > PV_LAG + HG:
                        divide(l * B * NG + (s - PV_LAG) // HG - 1)
                    if s < HEADS:
                        head_max(n, 0)
                    for f in extra.get(s - 0.5, []):
                        f()
                    if s < HEADS:
                        head_max(n, 1)
                    for f in extra.get(s, []):
                        f()

            dve.wait_ge(ld["x"], 16)
            norm_stats("a0", 0, x_sb[:, 0])
            normalise("a0", 0, x_sb[:, 0])
            dve.wait_ge(ld["col"], 16)
            dve.wait_ge(k_evacuated, 1)
            dve.scalar_tensor_tensor(out=k_rest[0][:, :], in0=bank[:, 0, :], scalar=col[:, COL_BK0:COL_BK0 + 1],
                                     in1=k_part[0][:, 0, :], op0=ALU.add, op1=ALU.subtract).then_inc(k_rest_ready[0], 1)
            xT_copy("a0", 0)
            dve.wait_ge(k_second, 1)
            tt(k_part[0][:, 2, :], k_rest[0][:, :], k_part[0][:, 1, :], ALU.subtract).then_inc(k_parts[0], 1)
            q_split(0, 0)
            norm_stats("a0", 1, x_sb[:, 1])
            dve.wait_ge(ld["mask"], 32)
            ts(bias_q[:, :, :], mask_q[:, :, :], 0.0, MASKED, ALU.is_equal, ALU.mult).then_inc(mask_ready, 1)
            normalise("a0", 1, x_sb[:, 1])
            v_copy(0, 4)
            xT_copy("a0", 1)
            q_split(0, 1)
            dve.wait_ge(mask_ready, 1)

            def bias_for_cols():
                ts(bias_k[:, :, :], mask_k[:, :, :], 0.0, MASKED, ALU.is_equal, ALU.mult).then_inc(mask_ready, 1)

            attention(0, {
                0: [lambda: v_copy(3, 3)],
                1: [lambda: v_copy(1, 5)],
                2: [bias_for_cols],
                3: [lambda: v_copy(2, OUT)],
                27.5: [lambda: attT_copy(0, 0)],
                28.5: [lambda: add_attention(0, 0)],
                30: [lambda: normalise("f0", 0, res[1][0])],
                31: [lambda: xT_copy("f0", 0)],
                34: [lambda: route0(0, 0), lambda: route0(0, 1)],
                35: [lambda: route0(0, 2), lambda: route0(0, 3)],
                40: [lambda: c_copy(0, 0)],
            })

            def experts0(b, extra):
                for i in range(T0 // 2 + 1):
                    for f in extra.get(i, []):
                        f()
                    hidden0(b, i)

            experts0(0, {
                0: [lambda: divide(B * NG - 1)],
                1: [lambda: attT_copy(0, 1)],
                2: [lambda: add_attention(0, 1)],
                3: [lambda: normalise("f0", 1, res[1][1]), lambda: xT_copy("f0", 1)],
                4: [lambda: route0(1, 0)],
                5: [lambda: route0(1, 1), lambda: route0(1, 2)],
                6: [lambda: route0(1, 3)],
            })
            c_copy(0, 1)
            experts0(1, {
                0: [lambda: add_experts0(0), lambda: normalise("a1", 0, res[2][0]),
                    lambda: norm_stats("a1n", 0, norm["a1"][0])],
                1: [lambda: normalise("a1n", 0, norm["a1"][0])],
                2: [lambda: xT_copy("a1n", 0)],
                3: [lambda: q_split(1, 0)],
            })
            dve.wait_ge(sel_ready, 1)
            attention(1, {
                0: [lambda: add_experts0(1), lambda: norm_twice(1)],
                2: [lambda: xT_copy("a1n", 1)],
                4: [lambda: q_split(1, 1)],
                27.5: [lambda: attT_copy(1, 0)],
                28.5: [lambda: add_attention(1, 0)],
                30: [lambda: normalise("f1", 0, res[3][0])],
                31: [lambda: xT_copy("f1", 0)],
                32: [lambda: gate_shift1(0)],
                33: [lambda: route1(0)],
                36: [lambda: c_copy(1, 0)],
                39: [lambda: start_acc(0)],
            })
            steps1 = [(b, i) for b in range(B) for i in range(E1 // 2)]
            tail = {0: [lambda: divide(2 * B * NG - 1)],
                    1: [lambda: attT_copy(1, 1)],
                    1.6: [lambda: add_attention(1, 1)],
                    2.3: [lambda: normalise("f1", 1, res[3][1])],
                    2.6: [lambda: xT_copy("f1", 1)],
                    3.3: [lambda: gate_shift1(1)],
                    4.6: [lambda: route1(1)],
                    5.6: [lambda: c_copy(1, 1)],
                    6.6: [lambda: start_acc(1)]}
            for k in range(len(steps1) + 3):
                for f in tail.get(k, []):
                    f()
                if k >= 3:
                    b, i = steps1[k - 3]
                    accumulate1(b, i)
                    if i == E1 // 2 - 1:
                        last_stats(b)
                if 1 <= k <= len(steps1):
                    normalise1(*steps1[k - 1])
                for f in tail.get(k + 0.3, []):
                    f()
                if k < len(steps1):
                    stats1(*steps1[k])
                if k >= 3 and steps1[k - 3][1] == E1 // 2 - 1:
                    finish(steps1[k - 3][0])
                for f in tail.get(k + 0.6, []):
                    f()

        @block.scalar
        def _(act):
            def k_evacuate(i):
                c = (COL_BK0, COL_BK1)[i // B]
                act.wait_ge(k_proj, i + 1)
                if i >= 1:
                    act.activation(k_full[i][:, :], bank[:, i, :], ACT.Identity, bias=col[:, c:c + 1])
                act.activation(k_part[i][:, 0, :], bank[:, i, :], ACT.Identity, bias=col[:, c:c + 1]).then_inc(k_evacuated, 1)

            def k_second_part(i):
                act.wait_ge(k_rest_ready[i], 1)
                act.copy(k_part[i][:, 1, :], k_rest[i][:, :]).then_inc(k_second, 1)

            act.dma_start(aw[:, 0], attn_w[:, 0]).then_inc(ld["aw0"], 16)
            act.dma_start(col[:, :], cols).then_inc(ld["col"], 16)
            act.dma_start(row[:, :, :], rows.to_broadcast([128, len(ROW_NAMES), D])).then_inc(ld["row"], 16)
            act.dma_start(aw[:, 1], attn_w[:, 1]).then_inc(ld["aw1"], 16)
            act.wait_ge(pad_ready, 2)
            act.dma_start(q_stack[STACK:MAX_ROW].rearrange("r b h s -> r (b h) s"),
                          zero_rows[:, 0:S].unsqueeze(1).to_broadcast([MAX_ROW - STACK, B * H, S])).then_inc(ld["pad"], 16)
            act.dma_start(k_stack[STACK:MAX_ROW].rearrange("r b h s -> r (b h) s"),
                          zero_rows[:, :].unsqueeze(1).to_broadcast([MAX_ROW - STACK, B * H, S2])).then_inc(ld["pad"], 16)
            act.dma_start(k_stack[MAX_ROW:ROWS_K].rearrange("r b h s -> r (b h) s"),
                          minus_ones[:, :].unsqueeze(1).to_broadcast([PARTS, B * H, S2])).then_inc(ld["pad"], 16)
            act.dma_start(sel_f[:, :, :], select0).then_inc(ld["sel"], 16)
            act.wait_ge(half_ready, 1)
            act.activation(table[:, :], minus_half[:, :], ACT.Exp)
            act.wait_ge(ld["col"], 16)
            k_evacuate(0)
            k_second_part(0)
            for i in range(1, 4):
                k_evacuate(i)
            for i in range(1, 4):
                k_second_part(i)
            act.wait_ge(ld["sel"], 16)
            act.copy(sel[:, :, :], sel_f[:, :, :]).then_inc(sel_ready, 1)

            def max_copy(g):
                b, h = g % (HEADS // MG) // (H // MG), g % (H // MG) * MG
                act.wait_ge(misc_ready, use[f"max{g}"])
                act.copy(q_stack[MAX_ROW:ROWS_K, b, h:h + MG, :].rearrange("p h s -> p (h s)"),
                         bank[MAX_ROW:ROWS_K, MISC, 0:MG * S // 2].bitcast(BF16)).then_inc(max_copied, 1)
                act.wait_ge(max_copied, g + 1)
                act.sem_inc(misc_free, 1)

            def exponentials(n):
                g = n // HG
                act.wait_ge(scores_ready, n + 1)
                if n >= 2 * HG:
                    act.wait_ge(pv_done, g - 1)
                at = 2 + 2 * (n % 2)
                act.activation(probs[:, n % (2 * HG), :], bank[:, at:at + 2, :].rearrange("p a n -> p (a n)"), ACT.Exp,
                               scale=SCALE).then_inc(exp_done, 1)

            def o_copy(g):
                act.wait_ge(pv_done, g + 1)
                if g >= 2:
                    act.wait_ge(misc_ready, use[f"o{g - 2}"])
                act.copy(o_sb[:, g % 2, :], bank[:, OUT, 0:S]).then_inc(o_copied, 1)

            def gate_exponential(l, b):
                e, src = (E0, bank[:, MISC, 0:QT * E0].rearrange("p (t e) -> p t e", t=QT)) if l == 0 else \
                    (E1, r_score[:, :, 0:E1])
                if l == 0:
                    act.wait_ge(misc_ready, use[f"gate0{b}"])
                else:
                    act.wait_ge(gate_in, b + 1)
                if b == 1:
                    act.wait_ge(combined[l], 1)
                elif l == 1:
                    act.wait_ge(combined[0], B)
                ins = act.activation(r_exp[:, :, 0:e], src, ACT.Exp, scale=(-1.0, 1.0)[l])
                ins.then_inc(gate_exp[l], 1)
                if l == 0:
                    act.wait_ge(gate_exp[l], b + 1)
                    act.sem_inc(misc_free, 1)

            def attention(l, extra):
                for s in range(HEADS + PV_LAG):
                    if s % MG == 1 and 0 <= (s - 3) // MG < HEADS // MG:
                        max_copy(l * HEADS // MG + (s - 3) // MG)
                    if 0 <= s - LAG < HEADS:
                        exponentials(l * HEADS + s - LAG)
                    if s % HG == (PV_LAG - 1) % HG and s >= PV_LAG:
                        o_copy(l * B * NG + (s - PV_LAG) // HG)
                    for f in extra.get(s, []):
                        f()

            def silu(b, i):
                u = b * (T0 // 2 + 1) + i
                at = 2 + 2 * (u % 2)
                if u >= 2:
                    act.wait_ge(hid0_ready, u - 1)
                if i < T0 // 2:
                    act.wait_ge(misc_ready, use[f"spread{u}"])
                    act.copy(c_sb[:, u % 2], bank[:, MISC, :].rearrange("p (j s) -> p j s", j=2)).then_inc(c_spread, 1)
                    act.wait_ge(c_spread, b * (T0 // 2) + i + 1)
                    act.sem_inc(misc_free, 1)
                act.wait_ge(gu_ready, u + 1)
                if i == T0 // 2:
                    ins = act.activation(silu_g[0:I0, u % 2, 0, :], bank[0:I0, at, 0:S], ACT.Silu)
                else:
                    ins = act.activation(silu_g[:, u % 2], bank[:, at:at + 2, 0:S], ACT.Silu)
                ins.then_inc(silu_done, 1)

            def normalise1(b, i):
                w = b * (E1 // 2) + i
                act.wait_ge(rstd1_ready, w + 1)
                if w >= 2:
                    act.wait_ge(tr1_ready, 4 * (w - 1))
                for e in range(2):
                    k = 2 + e
                    act.activation(hn1[:, w % 2, 1, e, :], bank[:, 2 * (w % 2) + 1, e * H1:(e + 1) * H1], ACT.Identity,
                                   bias=shift1[:, w % 2, k:k + 1], scale=rs1[:, w % 2, k:k + 1]).then_inc(norm1_done[1], 1)

            def gelu1(b, i):
                w = b * (E1 // 2) + i
                if w >= 2:
                    act.wait_ge(down1_done, w - 1)
                for e in range(2):
                    for half in range(2):
                        k = 2 * e + half
                        c = 2 * (2 * i + e) + half
                        act.wait_ge(tr1_ready, 4 * w + 2 * e + 2)
                        act.activation(hid1[:, w % 2, k, :], bank[:, 4 + e, half * S:(half + 1) * S], ACT.Gelu,
                                       bias=col[:, COL_B1 + c:COL_B1 + c + 1],
                                       scale=col[:, COL_G1 + c:COL_G1 + c + 1]).then_inc(gelu_done, 1)

            act.wait_ge(mask_ready, 2)
            attention(0, {32: [lambda: gate_exponential(0, 0)]})
            for i in range(4):
                act.wait_ge(k_written[i], 16)
            for b in range(B):
                for i in range(T0 // 2 + 1):
                    silu(b, i)
                    if (b, i) == (0, 3):
                        gate_exponential(0, 1)
            attention(1, {32: [lambda: gate_exponential(1, 0)]})
            for b in range(B):
                for i in range(E1 // 2):
                    normalise1(b, i)
                    gelu1(b, i)
                    if (b, i) == (0, 2):
                        gate_exponential(1, 1)

        @block.gpsimd
        def _(pool):
            steps = [0]

            def then(ins):
                steps[0] += 1
                ins.then_inc(pool_step, 1)
                pool.wait_ge(pool_step, steps[0])

            def root(n, b):
                pool.wait_ge(var_ready[n], QT * (b + 1))
                then(pool.tensor_scalar(var_eps[:, :], mean_var[n, b][:, :, 1], EPS, None, ALU.add))
                pool.tensor_tensor(rstd[n, b][:, :], var_eps[:, :], minus_half[:, 0:QT], ALU.pow).then_inc(rstd_ready[n], 1)

            def add_row(s, b, name):
                r = row[:, ROW_NAMES.index(name), :].unsqueeze(1).to_broadcast([128, QT, D])
                pool.tensor_tensor(res_bias[s][b][:, :, :], res[s][b], r, ALU.add).then_inc(res_bias_ready[s], 1)

            pool.memset(minus_half[:, :], -0.5).then_inc(half_ready, 1)
            pool.memset(zero_rows[:, :], 0.0).then_inc(pad_ready, 1)
            pool.memset(minus_ones[:, :], -1.0).then_inc(pad_ready, 1)
            pool.memset(ones_parts[:, :], 1.0).then_inc(ones_ready, 1)
            for l in range(2):
                pool.memset(v_ext[l][:, :, H * (DK + 1):], 0.0).then_inc(v_zeroed[l], 1)
                pool.memset(v_heads[l][:, :, :, DK], 1.0).then_inc(v_zeroed[l], 1)
            pool.wait_ge(half_ready, 1)
            root("a0", 0)
            pool.wait_ge(ld["ident"], 16)
            pool.tensor_copy(idb[:, :], idf[:, :]).then_inc(consts_ready, 1)
            root("a0", 1)

            def max_split(g):
                pool.wait_ge(max_done, 2 * MG * (g + 1))
                if g >= 2:
                    pool.wait_ge(misc_ready, use[f"max{g - 2}"])
                m = row_max[:, g % 2]
                part = [max_part[:, g % 2, :, :, a] for a in range(PARTS)]
                then(pool.tensor_copy(part[0], m))
                then(pool.tensor_tensor(max_rest[:, :, :], m, part[0], ALU.subtract))
                then(pool.tensor_copy(part[1], max_rest[:, :, :]))
                pool.tensor_tensor(part[2], max_rest[:, :, :], part[1], ALU.subtract).then_inc(max_parts, 1)

            for i in range(1, 4):
                l, b = divmod(i, B)
                pool.wait_ge(k_evacuated, i + 1)
                pool.tensor_tensor(k_rest[i][:, :], k_full[i][:, :], k_part[i][:, 0, :], ALU.subtract).then_inc(k_rest_ready[i], 1)
                pool.wait_ge(k_second, i + 1)
                pool.tensor_tensor(k_part[i][:, 2, :], k_rest[i][:, :], k_part[i][:, 1, :], ALU.subtract).then_inc(k_parts[i], 1)

            for g in range(4):
                max_split(g)
            pool.wait_ge(ld["row"], 16)
            pool.wait_ge(ld["x"], 16)
            for b in range(B):
                add_row(0, b, "bo0")
            pool.wait_ge(ld["bu1"], 16)
            then(pool.tensor_copy(bu1_part[:, 0, :], bu1_sb[:, :]))
            then(pool.tensor_tensor(bu1_rest[:, :], bu1_sb[:, :], bu1_part[:, 0, :], ALU.subtract))
            then(pool.tensor_copy(bu1_part[:, 1, :], bu1_rest[:, :]))
            pool.tensor_tensor(bu1_part[:, 2, :], bu1_rest[:, :], bu1_part[:, 1, :], ALU.subtract).then_inc(bu1_split, 1)

            for g in range(4, HEADS // MG):
                max_split(g)
                if MG * g + MG - 1 == 29:
                    root("f0", 0)
            root("f0", 1)
            root("a1", 0)
            root("a1n", 0)
            pool.wait_ge(res_ready[2], QT)
            add_row(2, 0, "bo1")
            root("a1", 1)
            root("a1n", 1)
            pool.wait_ge(res_ready[2], 2 * QT)
            add_row(2, 1, "bo1")
            for g in range(HEADS // MG, 2 * HEADS // MG):
                max_split(g)
                if MG * g + MG - 1 == HEADS + 29:
                    root("f1", 0)

            def root1(w):
                pool.wait_ge(var1_ready, 4 * (w + 1))
                then(pool.tensor_scalar(ve1[:, :], mv1[:, w % 2, :, 1], EPS, None, ALU.add))
                if w >= 2:
                    for t in range(QT):
                        pool.wait_ge(norm1_done[t], 2 * (w - 1))
                then(pool.tensor_tensor(rs1[:, w % 2, :], ve1[:, :], minus_half[:, :], ALU.pow))
                then(pool.tensor_tensor(shift1[:, w % 2, :], mv1[:, w % 2, :, 0], rs1[:, w % 2, :], ALU.mult))
                pool.tensor_scalar(shift1[:, w % 2, :], shift1[:, w % 2, :], -1.0, None, ALU.mult).then_inc(rstd1_ready, 1)

            pool.wait_ge(res_ready[3], 1)
            add_row(3, 0, "lnf_b")
            root1(0)
            root1(1)
            root("f1", 1)
            pool.wait_ge(res_ready[3], 2)
            add_row(3, 1, "lnf_b")
            for w in range(2, 6):
                root1(w)
            root("out", 0)
            for w in range(6, 8):
                root1(w)
            root("out", 1)

        @block.sync
        def _(sp):
            sp.dma_start(ctxT_sb[:, 0], ctxT[:, 0]).then_inc(ld["ctx0"], 16)
            sp.dma_start(x_sb[:, :, :, :], x.rearrange("b (t p) d -> p b t d", p=128)).then_inc(ld["x"], 16)
            sp.dma_start(idf[:, :], ident).then_inc(ld["ident"], 16)
            sp.dma_start(ctxT_sb[:, 1], ctxT[:, 1]).then_inc(ld["ctx1"], 16)
            sp.dma_start(mask_q[:, :, :], mask.rearrange("(t p) k -> p t k", p=128)).then_inc(ld["mask"], 16)
            sp.dma_start(mask_k[:, :, :], maskT.rearrange("(t p) q -> p t q", p=128)).then_inc(ld["mask"], 16)

            def k_out(i):
                sp.wait_ge(k_parts[i], 1)
                sp.dma_start(k_bounce[i].rearrange("a p s -> p a s"), k_part[i][:, :, :]).then_inc(k_written[i], 16)

            def k_in(i, heads, signal):
                sp.wait_ge(k_written[i], 16)
                for a in range(PARTS):
                    sp.dma_start(k_stack[a * PARTS * DK:(a + 1) * PARTS * DK, i % B, heads, :],
                                 k_bounce[i].rearrange("j (d h) s -> (j d) h s", h=H)[:, heads, :]).then_inc(signal, 16)

            def q_out(i):
                sp.wait_ge(q_parts[i], 1)
                for a in range(PARTS):
                    sp.dma_start(q_bounce[i][:, a].rearrange("a p s -> p a s"), q_part[i % B][:, :, :])\
                        .then_inc(q_written[i], 16)

            def q_in(i, heads, signal):
                sp.wait_ge(q_written[i], 16 * PARTS)
                sp.dma_start(q_stack[0:STACK, i % B, heads, :],
                             q_bounce[i].rearrange("i j (d h) s -> (i j d) h s", h=H)[:, heads, :]).then_inc(signal, 16)

            first, rest, every = slice(0, HG), slice(HG, H), slice(0, H)
            k_out(0)
            q_out(0)
            k_in(0, first, first_stacked)
            q_in(0, first, first_stacked)
            k_in(0, rest, k_stacked[0])
            q_in(0, rest, q_stacked[0])
            q_out(1)
            k_out(1)
            k_in(1, every, k_stacked[1])
            q_in(1, every, q_stacked[1])
            k_out(2)
            k_out(3)
            sp.dma_start(g0_sb[:, :], gate0).then_inc(ld["router"], 16)
            sp.dma_start(g1_sb[:, :], gate1).then_inc(ld["router"], 16)
            sp.dma_start(gbias[:, :], gate_bias.to_broadcast([128, E0])).then_inc(ld["router"], 16)
            sp.dma_start(tie[:, :, :], ties.to_broadcast([128, E0, E0])).then_inc(ld["router"], 16)

            sp.dma_start(bu1_sb[:, :], bu1).then_inc(ld["bu1"], 16)
            sp.dma_start(wg0_sb[:, :], wg0).then_inc(ld["wg0"], 16)
            sp.dma_start(wu0_sb[:, :], wu0).then_inc(ld["wu0"], 16)
            sp.dma_start(wd0_sb[:, :, :], wd0.rearrange("(t p) d -> p t d", p=128)).then_inc(ld["wd0"], 16)
            sp.dma_start(wsd0_sb[:, :], wsd0).then_inc(ld["wd0"], 16)
            sp.dma_start(bd1_sb[:, :], bd1).then_inc(ld["wd1"], 16)
            sp.wait_ge(bu1_split, 1)
            sp.wait_ge(k_proj, 4)
            sp.wait_ge(v_proj, 4)
            for a in range(PARTS):
                sp.dma_start(bu1_rows[a:a + 1, :].rearrange("o (p c) -> o p c", p=128),
                             bu1_part[:, a, :]).then_inc(bu1_ready, 16)
            sp.wait_ge(scores_ready, HEADS)
            for i in range(B, 2 * B):
                k_in(i, every, k_stacked[i])
            q_out(2)
            q_in(2, every, q_stacked[2])
            sp.wait_ge(down0_done, 2 * (T0 // 2 + 1))
            sp.dma_start(wu1_sb[:, :, :], wu1).then_inc(ld["wu1"], 16)
            sp.dma_start(wd1_sb[:, :, :], wd1.rearrange("(t p) d -> p t d", p=128)).then_inc(ld["wd1"], 16)
            q_out(3)
            q_in(3, every, q_stacked[3])
            for b in range(B):
                sp.wait_ge(stored_ready, b + 1)
                sp.dma_start(out[b].rearrange("(t p) d -> p t d", p=128), result[:, b]).then_inc(stored, 16)
            sp.wait_ge(stored, 16 * B)


def kernel(**inputs):
    import concourse.bacc as _bacc
    from concourse.bass_utils import run_bass_kernel_spmd as _run

    a = {k: np.asarray(v) for k, v in inputs.items()}

    def head_minor(w):
        return w.reshape(H, DK, *w.shape[1:]).swapaxes(0, 1).reshape(w.shape)

    def proj(l):
        q, k, v, o = (("L0_xattn_w_q", "L0_xattn_w_k", "L0_xattn_w_v", "L0_xattn_w_out"),
                      ("L1_xattn_Wq", "L1_xattn_Wk", "L1_xattn_Wv", "L1_xattn_Wo"))[l]
        return np.stack([head_minor(a[k]).T, head_minor(a[q]).T, a[v].T, a[o].T], axis=1)

    by_unit = [a[n].reshape(E1, 2, 128).transpose(2, 0, 1).reshape(128, 2 * E1) for n in ("L1_ffn_ln1_g", "L1_ffn_ln1_b")]
    cols = np.concatenate([np.stack([head_minor(a["L0_xattn_b_k"]), head_minor(a["L0_xattn_b_q"]),
                                     head_minor(a["L1_xattn_bk"]), head_minor(a["L1_xattn_bq"]),
                                     a["L1_xattn_ln_g"], a["L1_xattn_ln_b"]], axis=1)] + by_unit, axis=1)
    rows = np.stack([a[n] for n in ("L0_xattn_b_v", "L0_xattn_b_out", "L1_xattn_bv", "L1_xattn_bo",
                                    "L1_ffn_ln_g", "L1_ffn_ln_b")])[None]
    index = np.arange(E0)
    ties = (index[None, :] < index[:, None]).astype(np.float32)[None]
    expert_of_row = (np.arange(E0 * I0) // I0).reshape(T0, 128)
    select = np.tile((expert_of_row[None] == index[:, None, None]).astype(np.float32), (PARTS, 1, 1))
    arrays = {
        "x": a["x"],
        "ctxT": a["ctx_1024"].transpose(2, 0, 1),
        "mask": a["mask_SxS2_ik0"],
        "maskT": a["mask_SxS2_ik0"].T,
        "attn_w": np.stack([proj(0), proj(1)], axis=1),
        "cols": cols,
        "rows": rows,
        "gate_bias": a["L0_ffn_gate_bias"][None],
        "ties": ties,
        "ident": np.eye(128, dtype=np.float32),

        "gate0": a["L0_ffn_gate_w"].T,
        "gate1": a["L1_ffn_gate_w"],
        "wg0": np.concatenate([a["L0_ffn_w1"].reshape(E0 * I0, D), a["L0_ffn_ws1"]]).T,
        "wu0": np.concatenate([a["L0_ffn_w3"].reshape(E0 * I0, D), a["L0_ffn_ws3"]]).T,
        "wd0": a["L0_ffn_w2"].transpose(0, 2, 1).reshape(E0 * I0, D),
        "wsd0": a["L0_ffn_ws2"].T,
        "select0": select,
        "wu1": a["L1_ffn_w1"].transpose(1, 0, 2),
        "bu1": a["L1_ffn_b1"].reshape(128, E1 * H1 // 128),
        "wd1": a["L1_ffn_w2"].reshape(E1 * H1, D),
        "bd1": a["L1_ffn_b2"],
    }
    arrays = {f"in_{k}": np.ascontiguousarray(v) for k, v in arrays.items()}
    nc = _bacc.Bacc("TRN2", target_bir_lowering=False, num_devices=1)
    args = [nc.dram_tensor(k, v.shape, mybir.dt.from_np(v.dtype), kind="ExternalInput").ap() for k, v in arrays.items()]
    args.append(nc.dram_tensor("out_0", (B, S, D), F32, kind="ExternalOutput").ap())
    attention_ffn_kernel(nc, *args)
    r = _run(nc, [arrays], core_ids=[0])
    return r.results[0]["out_0"]
```

```python
from contextlib import ExitStack

import numpy as np

import concourse.bass as bass
from concourse import mybir

F32, BF16, I32 = mybir.dt.float32, mybir.dt.bfloat16, mybir.dt.int32
ALU = mybir.AluOpType
ACT = mybir.ActivationFunctionType
AX = mybir.AxisListType

B, S, S2, D = 2, 256, 512, 128
H, DK = 16, 8
QT, KT = S // 128, S2 // 128
PARTS = 3
STACK = PARTS * PARTS * DK
MAX_ROW = 96
ROWS_K = MAX_ROW + PARTS
MG = 2
E0, I0 = 16, 96
T0 = E0 * I0 // 128
E1, H1 = 8, 256
GROUPS0 = 4
HG = 4
NG = H // HG
VW = 32
SCALE = float(DK) ** -0.5
EPS = 1e-5
MASKED = -float(2.0 ** 100)
LOWEST = -3.0e38
LAG = 5
BEGUN = 6
PV_LAG = LAG + HG
HEADS = B * H

ROW_NAMES = ["bv0", "bo0", "bv1", "bo1", "lnf_g", "lnf_b"]
COL_BK0, COL_BQ0, COL_BK1, COL_BQ1, COL_LNG, COL_LNB, COL_G1 = 0, 1, 2, 3, 4, 5, 6
COL_B1 = COL_G1 + 2 * E1
NCOLS = COL_B1 + 2 * E1


def attention_ffn_kernel(nc, x, ctxT, mask, maskT, attn_w, cols, rows, gate_bias, ties, ident,
                         gate0, gate1, wg0, wu0, wd0, wsd0, select0, wu1, bu1, wd1, bd1, out):
    ctx = ExitStack()
    with ctx:
        def sb(name, shape, dt=F32):
            return ctx.enter_context(nc.sbuf_tensor(name, shape, dt))

        def sem(name):
            return ctx.enter_context(nc.semaphore(name))

        k_bounce = [nc.dram_tensor(f"k_bounce{i}", [PARTS, 128, S2], BF16, kind="Internal").ap()
                    for i in range(4)]
        q_bounce = [nc.dram_tensor(f"q_bounce{i}", [PARTS, PARTS, 128, S], BF16, kind="Internal").ap()
                    for i in range(4)]

        x_sb = sb("x_sb", [128, B, QT, D])
        ctxT_sb = sb("ctxT_sb", [128, B, S2])
        probs = sb("probs", [128, 2 * HG, KT * S])
        mask_q = probs[:, 0, :].bitcast(I32).rearrange("p (t k) -> p t k", t=QT)
        mask_k = probs[:, 1, :].bitcast(I32).rearrange("p (t q) -> p t q", t=KT)
        experts_w = sb("experts_w", [128, 2 * (T0 * 128 + I0) + T0 * D])
        early = sb("early", [128, 4 * (2 * S2 + PARTS * S2 // 2)])
        shared_area = sb("shared_area", [128, T0 * 128])
        aw = sb("aw", [128, 2, 4, 128])
        W_K, W_Q, W_V, W_O = 0, 1, 2, 3
        col = sb("col", [128, NCOLS])
        row = sb("row", [128, len(ROW_NAMES), D])
        gbias = sb("gbias", [128, E0])
        tie_f = sb("tie_f", [128, E0, E0])
        tie = sb("tie", [128, E0, E0], BF16)
        idf = sb("idf", [128, 128])
        g0_sb = sb("g0_sb", [128, E0])
        g1_sb = sb("g1_sb", [128, E1])
        up_cols = E0 * I0 + I0
        wg0_sb = experts_w[:, 0:up_cols]
        wu0_sb = experts_w[:, up_cols:2 * up_cols]
        wd0_sb = experts_w[:, 2 * up_cols:2 * up_cols + T0 * D].rearrange("p (t d) -> p t d", t=T0)
        wsd0_sb = sb("wsd0_sb", [I0, D])
        sel_f = shared_area[0:PARTS * E0, :].rearrange("p (t r) -> p t r", t=T0)
        wu1_sb = experts_w[:, 0:E1 * H1].rearrange("p (e n) -> p e n", e=E1)
        bu1_sb = sb("bu1_sb", [128, E1 * H1 // 128])
        wd1_sb = experts_w[:, E1 * H1:2 * E1 * H1].rearrange("p (t d) -> p t d", t=2 * E1)
        bd1_sb = sb("bd1_sb", [E1, D])

        idb = sb("idb", [128, 128], BF16)
        sel = sb("sel", [PARTS * E0, T0, 128], BF16)
        bias_q = sb("bias_q", [128, QT, S2])
        bias_k = sb("bias_k", [128, KT, S], BF16)
        minus_half = sb("minus_half", [128, 4])
        ones_parts = sb("ones_parts", [PARTS, 128], BF16)
        minus_ones = sb("minus_ones", [PARTS, S2], BF16)
        zero_rows = sb("zero_rows", [MAX_ROW - STACK, S2], BF16)
        bu1_part = sb("bu1_part", [128, PARTS, E1 * H1 // 128], BF16)
        bu1_rest = sb("bu1_rest", [128, E1 * H1 // 128])
        bu1_rows = ctxT_sb[0:PARTS].rearrange("p b k -> p (b k)").bitcast(BF16)

        k_full = [early[:, i * S2:(i + 1) * S2] for i in range(4)]
        k_rest = [early[:, (4 + i) * S2:(5 + i) * S2] for i in range(4)]
        part_cols = PARTS * S2 // 2
        k_part = [early[:, 8 * S2 + i * part_cols:8 * S2 + (i + 1) * part_cols].bitcast(BF16)
                  .rearrange("p (a s) -> p a s", a=PARTS) for i in range(4)]

        q_rest = sb("q_rest", [128, S])
        q_part = [sb(f"q_part{b}", [128, PARTS, S], BF16) for b in range(B)]
        k_stack = sb("k_stack", [ROWS_K, B, H, S2], BF16)
        q_stack = sb("q_stack", [ROWS_K, B, H, S], BF16)
        v_ext = [sb(f"v_ext{l}", [128, B * KT, H * (DK + 1) + VW - DK - 1]) for l in range(2)]
        v_heads = [v[:, :, 0:H * (DK + 1)].rearrange("p t (h c) -> p t h c", h=H) for v in v_ext]
        row_max = sb("row_max", [128, 2, MG, QT])
        max_rest = sb("max_rest", [128, MG, QT])
        max_part = sb("max_part", [128, 2, MG, QT, PARTS], BF16)
        table = sb("table", [128, 8])
        discard = sb("discard", [128, QT, S2], BF16)
        o_sb = sb("o_sb", [128, 2, S])
        rden = sb("rden", [128, QT, HG])
        att = [[sb(f"att{b}", [128, QT, D]) for b in range(B)],
               [shared_area[:, b * S:(b + 1) * S].rearrange("p (t d) -> p t d", t=QT) for b in range(B)]]
        attT = [[sb(f"attT{b}", [128, S]) for b in range(B)],
                [shared_area[:, (2 + b) * S:(3 + b) * S] for b in range(B)]]

        res = [[x_sb[:, b] for b in range(B)]] + [
            [sb(f"res{s}{b}", [128, QT, D])[:] for b in range(B)] for s in range(1, 3)]
        res.append(res[1])
        res_bias = {s: [sb(f"res_bias{s}{b}", [128, QT, D]) for b in range(B)] for s in (0, 3)}
        res_bias[2] = res_bias[0]
        norm = {n: [sb(f"norm_{n}{b}", [128, QT, D]) for b in range(B)] for n in ("a0", "f0", "f1")}
        norm["a1n"], norm["a1"], norm["out"] = norm["a0"], norm["f0"], norm["f0"]
        mean_var = {(n, b): sb(f"mv_{n}{b}", [128, QT, 2]) for n in norm for b in range(B)}
        rstd = {(n, b): sb(f"rstd_{n}{b}", [128, QT]) for n in norm for b in range(B)}

        var_eps = sb("var_eps", [128, QT])
        stats = sb("stats", [128, QT, 6])
        xT = {n: [sb(f"xT_{n}{b}", [128, S]) for b in range(B)] for n in ("a0", "f0")}
        xT["a1n"], xT["f1"] = xT["a0"], xT["f0"]

        r_exp = sb("r_exp", [128, QT, E0])
        r_score = sb("r_score", [128, QT, E0])
        r_biased = sb("r_biased", [128, QT, E0])
        r_pair = sb("r_pair", [128, 4, QT, GROUPS0])
        r_top = sb("r_top", [128, 3, QT, GROUPS0])
        r_gsum = sb("r_gsum", [128, QT, GROUPS0])
        r_ge, r_gt = [bias_q[:, t, 0:S2 // 2].bitcast(BF16).rearrange("p (t i j) -> p t i j", t=QT, i=E0)
                      for t in range(QT)]
        r_rank = sb("r_rank", [128, QT, E0])
        r_keep = sb("r_keep", [128, QT, GROUPS0])
        r_drop = sb("r_drop", [128, QT, GROUPS0])
        r_small = sb("r_small", [128, 2, QT])
        combine = [[sb(f"combine{l}{b}", [128, QT, (E0, E1)[l]]) for b in range(B)] for l in range(2)]
        c_part = sb("c_part", [128, QT, PARTS, E0], BF16)
        c_rest = sb("c_rest", [128, QT, E0])
        c_rows = [sb(f"c_rows{b}", [PARTS * E0, S], BF16) for b in range(B)]
        cT1 = [sb(f"cT1{b}", [E1, S]) for b in range(B)]

        def late(at, size, pattern, **kw):
            return early[:, at:at + size].rearrange(pattern, **kw)

        silu_g, gated, hid0 = [late(i * 4 * S, 4 * S, "p (u j s) -> p u j s", u=2, j=2) for i in range(3)]
        c_sb = late(12 * S, 4 * S, "p (u j s) -> p u j s", u=2, j=2)
        hn1 = late(12 * S, 2 * QT * 2 * H1, "p (u t e n) -> p u t e n", u=2, t=QT, e=2)
        hid1 = late(12 * S + 2 * QT * 2 * H1, 8 * S, "p (u k s) -> p u k s", u=2, k=4)
        PAIRS0 = T0 // 2 + 1
        st1 = sb("st1", [128, 4, 6])
        mv1 = sb("mv1", [128, 2, 4, 2])

        ve1 = sb("ve1", [128, 4])
        minus_mean = sb("minus_mean", [128, 4])
        rs1 = sb("rs1", [128, 2, 4])
        shift1 = sb("shift1", [128, 2, 4])
        acc = [shared_area[:, (4 + b) * S:(5 + b) * S].rearrange("p (t d) -> p t d", t=QT) for b in range(B)]
        result = x_sb

        bank = ctx.enter_context(nc.psum_tensor("bank", [128, 8, 512], F32))
        MISC, OUT = 7, 6

        ld = {n: sem(f"ld_{n}") for n in ("ctx0", "ctx1", "x", "aw0", "aw1", "col", "row", "ident", "mask",
                                          "router", "wg0", "wu0", "wd0", "sel", "wu1", "bu1", "wd1", "pad0", "pad1")}
        consts_ready = sem("consts_ready")
        half_ready = sem("half_ready")
        v_zeroed = [sem(f"v_zeroed{l}") for l in range(2)]
        ones_ready = sem("ones_ready")
        pad_ready = sem("pad_ready")

        mask_ready = sem("mask_ready")
        sel_ready = sem("sel_ready")
        bu1_split = sem("bu1_split")
        bu1_ready = sem("bu1_ready")
        k_proj = sem("k_proj")
        k_evacuated = sem("k_evacuated")
        k_rest_ready = [sem(f"k_rest_ready{i}") for i in range(4)]
        k_second = sem("k_second")
        k_parts = [sem(f"k_parts{i}") for i in range(4)]
        k_written = [sem(f"k_written{i}") for i in range(4)]
        k_stacked = [sem(f"k_stacked{i}") for i in range(4)]
        first_stacked = sem("first_stacked")
        q_parts = [sem(f"q_parts{i}") for i in range(4)]
        q_written = [sem(f"q_written{i}") for i in range(4)]
        q_stacked = [sem(f"q_stacked{i}") for i in range(4)]
        v_proj = sem("v_proj")
        v_copied = [sem(f"v_copied{i}") for i in range(2 * B)]
        v_ready = [sem(f"v_ready{i}") for i in range(2 * B)]
        misc_ready = sem("misc_ready")
        misc_free = sem("misc_free")
        for_max = sem("for_max")
        max_done = sem("max_done")
        max_parts = sem("max_parts")
        max_copied = sem("max_copied")
        scores_ready = sem("scores_ready")
        exp_done = sem("exp_done")
        pv_done = sem("pv_done")
        o_copied = sem("o_copied")
        att_done = sem("att_done")
        attT_done = sem("attT_done")
        var_ready = {n: sem(f"var_{n}") for n in norm}
        rstd_ready = {n: sem(f"rstd_{n}") for n in norm}
        normed = {n: sem(f"normed_{n}") for n in norm if n not in ("a1", "out")}
        xT_ready = {n: sem(f"xT_ready_{n}") for n in xT}
        res_ready = {s: sem(f"res_ready{s}") for s in (2, 3)}
        res_bias_ready = {s: sem(f"res_bias_ready{s}") for s in (0, 2, 3)}
        gate_in = sem("gate_in")
        gate_exp = [sem(f"gate_exp{l}") for l in range(2)]
        combined = [sem(f"combined{l}") for l in range(2)]
        c_ready = [sem(f"c_ready{l}") for l in range(2)]
        gu_ready = sem("gu_ready")
        silu_done = sem("silu_done")
        c_spread = sem("c_spread")
        tie_ready = sem("tie_ready")
        hid0_ready = sem("hid0_ready")
        down0_done = sem("down0_done")
        up1_ready = sem("up1_ready")
        var1_ready = sem("var1_ready")
        rstd1_ready = sem("rstd1_ready")
        norm1_done = [sem(f"norm1_done{t}") for t in range(QT)]
        tr1_ready = sem("tr1_ready")
        gelu_done = sem("gelu_done")
        down1_done = sem("down1_done")
        acc_done = sem("acc_done")
        stored_ready = sem("stored_ready")
        stored = sem("stored")
        dve_step = sem("dve_step")
        pool_step = sem("pool_step")

        block = ctx.enter_context(nc.Block())
        use = {}

        def banks0(b, i):
            if b == 0:
                return (0, 4, 2)[i % 3], i - 3
            return (4, 2)[i % 2], PAIRS0 + i - 2 if i >= 2 else 4 + i

        @block.tensor
        def _(pe):
            mm = pe.matmul

            def misc(name):
                if use:
                    pe.wait_ge(misc_free, len(use))
                use[name] = len(use) + 1

            def k_projection(i):
                l, b = divmod(i, B)
                pe.wait_ge(ld[f"ctx{b}"], 16)
                pe.wait_ge(ld[f"aw{l}"], 16)
                mm(bank[:, i, :], aw[:, l, W_K, :], ctxT_sb[:, b, :], start=True, stop=True).then_inc(k_proj, 1)

            def v_projection(i, at):
                l, b = divmod(i, B)
                pe.wait_ge(ld[f"ctx{b}"], 16)
                pe.wait_ge(ld[f"aw{l}"], 16)
                if at == 3:
                    pe.wait_ge(k_evacuated, 4)
                for t in range(KT):
                    last = mm(bank[:, at, t * D:(t + 1) * D], ctxT_sb[:, b, t * 128:(t + 1) * 128],
                              aw[:, l, W_V, :], start=True, stop=True)
                last.then_inc(v_proj, 1)

            def transpose_tokens(n, b):
                if n == "a0":
                    pe.wait_ge(ld["ident"], 16)
                pe.wait_ge(normed[n], QT * (b + 1))
                misc(f"xT_{n}{b}")
                for t in range(QT):
                    last = pe.transpose(bank[:, MISC, t * 128:(t + 1) * 128], norm[n][b][:, t, :], idf[:, :])
                last.then_inc(misc_ready, 1)

            def q_projection(l, b):
                n = ("a0", "a1n")[l]
                pe.wait_ge(xT_ready[n], b + 1)
                misc(f"q{l}{b}")
                mm(bank[:, MISC, 0:S], aw[:, l, W_Q, :], xT[n][b][:, :], start=True, stop=True).then_inc(misc_ready, 1)

            def score_rows(n, qt):
                l, b, h = n // HEADS, n % HEADS // H, n % H
                if n == 0 and qt == 0:
                    pe.wait_ge(first_stacked, 16 * (PARTS + 1))
                    pe.wait_ge(k_evacuated, 2)
                if h == (HG if n < H else 0) and qt == 0:
                    pe.wait_ge(k_stacked[l * B + b], 16 * PARTS)
                    pe.wait_ge(q_stacked[l * B + b], 16)
                if n >= 1:
                    pe.wait_ge(max_done, 2 * (n - 1) + qt + 1)
                mm(bank[:, qt, :], q_stack[0:STACK, b, h, qt * 128:(qt + 1) * 128],
                   k_stack[0:STACK, b, h, :], start=True, stop=True).then_inc(for_max, 1)

            def max_transpose(g):
                pe.wait_ge(max_parts, g + 1)
                if g == 0:
                    pe.wait_ge(consts_ready, 1)
                misc(f"max{g}")
                o = bank[MAX_ROW:ROWS_K, MISC, 0:MG * S // 2].bitcast(BF16)
                for j in range(MG):
                    for t in range(QT):
                        at = j * S + t * 128
                        last = pe.transpose(o[:, at:at + 128], max_part[:, g % 2, j, t, :], idb[:, :])
                last.then_inc(misc_ready, 1)

            def score_cols(n, kts):
                l, b, h = n // HEADS, n % HEADS // H, n % H
                if kts[0] == 0:
                    if n % MG == 0:
                        pe.wait_ge(max_copied, n // MG + 1)
                    if n == 0:
                        pe.wait_ge(ld["pad0"], 16 * 3)
                        pe.wait_ge(k_evacuated, 4)
                        pe.wait_ge(mask_ready, 2)
                        pe.wait_ge(v_copied[3], 1)
                    if n == 1:
                        pe.wait_ge(v_copied[0], 1)
                        pe.wait_ge(v_copied[1], 1)
                    if n == H:
                        pe.wait_ge(ld["pad1"], 16 * 3)
                    if n == HEADS:
                        pe.wait_ge(hid0_ready, B * PAIRS0)
                    if n >= 2:
                        pe.wait_ge(exp_done, n - 1)
                at = 2 + 2 * (n % 2)
                for kt in kts:
                    o = bank[:, at + kt // 2, kt % 2 * S:(kt % 2 + 1) * S]
                    last = mm(o, k_stack[:, b, h, kt * 128:(kt + 1) * 128], q_stack[:, b, h, :],
                              start=True, stop=(l == 1))
                    if l == 0:
                        last = mm(o, idb[:, :], bias_k[:, kt, :], start=False, stop=True)
                if kts[-1] == KT - 1:
                    last.then_inc(scores_ready, 1)

            def values(g, kt):
                l, b = g // (B * NG), g % (B * NG) // NG
                if kt == 0:
                    pe.wait_ge(exp_done, HG * (g + 1))
                    if g % NG == 0:
                        pe.wait_ge(v_ready[g // NG], 1)
                    if g == 0:
                        pe.wait_ge(v_copied[2], 1)
                    if g >= 1:
                        pe.wait_ge(o_copied, g)
                    if g == B * NG:
                        pe.wait_ge(res_ready[2], QT * B)
                for j in range(HG):
                    h = g % NG * HG + j
                    last = mm(bank[VW * j:VW * (j + 1), OUT, 0:S], v_ext[l][:, b * KT + kt, h * (DK + 1):h * (DK + 1) + VW],
                              probs[:, (g * HG + j) % (2 * HG), kt * S:(kt + 1) * S],
                              start=(kt == 0), stop=(kt == KT - 1))
                if kt == KT - 1:
                    last.then_inc(pv_done, 1)

            def o_transpose(g):
                pe.wait_ge(o_copied, g + 1)
                misc(f"o{g}")
                for t in range(QT):
                    last = pe.transpose(bank[:, MISC, t * 128:(t + 1) * 128], o_sb[:, g % 2, t * 128:(t + 1) * 128], idf[:, :])
                last.then_inc(misc_ready, 1)

            def att_transpose(l, b):
                pe.wait_ge(att_done, NG * (l * B + b + 1))
                misc(f"attT{l}{b}")
                for t in range(QT):
                    last = pe.transpose(bank[:, MISC, t * 128:(t + 1) * 128], att[l][b][:, t, :], idf[:, :])
                last.then_inc(misc_ready, 1)

            def out_projection(l, b):
                pe.wait_ge(attT_done, l * B + b + 1)
                misc(f"out{l}{b}")
                for t in range(QT):
                    last = mm(bank[:, MISC, t * D:(t + 1) * D], attT[l][b][:, t * 128:(t + 1) * 128], aw[:, l, W_O, :],
                              start=True, stop=True)
                last.then_inc(misc_ready, 1)

            def gate_logits(l, b):
                n, e, w = (("f0", E0, g0_sb), ("f1", E1, g1_sb))[l]
                pe.wait_ge(xT_ready[n], b + 1)
                pe.wait_ge(ld["router"], 16 * 4)
                misc(f"gate{l}{b}")
                for t in range(QT):
                    last = mm(bank[:, MISC, t * e:(t + 1) * e], xT[n][b][:, t * 128:(t + 1) * 128], w[:, :],
                              start=True, stop=True)
                last.then_inc(misc_ready, 1)

            def combine_transpose(l, b):
                pe.wait_ge(combined[l], b + 1)
                misc(f"c{l}{b}")
                for t in range(QT):
                    if l == 0:
                        o = bank[0:PARTS * E0, MISC, 0:128].bitcast(BF16)
                        last = pe.transpose(o[:, t * 128:(t + 1) * 128], c_part[:, t].rearrange("p a e -> p (a e)"), idb[:, :])
                    else:
                        last = pe.transpose(bank[0:E1, MISC, t * 128:(t + 1) * 128], combine[1][b][:, t, :], idf[:, :])
                last.then_inc(misc_ready, 1)

            def bias_down1(b):
                pe.wait_ge(c_ready[1], b + 1)
                misc(f"b2{b}")
                for t in range(QT):
                    last = mm(bank[:, MISC, t * D:(t + 1) * D], cT1[b][:, t * 128:(t + 1) * 128], bd1_sb[:, :],
                              start=True, stop=True)
                last.then_inc(misc_ready, 1)

            def spread0(b, i):
                if i == 0:
                    pe.wait_ge(sel_ready, 1)
                    pe.wait_ge(c_ready[0], b + 1)
                misc(f"spread{b * PAIRS0 + i}")
                for j in range(2):
                    last = mm(bank[:, MISC, j * S:(j + 1) * S], sel[:, 2 * i + j, :], c_rows[b][:, :], start=True, stop=True)
                last.then_inc(misc_ready, 1)

            def up0(b, i):
                u = b * PAIRS0 + i
                at, before = banks0(b, i)
                if u == 0:
                    pe.wait_ge(max_done, 2 * HEADS)
                    pe.wait_ge(ld["wg0"], 16)
                    pe.wait_ge(ld["wu0"], 16)
                if u == 1:
                    pe.wait_ge(exp_done, HEADS)
                if i == 0:
                    pe.wait_ge(xT_ready["f0"], b + 1)
                if before >= 0:
                    pe.wait_ge(hid0_ready, before + 1)
                shared = i == PAIRS0 - 1
                m = I0 if shared else 128
                for j in range(1 if shared else 2):
                    t = 2 * i + j
                    mm(bank[0:m, at + j, 0:S], wg0_sb[:, t * 128:t * 128 + m], xT["f0"][b][:, :], start=True, stop=True)
                    last = mm(bank[0:m, at + j, S:2 * S], wu0_sb[:, t * 128:t * 128 + m], xT["f0"][b][:, :], start=True, stop=True)
                last.then_inc(gu_ready, 1)

            def down0(b, i):
                u = b * PAIRS0 + i
                shared = i == PAIRS0 - 1
                pe.wait_ge(hid0_ready, u + 1)
                if u == 0:
                    pe.wait_ge(o_copied, B * NG)
                    pe.wait_ge(ld["wd0"], 32)
                if b == 1 and i == 0:
                    pe.wait_ge(res_ready[2], QT)
                m = I0 if shared else 128
                for j in range(1 if shared else 2):
                    w = wsd0_sb[:, :] if shared else wd0_sb[:, 2 * i + j, :]
                    for t in range(QT):
                        last = mm(bank[:, OUT, t * D:(t + 1) * D], hid0[0:m, u % 2, j, t * 128:(t + 1) * 128], w,
                                  start=(i == 0 and j == 0 and t == 0), stop=shared, skip_group_check=True)
                last.then_inc(down0_done, 1)

            def up1(b, i):
                w = b * (E1 // 2) + i
                if w == 1:
                    pe.wait_ge(exp_done, 2 * HEADS)
                if w == 0:
                    pe.wait_ge(max_done, 4 * HEADS)
                    pe.wait_ge(ld["wu1"], 16)
                    pe.wait_ge(bu1_ready, 16 * PARTS)
                    pe.wait_ge(ones_ready, 1)
                for t in range(QT):
                    if w >= 2:
                        pe.wait_ge(norm1_done[t], 2 * (w - 1))
                    o = bank[:, 2 * (w % 2) + t, :]
                    mm(o, xT["f1"][b][:, t * 128:(t + 1) * 128],
                       wu1_sb[:, 2 * i:2 * i + 2, :].rearrange("p e n -> p (e n)"), start=True, stop=False)
                    last = mm(o, ones_parts[:, 0:128], bu1_rows[:, 2 * i * H1:(2 * i + 2) * H1], start=False, stop=True)
                last.then_inc(up1_ready, 1)

            def transpose1(b, i):
                w = b * (E1 // 2) + i
                for e in range(2):
                    for t in range(QT):
                        pe.wait_ge(norm1_done[t], 2 * w + e + 1)
                    if w >= 1:
                        pe.wait_ge(gelu_done, 4 * (w - 1) + 2 * (e + 1))
                    for half in range(2):
                        for t in range(QT):
                            at = half * S + t * 128
                            last = pe.transpose(bank[:, 4 + e, at:at + 128],
                                                hn1[:, w % 2, t, e, half * 128:(half + 1) * 128], idf[:, :])
                        last.then_inc(tr1_ready, 1)

            def down1(b, i):
                w = b * (E1 // 2) + i
                if w == 0:
                    pe.wait_ge(o_copied, 2 * B * NG)
                    pe.wait_ge(ld["wd1"], 32)
                if w >= 1:
                    pe.wait_ge(acc_done, 4 * w)
                for e in range(2):
                    pe.wait_ge(gelu_done, 4 * w + 2 * (e + 1))
                    for t in range(QT):
                        for half in range(2):
                            last = mm(bank[:, OUT, (e * QT + t) * D:(e * QT + t + 1) * D],
                                      hid1[:, w % 2, 2 * e + half, t * 128:(t + 1) * 128],
                                      wd1_sb[:, 2 * (2 * i + e) + half, :], start=(half == 0), stop=(half == 1))
                last.then_inc(down1_done, 1)

            def attention(l, extra):
                for s in range(HEADS + PV_LAG):
                    n, m = l * HEADS + s, l * HEADS + s - LAG
                    if l * BEGUN <= s < HEADS:
                        score_rows(n, 0)
                    if 0 <= s - LAG < HEADS:
                        score_cols(m, range(0, KT // 2))
                    if l * BEGUN <= s < HEADS:
                        score_rows(n, 1)
                    if s % MG == 1 and 0 <= (s - 3) // MG < HEADS // MG:
                        max_transpose(l * HEADS // MG + (s - 3) // MG)
                    if 0 <= s - LAG < HEADS:
                        score_cols(m, range(KT // 2, KT))
                    if s % HG == (PV_LAG + 1) % HG and s >= PV_LAG + HG:
                        o_transpose(l * B * NG + (s - PV_LAG) // HG - 1)
                    if s >= PV_LAG:
                        values(l * B * NG + (s - PV_LAG) // HG, (s - PV_LAG) % HG)
                    for at, f in extra:
                        if at == s:
                            f()

            k_projection(0)
            v_projection(0, 4)
            transpose_tokens("a0", 0)
            k_projection(1)
            q_projection(0, 0)
            k_projection(2)
            k_projection(3)
            v_projection(1, 5)
            v_projection(2, OUT)
            v_projection(3, 3)
            transpose_tokens("a0", 1)
            q_projection(0, 1)

            attention(0, [
                (27, lambda: att_transpose(0, 0)),
                (28, lambda: out_projection(0, 0)),
                (30, lambda: transpose_tokens("f0", 0)),
                (31, lambda: gate_logits(0, 0)),
                (36, lambda: up0(0, 0)),
            ])

            up0(0, 1)
            o_transpose(B * NG - 1)
            up0(0, 2)
            combine_transpose(0, 0)
            spread0(0, 0)
            spread0(0, 1)
            att_transpose(0, 1)
            spread0(0, 2)
            down0(0, 0)
            out_projection(0, 1)
            down0(0, 1)
            spread0(0, 3)
            up0(0, 3)
            transpose_tokens("f0", 1)
            gate_logits(0, 1)
            up0(0, 4)
            spread0(0, 4)
            down0(0, 2)
            spread0(0, 5)
            up0(0, 5)
            down0(0, 3)
            down0(0, 4)
            up0(0, 6)
            down0(0, 5)
            up0(1, 0)
            combine_transpose(0, 1)
            down0(0, 6)
            spread0(1, 0)
            up0(1, 1)
            spread0(1, 1)
            down0(1, 0)
            spread0(1, 2)
            up0(1, 2)
            transpose_tokens("a1n", 0)
            q_projection(1, 0)
            down0(1, 1)
            spread0(1, 3)
            up0(1, 3)
            spread0(1, 4)
            up0(1, 4)
            down0(1, 2)
            down0(1, 3)
            spread0(1, 5)
            up0(1, 5)
            score_rows(HEADS + 0, 0)
            score_rows(HEADS + 0, 1)
            down0(1, 4)
            score_rows(HEADS + 1, 0)
            up0(1, 6)
            score_rows(HEADS + 1, 1)
            down0(1, 5)
            score_rows(HEADS + 2, 0)
            score_rows(HEADS + 2, 1)
            score_rows(HEADS + 3, 0)
            score_rows(HEADS + 3, 1)
            score_rows(HEADS + 4, 0)
            score_rows(HEADS + 4, 1)
            score_rows(HEADS + 5, 0)
            score_rows(HEADS + 5, 1)
            down0(1, 6)

            attention(1, [
                (34, lambda: up1(0, 0)),
                (6, lambda: transpose_tokens("a1n", 1)),
                (8, lambda: q_projection(1, 1)),
                (27, lambda: att_transpose(1, 0)),
                (28, lambda: out_projection(1, 0)),
                (31, lambda: transpose_tokens("f1", 0)),
                (32, lambda: gate_logits(1, 0)),
                (36, lambda: combine_transpose(1, 0)),
                (39, lambda: bias_down1(0)),
            ])

            o_transpose(2 * B * NG - 1)
            up1(0, 1)
            att_transpose(1, 1)
            transpose1(0, 0)
            out_projection(1, 1)
            up1(0, 2)
            down1(0, 0)
            transpose1(0, 1)
            transpose_tokens("f1", 1)
            up1(0, 3)
            gate_logits(1, 1)
            down1(0, 1)
            transpose1(0, 2)
            up1(1, 0)
            up1(1, 1)
            down1(0, 2)
            combine_transpose(1, 1)
            transpose1(0, 3)
            down1(0, 3)
            transpose1(1, 0)
            bias_down1(1)
            up1(1, 2)
            down1(1, 0)
            transpose1(1, 1)
            up1(1, 3)
            down1(1, 1)
            transpose1(1, 2)
            down1(1, 2)
            transpose1(1, 3)
            down1(1, 3)

        @block.vector
        def _(dve):
            steps = [0]

            def then(ins):
                steps[0] += 1
                ins.then_inc(dve_step, 1)
                dve.wait_ge(dve_step, steps[0])

            def noted(ins):
                steps[0] += 1
                ins.then_inc(dve_step, 1)

            tt, ts, copy = dve.tensor_tensor, dve.tensor_scalar, dve.tensor_copy

            def norm_stats(n, b, src):
                for t in range(QT):
                    (then if t == QT - 1 else noted)(dve.bn_stats(stats[:, t, :], src[:, t, :]))
                for t in range(QT):
                    dve.bn_aggr(mean_var[n, b][:, t, :], stats[:, t, :]).then_inc(var_ready[n], 1)

            def normalise(n, b, src):
                dve.wait_ge(rstd_ready[n], b + 1)
                for t in range(QT):
                    ins = ts(norm[n][b][:, t, :], src[:, t, :], mean_var[n, b][:, t, 0:1], rstd[n, b][:, t:t + 1],
                             ALU.subtract, ALU.mult)
                    if n in normed:
                        ins.then_inc(normed[n], 1)
                    else:
                        (then if t == QT - 1 else noted)(ins)

            def xT_copy(n, b):
                dve.wait_ge(misc_ready, use[f"xT_{n}{b}"])
                if n == "a1n":
                    then(ts(xT[n][b][:, :], bank[:, MISC, 0:S], col[:, COL_LNG:COL_LNG + 1],
                            col[:, COL_LNB:COL_LNB + 1], ALU.mult, ALU.add))
                else:
                    then(copy(xT[n][b][:, :], bank[:, MISC, 0:S]))
                dve.sem_inc(xT_ready[n], 1)
                dve.sem_inc(misc_free, 1)

            def q_split(l, b):
                i = l * B + b
                c = (COL_BQ0, COL_BQ1)[l]
                if l == 1:
                    dve.wait_ge(q_written[b], 16 * PARTS)
                dve.wait_ge(misc_ready, use[f"q{l}{b}"])
                then(ts(q_part[b][:, 0, :], bank[:, MISC, 0:S], col[:, c:c + 1], None, ALU.add))
                then(dve.scalar_tensor_tensor(out=q_rest[:, :], in0=bank[:, MISC, 0:S], scalar=col[:, c:c + 1],
                                              in1=q_part[b][:, 0, :], op0=ALU.add, op1=ALU.subtract))
                dve.sem_inc(misc_free, 1)
                then(copy(q_part[b][:, 1, :], q_rest[:, :]))
                tt(q_part[b][:, 2, :], q_rest[:, :], q_part[b][:, 1, :], ALU.subtract).then_inc(q_parts[i], 1)



            def head_max(n, qt):
                dve.wait_ge(for_max, 2 * n + qt + 1)
                g = n // MG
                if g >= 2 and n % MG == 0 and qt == 0:
                    dve.wait_ge(max_parts, g - 1)
                o = row_max[:, g % 2, n % MG, qt:qt + 1]
                if 2 * n + qt >= 2:
                    dve.wait_ge(max_done, 2 * n + qt - 1)
                if n == 0:
                    dve.wait_ge(mask_ready, 1)
                if n < HEADS:
                    ins = dve.tensor_tensor_reduce(discard[:, qt, :], bank[:, qt, :], bias_q[:, qt, :], 1.0, LOWEST,
                                                   ALU.add, ALU.max, o)
                else:
                    ins = dve.tensor_reduce(o, bank[:, qt, :], AX.X, ALU.max)
                ins.then_inc(max_done, 1)



            def divide(g):
                l, b = g // (B * NG), g % (B * NG) // NG
                dve.wait_ge(misc_ready, use[f"o{g}"])
                src = bank[:, MISC, 0:S].rearrange("p (t j v) -> p t j v", t=QT, j=HG)
                then(dve.reciprocal(rden[:, :, :], src[:, :, :, DK]))
                o = att[l][b][:, :, g % NG * HG * DK:(g % NG + 1) * HG * DK].rearrange("p t (j d) -> p t j d", j=HG)
                then(tt(o, src[:, :, :, 0:DK], rden[:, :, :].unsqueeze(3).to_broadcast([128, QT, HG, DK]), ALU.mult))
                dve.sem_inc(att_done, 1)
                dve.sem_inc(misc_free, 1)

            def attT_copy(l, b):
                dve.wait_ge(misc_ready, use[f"attT{l}{b}"])
                then(copy(attT[l][b][:, :], bank[:, MISC, 0:S]))
                dve.sem_inc(attT_done, 1)
                dve.sem_inc(misc_free, 1)

            def add_attention(l, b):
                s = 2 * l
                dve.wait_ge(misc_ready, use[f"out{l}{b}"])
                dve.wait_ge(res_bias_ready[s], b + 1)
                r = res[s + 1][b]
                then(tt(r, bank[:, MISC, 0:S].rearrange("p (t d) -> p t d", t=QT), res_bias[s][b][:, :, :], ALU.add))
                dve.sem_inc(misc_free, 1)
                if s + 1 == 3:
                    dve.sem_inc(res_ready[3], 1)
                norm_stats(("f0", "f1")[l], b, r)

            def ranks(values, e, beats_ge, beats_gt):
                mine = values.unsqueeze(3).to_broadcast([128, QT, e, e])
                other = values.unsqueeze(2).to_broadcast([128, QT, e, e])
                ge, gt = beats_ge[:, :, 0:e, 0:e], beats_gt[:, :, 0:e, 0:e]
                noted(tt(ge, other, mine, ALU.is_ge))
                then(tt(gt, other, mine, ALU.is_gt))
                for t in range(QT):
                    ins = tt(ge[:, t], ge[:, t], tie[:, 0:e, 0:e], ALU.mult)
                    (then if t == QT - 1 else noted)(ins)
                for t in range(QT):
                    ins = tt(gt[:, t], gt[:, t], ge[:, t], ALU.max)
                    (then if t == QT - 1 else noted)(ins)
                then(dve.tensor_reduce(r_rank[:, :, 0:e], gt, AX.X, ALU.add))

            def route0(b, part):
                v = r_biased[:, :, :].rearrange("p t (g k) -> p t g k", g=GROUPS0)
                c = combine[0][b]
                if part == 0:
                    dve.wait_ge(gate_exp[0], b + 1)
                    dve.wait_ge(ld["router"], 16 * 4)
                    dve.wait_ge(tie_ready, 1)
                    then(ts(r_exp[:, :, :], r_exp[:, :, :], 1.0, None, ALU.add))
                    then(dve.reciprocal(r_score[:, :, :], r_exp[:, :, :]))
                    for t in range(QT):
                        ins = tt(r_biased[:, t, :], r_score[:, t, :], gbias[:, :], ALU.add)
                        (then if t == QT - 1 else noted)(ins)
                    for i, (op, lo) in enumerate(((ALU.max, 0), (ALU.min, 0), (ALU.max, 2), (ALU.min, 2))):
                        ins = tt(r_pair[:, i], v[:, :, :, lo], v[:, :, :, lo + 1], op)
                        (then if i == 3 else noted)(ins)
                    noted(tt(r_top[:, 0], r_pair[:, 0], r_pair[:, 2], ALU.max))
                    noted(tt(r_top[:, 1], r_pair[:, 0], r_pair[:, 2], ALU.min))
                    then(tt(r_top[:, 2], r_pair[:, 1], r_pair[:, 3], ALU.max))
                    then(tt(r_top[:, 1], r_top[:, 1], r_top[:, 2], ALU.max))
                    then(tt(r_gsum[:, :, :], r_top[:, 0], r_top[:, 1], ALU.add))
                elif part == 1:
                    ranks(r_gsum[:, :, :], GROUPS0, r_ge, r_gt)
                    noted(ts(r_keep[:, :, :], r_rank[:, :, 0:GROUPS0], 2.0, None, ALU.is_lt))
                    then(ts(r_drop[:, :, :], r_rank[:, :, 0:GROUPS0], 2.0, LOWEST, ALU.is_ge, ALU.mult))
                    for t in range(QT):
                        keep = r_keep[:, t, :].unsqueeze(2).to_broadcast([128, GROUPS0, E0 // GROUPS0])
                        ins = tt(v[:, t], v[:, t], keep, ALU.mult)
                        (then if t == QT - 1 else noted)(ins)
                    for t in range(QT):
                        drop = r_drop[:, t, :].unsqueeze(2).to_broadcast([128, GROUPS0, E0 // GROUPS0])
                        ins = tt(v[:, t], v[:, t], drop, ALU.add)
                        (then if t == QT - 1 else noted)(ins)
                elif part == 2:
                    ranks(r_biased[:, :, :], E0, r_ge, r_gt)
                else:
                    then(dve.scalar_tensor_tensor(out=c[:, :, :], in0=r_rank[:, :, :], scalar=4.0, in1=r_score[:, :, :],
                                                  op0=ALU.is_lt, op1=ALU.mult))
                    then(dve.tensor_reduce(r_small[:, 0, :], c[:, :, :], AX.X, ALU.add))
                    then(ts(r_small[:, 0, :], r_small[:, 0, :], 1e-20, None, ALU.add))
                    then(dve.reciprocal(r_small[:, 1, :], r_small[:, 0, :]))
                    for t in range(QT):
                        ins = ts(c[:, t, :], c[:, t, :], r_small[:, 1, t:t + 1], 2.5, ALU.mult, ALU.mult)
                        (then if t == QT - 1 else noted)(ins)
                    then(copy(c_part[:, :, 0, :], c[:, :, :]))
                    then(tt(c_rest[:, :, :], c[:, :, :], c_part[:, :, 0, :], ALU.subtract))
                    then(copy(c_part[:, :, 1, :], c_rest[:, :, :]))
                    tt(c_part[:, :, 2, :], c_rest[:, :, :], c_part[:, :, 1, :], ALU.subtract).then_inc(combined[0], 1)

            def c_copy(l, b):
                dve.wait_ge(misc_ready, use[f"c{l}{b}"])
                if l == 0:
                    then(copy(c_rows[b][:, :], bank[0:PARTS * E0, MISC, 0:128].bitcast(BF16)))
                else:
                    then(copy(cT1[b][:, :], bank[0:E1, MISC, 0:S]))
                dve.sem_inc(c_ready[l], 1)
                dve.sem_inc(misc_free, 1)

            def gate_shift1(b):
                dve.wait_ge(misc_ready, use[f"gate1{b}"])
                src = bank[:, MISC, 0:QT * E1].rearrange("p (t e) -> p t e", t=QT)
                then(dve.tensor_reduce(r_small[:, 0, :], src, AX.X, ALU.max))
                then(tt(r_score[:, :, 0:E1], src, r_small[:, 0, :].unsqueeze(2).to_broadcast([128, QT, E1]), ALU.subtract))
                dve.sem_inc(misc_free, 1)
                dve.sem_inc(gate_in, 1)

            def route1(b, part):
                e = r_exp[:, :, 0:E1]
                if part == 0:
                    dve.wait_ge(gate_exp[1], b + 1)
                    then(dve.tensor_reduce(r_small[:, 0, :], e, AX.X, ALU.add))
                    then(dve.reciprocal(r_small[:, 1, :], r_small[:, 0, :]))
                    then(tt(r_score[:, :, 0:E1], e, r_small[:, 1, :].unsqueeze(2).to_broadcast([128, QT, E1]), ALU.mult))
                    return
                ranks(r_score[:, :, 0:E1], E1, r_ge, r_gt)
                c = combine[1][b]
                then(dve.scalar_tensor_tensor(out=c[:, :, :], in0=r_rank[:, :, 0:E1], scalar=2.0, in1=r_score[:, :, 0:E1],
                                              op0=ALU.is_lt, op1=ALU.mult))
                then(dve.tensor_reduce(r_small[:, 0, :], c[:, :, :], AX.X, ALU.add))
                then(dve.reciprocal(r_small[:, 1, :], r_small[:, 0, :]))
                tt(c[:, :, :], c[:, :, :], r_small[:, 1, :].unsqueeze(2).to_broadcast([128, QT, E1]), ALU.mult)\
                    .then_inc(combined[1], 1)

            def hidden0(b, i):
                u = b * PAIRS0 + i
                at, _ = banks0(b, i)
                dve.wait_ge(silu_done, u + 1)
                if u >= 2:
                    dve.wait_ge(down0_done, u - 1)
                if i == T0 // 2:
                    tt(hid0[0:I0, u % 2, 0, :], silu_g[0:I0, u % 2, 0, :], bank[0:I0, at, S:2 * S], ALU.mult)\
                        .then_inc(hid0_ready, 1)
                    return
                then(tt(gated[:, u % 2], silu_g[:, u % 2], bank[:, at:at + 2, S:2 * S], ALU.mult))
                dve.wait_ge(c_spread, b * (T0 // 2) + i + 1)
                tt(hid0[:, u % 2], gated[:, u % 2], c_sb[:, u % 2], ALU.mult).then_inc(hid0_ready, 1)

            def add_experts0(b):
                dve.wait_ge(down0_done, (b + 1) * PAIRS0)
                for t in range(QT):
                    ins = tt(res[2][b][:, t, :], bank[:, OUT, t * D:(t + 1) * D], res[1][b][:, t, :], ALU.add)
                    ins.then_inc(res_ready[2], 1)
                dve.wait_ge(res_ready[2], QT * (b + 1))
                norm_stats("a1", b, res[2][b])



            def stats1(b, i):
                w = b * (E1 // 2) + i
                dve.wait_ge(up1_ready, w + 1)
                if w >= 2:
                    dve.wait_ge(rstd1_ready, w - 1)
                    dve.wait_ge(norm1_done[1], 2 * (w - 1))
                for t in range(QT):
                    for e in range(2):
                        k = 2 * t + e
                        ins = dve.bn_stats(st1[:, k, :], bank[:, 2 * (w % 2) + t, e * H1:(e + 1) * H1])
                        (then if k == 3 else noted)(ins)
                for k in range(4):
                    dve.bn_aggr(mv1[:, w % 2, k, :], st1[:, k, :]).then_inc(var1_ready, 1)

            def normalise1(b, i):
                w = b * (E1 // 2) + i
                dve.wait_ge(rstd1_ready, w + 1)
                if w >= 2:
                    dve.wait_ge(tr1_ready, 4 * (w - 1))
                for e in range(2):
                    ts(hn1[:, w % 2, 0, e, :], bank[:, 2 * (w % 2), e * H1:(e + 1) * H1],
                       mv1[:, w % 2, e, 0:1], rs1[:, w % 2, e:e + 1], ALU.subtract, ALU.mult).then_inc(norm1_done[0], 1)

            def start_acc(b):
                dve.wait_ge(misc_ready, use[f"b2{b}"])
                then(tt(acc[b][:, :, :], bank[:, MISC, 0:S].rearrange("p (t d) -> p t d", t=QT), norm["f1"][b][:, :, :], ALU.add))
                dve.sem_inc(misc_free, 1)

            def accumulate1(b, i):
                w = b * (E1 // 2) + i
                dve.wait_ge(down1_done, w + 1)
                for e in range(2):
                    if e == 1:
                        dve.wait_ge(acc_done, 4 * w + QT)
                    elif i >= 1:
                        dve.wait_ge(acc_done, 4 * w)
                    for t in range(QT):
                        at = (e * QT + t) * D
                        dve.scalar_tensor_tensor(out=acc[b][:, t, :], in0=bank[:, OUT, at:at + D],
                                                 scalar=combine[1][b][:, t, 2 * i + e:2 * i + e + 1], in1=acc[b][:, t, :],
                                                 op0=ALU.mult, op1=ALU.add).then_inc(acc_done, 1)

            def last_stats(b):
                dve.wait_ge(acc_done, 4 * (E1 // 2) * (b + 1))
                norm_stats("out", b, acc[b])

            def finish(b):
                g = row[:, ROW_NAMES.index("lnf_g"), :]
                o = norm["out"][b]
                dve.wait_ge(var_ready["out"], QT * (b + 1))
                for t in range(QT):
                    ins = dve.scalar_tensor_tensor(out=o[:, t, :], in0=acc[b][:, t, :], scalar=mean_var["out", b][:, t, 0:1],
                                                   in1=g, op0=ALU.subtract, op1=ALU.mult)
                    (then if t == QT - 1 else noted)(ins)
                dve.wait_ge(res_bias_ready[3], b + 1)
                dve.wait_ge(rstd_ready["out"], b + 1)
                for t in range(QT):
                    dve.scalar_tensor_tensor(out=result[:, b, t, :], in0=o[:, t, :], scalar=rstd["out", b][:, t:t + 1],
                                             in1=res_bias[3][b][:, t, :], op0=ALU.mult, op1=ALU.add).then_inc(stored_ready, 1)

            def attention(l, extra):
                for s in range(HEADS + PV_LAG):
                    n = l * HEADS + s
                    if s % HG == (PV_LAG + 2) % HG and s > PV_LAG + HG:
                        divide(l * B * NG + (s - PV_LAG) // HG - 1)
                    if l * BEGUN <= s < HEADS:
                        head_max(n, 0)
                    for at, f in extra:
                        if at == s - 0.5:
                            f()
                    if l * BEGUN <= s < HEADS:
                        head_max(n, 1)
                    for at, f in extra:
                        if at == s:
                            f()

            def first_k_rest():
                dve.wait_ge(ld["col"], 16)
                dve.wait_ge(k_evacuated, 1)
                dve.scalar_tensor_tensor(out=k_rest[0][:, :], in0=bank[:, 0, :], scalar=col[:, COL_BK0:COL_BK0 + 1],
                                         in1=k_part[0][:, 0, :], op0=ALU.add, op1=ALU.subtract).then_inc(k_rest_ready[0], 1)

            def first_k_third():
                dve.wait_ge(k_second, 1)
                tt(k_part[0][:, 2, :], k_rest[0][:, :], k_part[0][:, 1, :], ALU.subtract).then_inc(k_parts[0], 1)



            dve.wait_ge(ld["x"], 16)
            norm_stats("a0", 0, x_sb[:, 0])
            normalise("a0", 0, x_sb[:, 0])
            first_k_rest()
            xT_copy("a0", 0)
            first_k_third()
            q_split(0, 0)
            norm_stats("a0", 1, x_sb[:, 1])
            dve.wait_ge(ld["mask"], 32)
            ts(bias_q[:, :, :], mask_q[:, :, :], 0.0, MASKED, ALU.is_equal, ALU.mult).then_inc(mask_ready, 1)
            ts(bias_k[:, :, :], mask_k[:, :, :], 0.0, MASKED, ALU.is_equal, ALU.mult).then_inc(mask_ready, 1)
            normalise("a0", 1, x_sb[:, 1])
            xT_copy("a0", 1)
            q_split(0, 1)

            attention(0, [
                (27.5, lambda: attT_copy(0, 0)),
                (29, lambda: add_attention(0, 0)),
                (29.5, lambda: normalise("f0", 0, res[1][0])),
                (30.5, lambda: xT_copy("f0", 0)),
                (31, lambda: route0(0, 0)),
                (33.5, lambda: route0(0, 1)),
                (34, lambda: route0(0, 2)),
                (39, lambda: route0(0, 3)),
            ])

            divide(B * NG - 1)
            c_copy(0, 0)
            hidden0(0, 0)
            attT_copy(0, 1)
            hidden0(0, 1)
            add_attention(0, 1)
            normalise("f0", 1, res[1][1])
            hidden0(0, 2)
            xT_copy("f0", 1)
            hidden0(0, 3)
            route0(1, 0)
            route0(1, 1)
            hidden0(0, 4)
            route0(1, 2)
            hidden0(0, 5)
            hidden0(0, 6)
            route0(1, 3)
            c_copy(0, 1)
            add_experts0(0)
            hidden0(1, 0)
            normalise("a1", 0, res[2][0])
            norm_stats("a1n", 0, norm["a1"][0])
            hidden0(1, 1)
            normalise("a1n", 0, norm["a1"][0])
            xT_copy("a1n", 0)
            q_split(1, 0)
            hidden0(1, 2)
            hidden0(1, 3)
            hidden0(1, 4)
            hidden0(1, 5)
            head_max(HEADS + 0, 0)
            head_max(HEADS + 0, 1)
            head_max(HEADS + 1, 0)
            head_max(HEADS + 1, 1)
            hidden0(1, 6)
            head_max(HEADS + 2, 0)
            head_max(HEADS + 2, 1)
            head_max(HEADS + 3, 0)
            head_max(HEADS + 3, 1)
            head_max(HEADS + 4, 0)
            head_max(HEADS + 4, 1)
            head_max(HEADS + 5, 0)
            head_max(HEADS + 5, 1)

            attention(1, [
                (0.5, lambda: add_experts0(1)),
                (3.5, lambda: normalise("a1", 1, res[2][1])),
                (4, lambda: norm_stats("a1n", 1, norm["a1"][1])),
                (4.5, lambda: normalise("a1n", 1, norm["a1"][1])),
                (6.5, lambda: xT_copy("a1n", 1)),
                (8, lambda: q_split(1, 1)),
                (27, lambda: attT_copy(1, 0)),
                (28, lambda: add_attention(1, 0)),
                (30.5, lambda: normalise("f1", 0, res[3][0])),
                (31, lambda: xT_copy("f1", 0)),
                (31, lambda: gate_shift1(0)),
                (33, lambda: route1(0, 0)),
                (33.5, lambda: route1(0, 1)),
                (37, lambda: c_copy(1, 0)),
                (33.5, lambda: stats1(0, 0)),
                (40, lambda: start_acc(0)),
                (39, lambda: normalise1(0, 0)),
            ])
            divide(2 * B * NG - 1)
            attT_copy(1, 1)
            stats1(0, 1)
            add_attention(1, 1)
            normalise1(0, 1)
            normalise("f1", 1, res[3][1])
            stats1(0, 2)
            xT_copy("f1", 1)
            accumulate1(0, 0)
            gate_shift1(1)
            stats1(0, 3)
            normalise1(0, 2)
            route1(1, 0)
            accumulate1(0, 1)
            normalise1(0, 3)
            stats1(1, 0)
            route1(1, 1)
            normalise1(1, 0)
            accumulate1(0, 2)
            stats1(1, 1)
            c_copy(1, 1)
            accumulate1(0, 3)
            start_acc(1)
            last_stats(0)
            normalise1(1, 1)
            stats1(1, 2)
            finish(0)
            accumulate1(1, 0)
            normalise1(1, 2)
            stats1(1, 3)
            accumulate1(1, 1)
            normalise1(1, 3)
            accumulate1(1, 2)
            accumulate1(1, 3)
            last_stats(1)
            finish(1)

        @block.scalar
        def _(act):
            def k_evacuate(i):
                c = (COL_BK0, COL_BK1)[i // B]
                act.wait_ge(k_proj, i + 1)
                if i >= 1:
                    act.activation(k_full[i][:, :], bank[:, i, :], ACT.Identity, bias=col[:, c:c + 1])
                act.activation(k_part[i][:, 0, :], bank[:, i, :], ACT.Identity, bias=col[:, c:c + 1]).then_inc(k_evacuated, 1)

            def k_second_part(i):
                act.wait_ge(k_rest_ready[i], 1)
                act.copy(k_part[i][:, 1, :], k_rest[i][:, :]).then_inc(k_second, 1)

            act.dma_start(aw[:, 0], attn_w[:, 0]).then_inc(ld["aw0"], 16)
            act.dma_start(col[:, :], cols).then_inc(ld["col"], 16)
            act.dma_start(row[:, :, :], rows.to_broadcast([128, len(ROW_NAMES), D])).then_inc(ld["row"], 16)
            act.dma_start(aw[:, 1], attn_w[:, 1]).then_inc(ld["aw1"], 16)
            def load_table(k, function):
                act.wait_ge(half_ready, 1)
                act.activation(table[:, k:k + 1], minus_half[:, 0:1], function)

            load_table(0, ACT.Exp)
            act.wait_ge(ld["col"], 16)


            def v_copy(i, at):
                l, b = divmod(i, B)
                act.wait_ge(v_proj, i + 1)
                act.wait_ge(v_zeroed[l], 2)
                act.copy(v_heads[l][:, b * KT:(b + 1) * KT, :, 0:DK],
                         bank[:, at, :].rearrange("p (t h d) -> p t h d", t=KT, h=H)).then_inc(v_copied[i], 1)

            k_evacuate(0)
            k_second_part(0)
            k_evacuate(1)
            v_copy(0, 4)
            k_evacuate(2)
            k_evacuate(3)
            v_copy(1, 5)
            v_copy(2, OUT)
            v_copy(3, 3)

            def sel_cast():
                act.wait_ge(ld["sel"], 16)
                act.copy(sel[:, :, :], sel_f[:, :, :]).then_inc(sel_ready, 1)

            def max_copy(g):
                b, h = g % (HEADS // MG) // (H // MG), g % (H // MG) * MG
                act.wait_ge(misc_ready, use[f"max{g}"])
                act.copy(q_stack[MAX_ROW:ROWS_K, b, h:h + MG, :].rearrange("p h s -> p (h s)"),
                         bank[MAX_ROW:ROWS_K, MISC, 0:MG * S // 2].bitcast(BF16)).then_inc(max_copied, 1)
                act.wait_ge(max_copied, g + 1)
                act.sem_inc(misc_free, 1)

            def exponentials(n):
                g = n // HG
                if n == 0:
                    act.wait_ge(mask_ready, 2)
                act.wait_ge(scores_ready, n + 1)
                if n >= 2 * HG:
                    act.wait_ge(pv_done, g - 1)
                at = 2 + 2 * (n % 2)
                act.activation(probs[:, n % (2 * HG), :], bank[:, at:at + 2, :].rearrange("p a n -> p (a n)"), ACT.Exp,
                               scale=SCALE).then_inc(exp_done, 1)

            def o_copy(g):
                act.wait_ge(pv_done, g + 1)
                if g >= 2:
                    act.wait_ge(misc_ready, use[f"o{g - 2}"])
                act.copy(o_sb[:, g % 2, :], bank[:, OUT, 0:S]).then_inc(o_copied, 1)

            def gate_exponential(l, b):
                e, src = (E0, bank[:, MISC, 0:QT * E0].rearrange("p (t e) -> p t e", t=QT)) if l == 0 else \
                    (E1, r_score[:, :, 0:E1])
                if l == 0:
                    act.wait_ge(misc_ready, use[f"gate0{b}"])
                else:
                    act.wait_ge(gate_in, b + 1)
                if b == 1:
                    act.wait_ge(combined[l], 1)
                elif l == 1:
                    act.wait_ge(combined[0], B)
                ins = act.activation(r_exp[:, :, 0:e], src, ACT.Exp, scale=(-1.0, 1.0)[l])
                ins.then_inc(gate_exp[l], 1)
                if l == 0:
                    act.wait_ge(gate_exp[l], b + 1)
                    act.sem_inc(misc_free, 1)

            def attention(l, extra):
                for s in range(HEADS + PV_LAG):
                    if s % MG == 1 and 0 <= (s - 3) // MG < HEADS // MG:
                        max_copy(l * HEADS // MG + (s - 3) // MG)
                    if 0 <= s - LAG < HEADS:
                        exponentials(l * HEADS + s - LAG)
                    if s % HG == (PV_LAG - 1) % HG and s >= PV_LAG:
                        o_copy(l * B * NG + (s - PV_LAG) // HG)
                    for at, f in extra:
                        if at == s:
                            f()

            def c_evacuate(b, i):
                u = b * PAIRS0 + i
                if u >= 2:
                    act.wait_ge(hid0_ready, u - 1)
                act.wait_ge(misc_ready, use[f"spread{u}"])
                act.copy(c_sb[:, u % 2], bank[:, MISC, :].rearrange("p (j s) -> p j s", j=2)).then_inc(c_spread, 1)
                act.wait_ge(c_spread, b * (PAIRS0 - 1) + i + 1)
                act.sem_inc(misc_free, 1)

            def silu(b, i):
                u = b * PAIRS0 + i
                at, _ = banks0(b, i)
                if u >= 2:
                    act.wait_ge(hid0_ready, u - 1)
                act.wait_ge(gu_ready, u + 1)
                if i == T0 // 2:
                    ins = act.activation(silu_g[0:I0, u % 2, 0, :], bank[0:I0, at, 0:S], ACT.Silu)
                else:
                    ins = act.activation(silu_g[:, u % 2], bank[:, at:at + 2, 0:S], ACT.Silu)
                ins.then_inc(silu_done, 1)

            def normalise1(b, i):
                w = b * (E1 // 2) + i
                act.wait_ge(rstd1_ready, w + 1)
                if w >= 2:
                    act.wait_ge(tr1_ready, 4 * (w - 1))
                for e in range(2):
                    k = 2 + e
                    act.activation(hn1[:, w % 2, 1, e, :], bank[:, 2 * (w % 2) + 1, e * H1:(e + 1) * H1], ACT.Identity,
                                   bias=shift1[:, w % 2, k:k + 1], scale=rs1[:, w % 2, k:k + 1]).then_inc(norm1_done[1], 1)

            def gelu1(b, i):
                w = b * (E1 // 2) + i
                if w >= 2:
                    act.wait_ge(down1_done, w - 1)
                for e in range(2):
                    for half in range(2):
                        k = 2 * e + half
                        c = 2 * (2 * i + e) + half
                        act.wait_ge(tr1_ready, 4 * w + 2 * e + 2)
                        act.activation(hid1[:, w % 2, k, :], bank[:, 4 + e, half * S:(half + 1) * S], ACT.Gelu,
                                       bias=col[:, COL_B1 + c:COL_B1 + c + 1],
                                       scale=col[:, COL_G1 + c:COL_G1 + c + 1]).then_inc(gelu_done, 1)

            attention(0, [
                (24, lambda: sel_cast()),
                (31, lambda: gate_exponential(0, 0)),
                (37, lambda: load_table(1, ACT.Silu)),
            ])
            for i in range(4):
                act.wait_ge(k_written[i], 16)
            silu(0, 0)
            c_evacuate(0, 0)
            c_evacuate(0, 1)
            silu(0, 1)
            c_evacuate(0, 2)
            c_evacuate(0, 3)
            silu(0, 2)
            silu(0, 3)
            gate_exponential(0, 1)
            silu(0, 4)
            c_evacuate(0, 4)
            silu(0, 5)
            load_table(2, ACT.Silu)
            c_evacuate(0, 5)
            silu(0, 6)
            silu(1, 0)
            c_evacuate(1, 0)
            silu(1, 1)
            c_evacuate(1, 1)
            c_evacuate(1, 2)
            silu(1, 2)
            c_evacuate(1, 3)
            silu(1, 3)
            silu(1, 4)
            c_evacuate(1, 4)
            c_evacuate(1, 5)
            silu(1, 5)
            silu(1, 6)
            load_table(3, ACT.Exp)
            attention(1, [
                (36, lambda: load_table(4, ACT.Gelu)),
                (32, lambda: gate_exponential(1, 0)),
                (39, lambda: normalise1(0, 0)),
            ])
            gelu1(0, 0)
            normalise1(0, 1)
            gelu1(0, 1)
            normalise1(0, 2)
            gate_exponential(1, 1)
            load_table(5, ACT.Gelu)
            gelu1(0, 2)
            normalise1(0, 3)
            gelu1(0, 3)
            normalise1(1, 0)
            gelu1(1, 0)
            normalise1(1, 1)
            gelu1(1, 1)
            normalise1(1, 2)
            gelu1(1, 2)
            normalise1(1, 3)
            gelu1(1, 3)

        @block.gpsimd
        def _(pool):
            steps = [0]

            def then(ins):
                steps[0] += 1
                ins.then_inc(pool_step, 1)
                pool.wait_ge(pool_step, steps[0])

            def root(n, b):
                pool.wait_ge(var_ready[n], QT * (b + 1))
                then(pool.tensor_scalar(var_eps[:, :], mean_var[n, b][:, :, 1], EPS, None, ALU.add))
                pool.tensor_tensor(rstd[n, b][:, :], var_eps[:, :], minus_half[:, 0:QT], ALU.pow).then_inc(rstd_ready[n], 1)

            def add_row(s, b, name):
                r = row[:, ROW_NAMES.index(name), :].unsqueeze(1).to_broadcast([128, QT, D])
                if s == 0:
                    pool.wait_ge(ld["row"], 16)
                    pool.wait_ge(ld["x"], 16)
                if s == 2:
                    pool.wait_ge(res_ready[2], QT * (b + 1))
                if s == 3:
                    pool.wait_ge(res_ready[3], b + 1)
                pool.tensor_tensor(res_bias[s][b][:, :, :], res[s][b], r, ALU.add).then_inc(res_bias_ready[s], 1)

            pool.memset(minus_half[:, :], -0.5).then_inc(half_ready, 1)
            pool.memset(zero_rows[:, :], 0.0).then_inc(pad_ready, 1)
            pool.memset(minus_ones[:, :], -1.0).then_inc(pad_ready, 1)
            pool.memset(ones_parts[:, :], 1.0).then_inc(ones_ready, 1)
            for l in range(2):
                pool.memset(v_ext[l][:, :, H * (DK + 1):], 0.0).then_inc(v_zeroed[l], 1)
                pool.memset(v_heads[l][:, :, :, DK], 1.0).then_inc(v_zeroed[l], 1)
            pool.wait_ge(half_ready, 1)
            root("a0", 0)
            pool.wait_ge(ld["ident"], 16)
            pool.tensor_copy(idb[:, :], idf[:, :]).then_inc(consts_ready, 1)

            root("a0", 1)

            def v_bias(i):
                l, b = divmod(i, B)
                pool.wait_ge(v_copied[i], 1)
                pool.wait_ge(ld["row"], 16)
                v = v_heads[l][:, b * KT:(b + 1) * KT, :, 0:DK]
                bias = row[:, ROW_NAMES.index(f"bv{l}"), :].rearrange("p (h d) -> p h d", h=H)
                pool.tensor_tensor(v, v, bias.unsqueeze(1).to_broadcast([128, KT, H, DK]), ALU.add)\
                    .then_inc(v_ready[i], 1)

            def max_split(g):
                pool.wait_ge(max_done, 2 * MG * (g + 1))
                if g >= 2:
                    pool.wait_ge(misc_ready, use[f"max{g - 2}"])
                m = row_max[:, g % 2]
                part = [max_part[:, g % 2, :, :, a] for a in range(PARTS)]
                then(pool.tensor_copy(part[0], m))
                then(pool.tensor_tensor(max_rest[:, :, :], m, part[0], ALU.subtract))
                then(pool.tensor_copy(part[1], max_rest[:, :, :]))
                pool.tensor_tensor(part[2], max_rest[:, :, :], part[1], ALU.subtract).then_inc(max_parts, 1)

            def k_split(i, part):
                if part == 0:
                    pool.wait_ge(k_evacuated, i + 1)
                    pool.tensor_tensor(k_rest[i][:, :], k_full[i][:, :], k_part[i][:, 0, :], ALU.subtract)\
                        .then_inc(k_rest_ready[i], 1)
                elif part == 1:
                    pool.wait_ge(k_rest_ready[i], 1)
                    then(pool.tensor_copy(k_part[i][:, 1, :], k_rest[i][:, :]))
                else:
                    pool.tensor_tensor(k_part[i][:, 2, :], k_rest[i][:, :], k_part[i][:, 1, :], ALU.subtract)\
                        .then_inc(k_parts[i], 1)

            def tie_cast():
                pool.wait_ge(ld["router"], 16 * 4)
                pool.tensor_copy(tie[:, :, :], tie_f[:, :, :]).then_inc(tie_ready, 1)

            def bias_split1():
                pool.wait_ge(ld["bu1"], 16)
                then(pool.tensor_copy(bu1_part[:, 0, :], bu1_sb[:, :]))
                then(pool.tensor_tensor(bu1_rest[:, :], bu1_sb[:, :], bu1_part[:, 0, :], ALU.subtract))
                then(pool.tensor_copy(bu1_part[:, 1, :], bu1_rest[:, :]))
                pool.tensor_tensor(bu1_part[:, 2, :], bu1_rest[:, :], bu1_part[:, 1, :], ALU.subtract).then_inc(bu1_split, 1)

            def maxima(groups, extra):
                for g in groups:
                    max_split(g)
                    for at, f in extra:
                        if at == g:
                            f()

            k_split(1, 0)
            k_split(1, 1)
            k_split(1, 2)
            v_bias(0)
            maxima(range(0, HEADS // MG), [
                (0, lambda: v_bias(1)),
                (4, lambda: v_bias(2)),
                (5, lambda: v_bias(3)),
                (2, lambda: k_split(2, 0)),
                (2, lambda: k_split(2, 1)),
                (11, lambda: k_split(2, 2)),
                (11, lambda: k_split(3, 0)),
                (11, lambda: k_split(3, 1)),
                (12, lambda: k_split(3, 2)),
                (0, lambda: add_row(0, 0, "bo0")),
                (5, lambda: add_row(0, 1, "bo0")),
                (3, lambda: tie_cast()),
                (7, lambda: bias_split1()),
                (13, lambda: root("f0", 0)),
            ])
            root("f0", 1)
            root("a1", 0)
            add_row(2, 0, "bo1")
            root("a1n", 0)
            maxima(range(HEADS // MG, 2 * HEADS // MG), [
                (16, lambda: root("a1", 1)),
                (18, lambda: root("a1n", 1)),
                (19, lambda: add_row(2, 1, "bo1")),
                (30, lambda: root("f1", 0)),
            ])

            def root1(w):
                pool.wait_ge(var1_ready, 4 * (w + 1))
                then(pool.tensor_scalar(ve1[:, :], mv1[:, w % 2, :, 1], EPS, None, ALU.add))
                then(pool.tensor_scalar(minus_mean[:, :], mv1[:, w % 2, :, 0], -1.0, None, ALU.mult))
                if w >= 2:
                    for t in range(QT):
                        pool.wait_ge(norm1_done[t], 2 * (w - 1))
                then(pool.tensor_tensor(rs1[:, w % 2, :], ve1[:, :], minus_half[:, :], ALU.pow))
                pool.tensor_tensor(shift1[:, w % 2, :], minus_mean[:, :], rs1[:, w % 2, :], ALU.mult).then_inc(rstd1_ready, 1)

            root1(0)
            root1(1)
            root("f1", 1)
            root1(2)
            root1(3)
            add_row(3, 0, "lnf_b")
            root1(4)
            root1(5)
            root("out", 0)
            root1(6)
            add_row(3, 1, "lnf_b")
            root1(7)
            root("out", 1)

        @block.sync
        def _(sp):
            sp.dma_start(ctxT_sb[:, 0], ctxT[:, 0]).then_inc(ld["ctx0"], 16)
            sp.dma_start(x_sb[:, :, :, :], x.rearrange("b (t p) d -> p b t d", p=128)).then_inc(ld["x"], 16)
            sp.dma_start(idf[:, :], ident).then_inc(ld["ident"], 16)
            sp.dma_start(ctxT_sb[:, 1], ctxT[:, 1]).then_inc(ld["ctx1"], 16)
            sp.dma_start(mask_q[:, :, :], mask.rearrange("(t p) k -> p t k", p=128)).then_inc(ld["mask"], 16)
            sp.dma_start(mask_k[:, :, :], maskT.rearrange("(t p) q -> p t q", p=128)).then_inc(ld["mask"], 16)

            def k_out(i):
                sp.wait_ge(k_parts[i], 1)
                sp.dma_start(k_bounce[i].rearrange("a p s -> p a s"), k_part[i][:, :, :]).then_inc(k_written[i], 16)

            def k_in(i, heads, signal):
                sp.wait_ge(k_written[i], 16)
                for a in range(PARTS):
                    sp.dma_start(k_stack[a * PARTS * DK:(a + 1) * PARTS * DK, i % B, heads, :],
                                 k_bounce[i].rearrange("j (d h) s -> (j d) h s", h=H)[:, heads, :]).then_inc(signal, 16)

            def q_out(i):
                sp.wait_ge(q_parts[i], 1)
                for a in range(PARTS):
                    sp.dma_start(q_bounce[i][:, a].rearrange("a p s -> p a s"), q_part[i % B][:, :, :])\
                        .then_inc(q_written[i], 16)

            def q_in(i, heads, signal):
                sp.wait_ge(q_written[i], 16 * PARTS)
                sp.dma_start(q_stack[0:STACK, i % B, heads, :],
                             q_bounce[i].rearrange("i j (d h) s -> (i j d) h s", h=H)[:, heads, :]).then_inc(signal, 16)

            def pad_rows(b):
                sp.wait_ge(pad_ready, 2)
                for o, rows_in in ((q_stack[STACK:MAX_ROW, b], zero_rows[:, 0:S]), (k_stack[STACK:MAX_ROW, b], zero_rows[:, :]),
                                   (k_stack[MAX_ROW:ROWS_K, b], minus_ones[:, :])):
                    shape = [o.shape[0], H, rows_in.shape[1]]
                    sp.dma_start(o, rows_in.unsqueeze(1).to_broadcast(shape)).then_inc(ld[f"pad{b}"], 16)

            first, rest, every = slice(0, HG), slice(HG, H), slice(0, H)
            k_out(0)
            q_out(0)
            k_in(0, first, first_stacked)
            q_in(0, first, first_stacked)
            q_in(0, rest, q_stacked[0])
            k_in(0, rest, k_stacked[0])
            pad_rows(0)
            k_out(1)
            q_out(1)
            k_in(1, every, k_stacked[1])
            q_in(1, every, q_stacked[1])
            pad_rows(1)
            sp.dma_start(sel_f[:, :, :], select0).then_inc(ld["sel"], 16)
            sp.dma_start(g0_sb[:, :], gate0).then_inc(ld["router"], 16)
            sp.dma_start(g1_sb[:, :], gate1).then_inc(ld["router"], 16)
            sp.dma_start(gbias[:, :], gate_bias.to_broadcast([128, E0])).then_inc(ld["router"], 16)
            sp.dma_start(tie_f[:, :, :], ties.to_broadcast([128, E0, E0])).then_inc(ld["router"], 16)

            sp.dma_start(bu1_sb[:, :], bu1).then_inc(ld["bu1"], 16)
            sp.dma_start(wg0_sb[:, :], wg0).then_inc(ld["wg0"], 16)
            sp.dma_start(wu0_sb[:, :], wu0).then_inc(ld["wu0"], 16)
            sp.dma_start(wd0_sb[:, :, :], wd0.rearrange("(t p) d -> p t d", p=128)).then_inc(ld["wd0"], 16)
            sp.dma_start(wsd0_sb[:, :], wsd0).then_inc(ld["wd0"], 16)
            sp.dma_start(bd1_sb[:, :], bd1).then_inc(ld["wd1"], 16)
            k_out(2)
            k_out(3)
            sp.wait_ge(bu1_split, 1)
            sp.wait_ge(k_proj, 4)
            sp.wait_ge(v_proj, 4)
            for a in range(PARTS):
                sp.dma_start(bu1_rows[a:a + 1, :].rearrange("o (p c) -> o p c", p=128),
                             bu1_part[:, a, :]).then_inc(bu1_ready, 16)
            sp.wait_ge(scores_ready, HEADS)
            for i in range(B, 2 * B):
                k_in(i, every, k_stacked[i])
            q_out(2)
            q_in(2, every, q_stacked[2])
            sp.wait_ge(down0_done, 2 * PAIRS0)
            sp.dma_start(wu1_sb[:, :, :], wu1).then_inc(ld["wu1"], 16)
            sp.dma_start(wd1_sb[:, :, :], wd1.rearrange("(t p) d -> p t d", p=128)).then_inc(ld["wd1"], 16)
            q_out(3)
            q_in(3, every, q_stacked[3])
            for b in range(B):
                sp.wait_ge(stored_ready, QT * (b + 1))
                sp.dma_start(out[b].rearrange("(t p) d -> p t d", p=128), result[:, b]).then_inc(stored, 16)
            sp.wait_ge(stored, 16 * B)


def kernel(**inputs):
    import concourse.bacc as _bacc
    from concourse.bass_utils import run_bass_kernel_spmd as _run

    a = {k: np.asarray(v) for k, v in inputs.items()}

    def head_minor(w):
        return w.reshape(H, DK, *w.shape[1:]).swapaxes(0, 1).reshape(w.shape)

    def proj(l):
        q, k, v, o = (("L0_xattn_w_q", "L0_xattn_w_k", "L0_xattn_w_v", "L0_xattn_w_out"),
                      ("L1_xattn_Wq", "L1_xattn_Wk", "L1_xattn_Wv", "L1_xattn_Wo"))[l]
        return np.stack([head_minor(a[k]).T, head_minor(a[q]).T, a[v].T, a[o].T], axis=1)

    by_unit = [a[n].reshape(E1, 2, 128).transpose(2, 0, 1).reshape(128, 2 * E1) for n in ("L1_ffn_ln1_g", "L1_ffn_ln1_b")]
    cols = np.concatenate([np.stack([head_minor(a["L0_xattn_b_k"]), head_minor(a["L0_xattn_b_q"]),
                                     head_minor(a["L1_xattn_bk"]), head_minor(a["L1_xattn_bq"]),
                                     a["L1_xattn_ln_g"], a["L1_xattn_ln_b"]], axis=1)] + by_unit, axis=1)
    rows = np.stack([a[n] for n in ("L0_xattn_b_v", "L0_xattn_b_out", "L1_xattn_bv", "L1_xattn_bo",
                                    "L1_ffn_ln_g", "L1_ffn_ln_b")])[None]
    index = np.arange(E0)
    ties = (index[None, :] < index[:, None]).astype(np.float32)[None]
    expert_of_row = (np.arange(E0 * I0) // I0).reshape(T0, 128)
    select = np.tile((expert_of_row[None] == index[:, None, None]).astype(np.float32), (PARTS, 1, 1))
    arrays = {
        "x": a["x"],
        "ctxT": a["ctx_1024"].transpose(2, 0, 1),
        "mask": a["mask_SxS2_ik0"],
        "maskT": a["mask_SxS2_ik0"].T,
        "attn_w": np.stack([proj(0), proj(1)], axis=1),
        "cols": cols,
        "rows": rows,
        "gate_bias": a["L0_ffn_gate_bias"][None],
        "ties": ties,
        "ident": np.eye(128, dtype=np.float32),

        "gate0": a["L0_ffn_gate_w"].T,
        "gate1": a["L1_ffn_gate_w"],
        "wg0": np.concatenate([a["L0_ffn_w1"].reshape(E0 * I0, D), a["L0_ffn_ws1"]]).T,
        "wu0": np.concatenate([a["L0_ffn_w3"].reshape(E0 * I0, D), a["L0_ffn_ws3"]]).T,
        "wd0": a["L0_ffn_w2"].transpose(0, 2, 1).reshape(E0 * I0, D),
        "wsd0": a["L0_ffn_ws2"].T,
        "select0": select,
        "wu1": a["L1_ffn_w1"].transpose(1, 0, 2),
        "bu1": a["L1_ffn_b1"].reshape(128, E1 * H1 // 128),
        "wd1": a["L1_ffn_w2"].reshape(E1 * H1, D),
        "bd1": a["L1_ffn_b2"],
    }
    arrays = {f"in_{k}": np.ascontiguousarray(v) for k, v in arrays.items()}
    nc = _bacc.Bacc("TRN2", target_bir_lowering=False, num_devices=1)
    args = [nc.dram_tensor(k, v.shape, mybir.dt.from_np(v.dtype), kind="ExternalInput").ap() for k, v in arrays.items()]
    args.append(nc.dram_tensor("out_0", (B, S, D), F32, kind="ExternalOutput").ap())
    attention_ffn_kernel(nc, *args)
    r = _run(nc, [arrays], core_ids=[0])
    return r.results[0]["out_0"]
```
